# Optimizing a Trainium2 kernel written in Bass

```python
import numpy as np
import jax
import jax.numpy as jnp

def _softmax(x, axis=-1):
    return jax.nn.softmax(x, axis=axis)

def _gelu(x):
    return jax.nn.gelu(x, approximate=True)

def _silu(x):
    return jax.nn.silu(x)

def _sigmoid(x):
    return jax.nn.sigmoid(x)

def _layernorm(x, axis=-1, eps=1e-05):
    m = jnp.mean(x, axis=axis, keepdims=True)
    v = jnp.var(x, axis=axis, keepdims=True)
    return (x - m) / jnp.sqrt(v + eps)

def _scatter_add(tgt, idx, src, axis=0):
    return tgt.at[idx].add(src)

def _segment_sum(src, seg, n):
    return jax.ops.segment_sum(src, seg, n)
kernel_name = 'mk_adaln_d1_jaxref_r4_c2318d'

def setup_inputs(seed: int=0):
    np.random.seed(seed)
    _w = jnp.asarray

    def _L0_attn_setup():
        import jax, jax.numpy as jnp
        import numpy as np
        B, S, D = (2, 512, 256)
        H = 16
        HD = D // H
        SCALE = HD ** (-0.5)
        EPS = 1e-12

        def _rope_sin_cos(length, half, dtype):
            positions = jnp.arange(length, dtype=dtype)
            freqs = jnp.arange(half, dtype=dtype)
            inv_freq = 1.0 / 2500 ** (freqs / max(1, half))
            theta = jnp.einsum('s,f->sf', positions, inv_freq)
            return (jnp.sin(theta)[None, None], jnp.cos(theta)[None, None])

        def _rotate(x, sin, cos):
            x_even = x[..., 0::2]
            x_odd = x[..., 1::2]
            r_even = x_even * cos - x_odd * sin
            r_odd = x_even * sin + x_odd * cos
            return jnp.stack([r_even, r_odd], axis=-1).reshape(x.shape)
        key = jax.random.key(seed)
        k1, k2, k3 = jax.random.split(key, 3)
        tokens = jax.random.normal(k1, (B, S, D), dtype=jnp.float32)
        qkv_w = jax.random.normal(k2, (3 * D, D), dtype=jnp.float32) * D ** (-0.5)
        qkv_b = jnp.zeros((3 * D,), dtype=jnp.float32)
        out_w = jax.random.normal(k3, (D, D), dtype=jnp.float32) * D ** (-0.5)
        out_b = jnp.zeros((D,), dtype=jnp.float32)
        return {'tokens': tokens, 'qkv_w': qkv_w, 'qkv_b': qkv_b, 'out_w': out_w, 'out_b': out_b}
    _L0_attn_in = _L0_attn_setup()

    def _L0_ffn_setup():
        import jax, jax.numpy as jnp
        import numpy as np
        E = 8
        JITTER = 0.01

        def _sparse_mixer_routing(logits):
            top_vals, top_idx = jax.lax.top_k(logits, 2)
            eidx = jnp.arange(logits.shape[-1])

            def _multiplier(thr, base_logits, idx):
                factor = jnp.maximum(jnp.abs(logits), thr)
                mask = (thr - logits) / factor > 2.0 * JITTER
                probs = jax.nn.softmax(jnp.where(mask, -jnp.inf, base_logits), axis=-1)
                return jnp.take_along_axis(probs, idx, axis=-1)
            mult1 = _multiplier(top_vals[:, :1], logits, top_idx[:, :1])
            scat = jnp.where(eidx[None, :] == top_idx[:, :1], -jnp.inf, logits)
            mult2 = _multiplier(top_vals[:, 1:2], scat, top_idx[:, 1:2])
            return (jnp.concatenate([mult1, mult2], axis=-1), top_idx)
        key = jax.random.key(seed)
        ks = jax.random.split(key, 5)
        H, F = (256, 1024)
        scale = 0.02
        return {'hidden_states': jax.random.normal(ks[0], (1, 512, H), jnp.float32), 'gate_w': jax.random.normal(ks[1], (H, E), jnp.float32) * scale, 'w1': jax.random.normal(ks[2], (E, H, F), jnp.float32) * scale, 'w2': jax.random.normal(ks[3], (E, F, H), jnp.float32) * scale, 'w3': jax.random.normal(ks[4], (E, H, F), jnp.float32) * scale}
    _L0_ffn_in = _L0_ffn_setup()
    _L0_c = _w((lambda *s: np.random.randn(*s).astype(np.float32) * 0.05)(4, 256))
    _L0_wmod = _w((lambda *s: np.random.randn(*s).astype(np.float32) * 0.05)(256, 6 * 256) * 256 ** (-0.5))
    _d = {'L0_attn_tokens': _L0_attn_in['tokens'], 'L0_attn_qkv_w': _L0_attn_in['qkv_w'], 'L0_attn_qkv_b': _L0_attn_in['qkv_b'], 'L0_attn_out_w': _L0_attn_in['out_w'], 'L0_attn_out_b': _L0_attn_in['out_b'], 'L0_ffn_gate_w': _L0_ffn_in['gate_w'], 'L0_ffn_w1': _L0_ffn_in['w1'], 'L0_ffn_w2': _L0_ffn_in['w2'], 'L0_ffn_w3': _L0_ffn_in['w3'], 'L0_c': _L0_c, 'L0_wmod': _L0_wmod}
    _x0 = _d['L0_attn_tokens']
    _d['L0_attn_tokens'] = jax.random.normal(jax.random.fold_in(jax.random.key(seed), 1), (4, 1024, 256), dtype=_x0.dtype)
    del _x0
    return _d

def reference(L0_attn_tokens, L0_attn_qkv_w, L0_attn_qkv_b, L0_attn_out_w, L0_attn_out_b, L0_ffn_gate_w, L0_ffn_w1, L0_ffn_w2, L0_ffn_w3, L0_c, L0_wmod):

    def _L0_attn_ref(tokens, qkv_w, qkv_b, out_w, out_b):
        import jax, jax.numpy as jnp
        import numpy as np
        B, S, D = (2, 512, 256)
        H = 16
        HD = D // H
        SCALE = HD ** (-0.5)
        EPS = 1e-12

        def _rope_sin_cos(length, half, dtype):
            positions = jnp.arange(length, dtype=dtype)
            freqs = jnp.arange(half, dtype=dtype)
            inv_freq = 1.0 / 2500 ** (freqs / max(1, half))
            theta = jnp.einsum('s,f->sf', positions, inv_freq)
            return (jnp.sin(theta)[None, None], jnp.cos(theta)[None, None])

        def _rotate(x, sin, cos):
            x_even = x[..., 0::2]
            x_odd = x[..., 1::2]
            r_even = x_even * cos - x_odd * sin
            r_odd = x_even * sin + x_odd * cos
            return jnp.stack([r_even, r_odd], axis=-1).reshape(x.shape)
        batch, length, _ = tokens.shape
        qkv = tokens @ qkv_w.T + qkv_b
        qkv = qkv.reshape(batch, length, 3, H, HD)
        qkv = jnp.transpose(qkv, (0, 3, 1, 2, 4))
        q, k, v = (qkv[..., 0, :], qkv[..., 1, :], qkv[..., 2, :])
        sin, cos = _rope_sin_cos(length, HD // 2, q.dtype)
        q = _rotate(q, sin, cos)
        k = _rotate(k, sin, cos)
        q = q / jnp.maximum(jnp.linalg.norm(q, axis=-1, keepdims=True), EPS)
        k = k / jnp.maximum(jnp.linalg.norm(k, axis=-1, keepdims=True), EPS)
        scores = jnp.einsum('bhqd,bhkd->bhqk', q, k) * SCALE
        attn = jax.nn.softmax(scores, axis=-1)
        out = jnp.einsum('bhqk,bhkd->bhqd', attn, v)
        out = jnp.transpose(out, (0, 2, 1, 3)).reshape(batch, length, D)
        return out @ out_w.T + out_b

    def _L0_ffn_ref(hidden_states, gate_w, w1, w2, w3):
        import jax, jax.numpy as jnp
        import numpy as np
        E = 8
        JITTER = 0.01

        def _sparse_mixer_routing(logits):
            top_vals, top_idx = jax.lax.top_k(logits, 2)
            eidx = jnp.arange(logits.shape[-1])

            def _multiplier(thr, base_logits, idx):
                factor = jnp.maximum(jnp.abs(logits), thr)
                mask = (thr - logits) / factor > 2.0 * JITTER
                probs = jax.nn.softmax(jnp.where(mask, -jnp.inf, base_logits), axis=-1)
                return jnp.take_along_axis(probs, idx, axis=-1)
            mult1 = _multiplier(top_vals[:, :1], logits, top_idx[:, :1])
            scat = jnp.where(eidx[None, :] == top_idx[:, :1], -jnp.inf, logits)
            mult2 = _multiplier(top_vals[:, 1:2], scat, top_idx[:, 1:2])
            return (jnp.concatenate([mult1, mult2], axis=-1), top_idx)
        B, S, H = hidden_states.shape
        x = hidden_states.reshape(-1, H)
        logits = x @ gate_w
        mult, sel = _sparse_mixer_routing(logits)
        w = jnp.sum(mult[:, :, None] * (sel[:, :, None] == jnp.arange(E)[None, None, :]), axis=1)
        h = jax.nn.silu(jnp.einsum('th,ehf->etf', x, w1)) * jnp.einsum('th,ehf->etf', x, w3)
        out = jnp.einsum('etf,efh,te->th', h, w2, w)
        return out.reshape(B, S, H)
    x = L0_attn_tokens
    mod = (_silu(L0_c) @ L0_wmod).reshape(L0_c.shape[0], 6, 1, -1)
    sa, ca, ga, sb, cb, gb = (mod[:, 0], mod[:, 1], mod[:, 2], mod[:, 3], mod[:, 4], mod[:, 5])
    ga = (2 * (ga >= 0) - 1) * jnp.maximum(jnp.abs(ga), 0.25)
    gb = (2 * (gb >= 0) - 1) * jnp.maximum(jnp.abs(gb), 0.25)
    h = _layernorm(x, axis=-1) * (1 + ca) + sa
    x = x + ga * _L0_attn_ref(h, L0_attn_qkv_w, L0_attn_qkv_b, L0_attn_out_w, L0_attn_out_b)
    h = _layernorm(x, axis=-1) * (1 + cb) + sb
    x = x + gb * _L0_ffn_ref(h, L0_ffn_gate_w, L0_ffn_w1, L0_ffn_w2, L0_ffn_w3)
    return x

_drawn_inputs = setup_inputs


def setup_inputs(seed=0):
    import zlib

    import numpy as np

    out = dict(_drawn_inputs(seed))
    spreads = {'L0_attn_qkv_b': (0.0, 0.32), 'L0_attn_out_b': (0.0, 0.339)}
    factors = {'L0_attn_qkv_w': 7.399,
     'L0_ffn_gate_w': 5.531,
     'L0_ffn_w1': 4.822,
     'L0_ffn_w2': 4.775,
     'L0_ffn_w3': 4.774}
    for name, (base, spread) in spreads.items():
        noise = np.random.default_rng([zlib.crc32(name.encode()), seed]).standard_normal(out[name].shape)
        drawn = base * np.exp(spread * noise) if base else spread * noise
        out[name] = jnp.asarray(drawn.astype(out[name].dtype))
    for name, factor in factors.items():
        out[name] = (out[name] * factor).astype(out[name].dtype)
    return out
```

```python
from contextlib import ExitStack

import concourse.bass as bass
from concourse import mybir

F32 = mybir.dt.float32
F16 = mybir.dt.float16
ALU = mybir.AluOpType
ACT = mybir.ActivationFunctionType
AX = mybir.AxisListType

P = 128
B, S, D = 4, 1024, 256
H, HD = 16, 16
KD = D // P
TPB = S // P
NT = B * TPB
PAIRS = H // 2
HV = 2 * HD + 1
STEPS = 2 * TPB
T_AT = (8, 9, 12, 13)
QCH = S // 512
LN_EPS = 1e-5
CREDIT = 1
NORM_CAP = 1e12
SCALE = HD ** -0.5
E, F = 8, 1024
FC = F // P
ROWS = 256
RC = ROWS // P
BLOCKS = (2 * B * S + E * (ROWS - 1)) // ROWS
JITTER = 0.01
LOWEST = -3.0e38
SA, CA, GA, SB, CB, GB = range(6)


def adaln(nc, x, qkv_wT, qkv_b, out_wT, out_b, cT, wmod, gate_w, w1, w2, w3, ident, ident16, rope, below, counts, out):
    mod_dram = nc.dram_tensor("mod_dram", (B, 6 * D), F32, kind="Internal").ap()
    x1_dram = nc.dram_tensor("x1_dram", (B * S, D), F32, kind="Internal").ap()
    h2_dram = nc.dram_tensor("h2_dram", (B * S, D), F32, kind="Internal").ap()

    xs_dram = nc.dram_tensor("xs_dram", (BLOCKS * ROWS, D), F32, kind="Internal").ap()
    ys_dram = nc.dram_tensor("ys_dram", (BLOCKS * ROWS, D), F32, kind="Internal").ap()

    with ExitStack() as whole:
        LG = whole.enter_context(nc.sbuf_tensor("LG", [P, NT, E], F32))
        attention(nc, x, qkv_wT, qkv_b, out_wT, out_b, cT, wmod, gate_w, ident, ident16, rope, mod_dram, x1_dram, h2_dram, LG)
        experts(nc, w1, w2, w3, ident, below, counts, mod_dram, x1_dram, h2_dram, xs_dram, ys_dram, LG, out)


def attention(nc, x, qkv_wT, qkv_b, out_wT, out_b, cT, wmod, gate_w, ident, ident16, rope, mod_dram, x1_dram, h2_dram, LG):
    with ExitStack() as ctx:
        def sb(name, shape, dt=F32):
            return ctx.enter_context(nc.sbuf_tensor(name, shape, dt))

        def sem(name):
            return ctx.enter_context(nc.semaphore(name))

        modB = sb("modB", [P, B, 2, D])
        idn = sb("idn", [P, P])
        idn16 = sb("idn16", [P, P], F16)
        wqkv = sb("wqkv", [P, KD, 3 * D])
        qkvb = sb("qkvb", [P, 3 * D])
        wo = sb("wo", [P, KD, D])
        wog = sb("wog", [P, B, KD, D])
        ob = sb("ob", [P, D])
        gob = sb("gob", [P, B, D])
        rp = sb("rp", [P, TPB, 2, HD])
        ct = sb("ct", [P, KD, B])
        ce = sb("ce", [P, KD, B])
        cs = sb("cs", [P, KD, B])
        modT = sb("modT", [P, 2, KD, B])
        xA = sb("xA", [P, 2, D])
        xC = sb("xC", [P, 2, D])
        mod = sb("mod", [B, 6 * D])
        sgn = sb("sgn", [B, 2, D])
        eps = sb("eps", [P, 1])
        mhalf = sb("mhalf", [P, 2 * H])
        bnA = sb("bnA", [P, 6])
        dfA = sb("dfA", [P, 3])
        mvA = sb("mvA", [P, 2])
        veA = sb("veA", [P, 1])
        rsA = sb("rsA", [P, 1])
        xnA = sb("xnA", [P, D])
        hTA = sb("hTA", [P, KD, P])
        qk = sb("qk", [P, 2 * H, HD])
        rc = sb("rc", [P, 2 * H, HD])
        rs_ = sb("rs_", [P, 2 * H, HD])
        ss = sb("ss", [P, 2 * H])
        inv = sb("inv", [P, 2 * H])
        QK = sb("QK", [P, 2, TPB, 2, H, 4, HD], F16)
        V = sb("V", [P, 2, TPB, H, HV], F16)
        vA = sb("vA", [P, H, HD])
        EX = sb("EX", [P, 4, S])
        PH = sb("PH", [P, 4, S], F16)
        PL = sb("PL", [P, 4, S], F16)
        wm = EX[:, 0:3, :].rearrange("p a n -> p (a n)").rearrange("p (k n) -> p k n", k=KD)
        gaB = EX[:, 3, :].rearrange("p (b d) -> p b d", b=B)
        QT = sb("QT", [P, 2, S], F16)
        KT = sb("KT", [P, 2, S], F16)
        orec = sb("orec", [P, 2, TPB])
        oh = sb("oh", [P, 2, TPB, HD])
        ol = sb("ol", [P, 2, TPB, HD])
        AT = sb("AT", [P, 2, TPB, D])
        aS = sb("aS", [P, D])
        aT = sb("aT", [P, KD, P])
        xg = sb("xg", [P, D])
        x1 = sb("x1", [P, 2, D])
        bnC = sb("bnC", [P, 6])
        dfC = sb("dfC", [P, 3])
        mvC = sb("mvC", [P, 2])
        veC = sb("veC", [P, 1])
        rsC = sb("rsC", [P, 1])
        xnC = sb("xnC", [P, D])
        h2 = sb("h2", [P, 2, D])
        h2T = sb("h2T", [P, KD, P])
        gw = sb("gw", [P, KD, E])

        psS = [ctx.enter_context(nc.psum_tensor(f"psS{i}", [P, S], F32)) for i in range(2)]
        psO = [ctx.enter_context(nc.psum_tensor(f"psO{i}", [P, TPB, 64], F32)) for i in range(2)]
        psM = [ctx.enter_context(nc.psum_tensor(f"psM{i}", [P, 512], F32)) for i in range(2)]

        s_xA = [sem(f"s_xA{u}") for u in range(2)]
        s_xC = [sem(f"s_xC{u}") for u in range(2)]
        s_w = sem("s_w")
        s_modw = sem("s_modw")
        s_modb = sem("s_modb")
        setup = sem("setup")
        silu_exp = sem("silu_exp")
        silu_done = sem("silu_done")
        mod_ps = sem("mod_ps")
        mod_ready = sem("mod_ready")
        a_step = sem("a_step")
        a_rstd = sem("a_rstd")
        a_pool = sem("a_pool")
        a_xn = sem("a_xn")
        a_hT_ps = sem("a_hT_ps")
        a_hT = sem("a_hT")
        a_qk_ps = sem("a_qk_ps")
        a_v_ps = sem("a_v_ps")
        a_qk = sem("a_qk")
        a_vps = sem("a_vps")
        a_v = sem("a_v")
        a_rope = sem("a_rope")
        a_ss = sem("a_ss")
        a_inv = sem("a_inv")
        a_split = sem("a_split")
        t_ps = sem("t_ps")
        t_ev = sem("t_ev")
        b_scores = sem("b_scores")
        b_exp = sem("b_exp")
        b_hi = sem("b_hi")
        b_split = sem("b_split")
        b_pv = sem("b_pv")
        b_ostep = sem("b_ostep")
        b_o = sem("b_o")
        c_copy = sem("c_copy")
        c_at_ps = sem("c_at_ps")
        c_at = sem("c_at")
        c_proj = sem("c_proj")
        c_xg = sem("c_xg")
        c_x1 = sem("c_x1")
        c_step = sem("c_step")
        c_var = sem("c_var")
        c_pool = sem("c_pool")
        c_rstd = sem("c_rstd")
        c_xn = sem("c_xn")
        c_h2 = sem("c_h2")
        c_st = [sem(f"c_st{u}") for u in range(2)]
        c_h2T_ps = sem("c_h2T_ps")
        c_h2T = sem("c_h2T")
        c_lg_ps = sem("c_lg_ps")
        c_lg = sem("c_lg")

        x_v = x.rearrange("b (t p) d -> p (b t) d", p=P)

        PHASES = [("A", 0, 0, 0, 0, TPB // 2),
                  ("t", 0, 0, 0, 0, 1),
                  ("ATB", TPB, 1, 0, 0, PAIRS // 2),
                  ("ATBC", 2 * TPB, PAIRS + 1, PAIRS, 0, PAIRS),
                  ("TBC", 0, 3 * PAIRS + 1, 3 * PAIRS, 2 * TPB, PAIRS // 2 - 1),
                  ("tBC", 0, 4 * PAIRS - 1, 4 * PAIRS - 2, 3 * TPB - 2, 1),
                  ("C", 0, 0, 0, 3 * TPB, TPB // 2)]

        def phases(eng, body):
            for stages, a0, t0, b0, c0, n in PHASES:
                if stages == "t":
                    body("T1", 0, 0, 0, 0, 0)
                elif n == 1:
                    body("TBC", 0, a0, t0, b0, c0)
                    body("BC", 1, a0 + 1, t0 + 1, b0 + 1, c0 + 1)
                else:
                    with eng.Fori(0, n) as it:
                        for u in range(2):
                            body(stages, u, it * 2 + (a0 + u), it * 2 + (t0 + u), it * 2 + (b0 + u), it * 2 + (c0 + u))

        block = ctx.enter_context(nc.Block())

        @block.sync
        def _(sp):
            sp.dma_start(ct[:], cT.rearrange("(k p) b -> p k b", p=P)).then_inc(s_modw, 16)
            sp.dma_start(wm[:], wmod.rearrange("(k p) n -> p k n", p=P)).then_inc(s_modw, 16)
            for u in range(2):
                sp.dma_start(xA[:, u, :], x_v[:, u, :]).then_inc(s_xA[u], 16)
                sp.dma_start(xC[:, u, :], x_v[:, u, :]).then_inc(s_xC[u], 16)
            sp.dma_start(wqkv[:], qkv_wT.rearrange("(k p) n -> p k n", p=P)).then_inc(s_w, 16)
            sp.dma_start(wo[:], out_wT.rearrange("(k p) n -> p k n", p=P)).then_inc(s_w, 16)
            sp.dma_start(qkvb[:], qkv_b.rearrange("(a n) -> a n", a=1).to_broadcast([P, 3 * D])).then_inc(s_w, 16)
            sp.dma_start(ob[:], out_b.rearrange("(a n) -> a n", a=1).to_broadcast([P, D])).then_inc(s_w, 16)
            sp.dma_start(idn[:], ident).then_inc(s_w, 16)
            sp.dma_start(idn16[:], ident16).then_inc(s_w, 16)
            sp.dma_start(rp[:], rope).then_inc(s_w, 16)
            sp.dma_start(gw[:], gate_w.rearrange("(k p) e -> p k e", p=P)).then_inc(s_w, 16)
            sp.wait_ge(mod_ready, 6)
            sp.dma_start(mod_dram, mod[:]).then_inc(s_modb, 16)
            sp.wait_ge(s_modb, 16)
            m6 = mod_dram.rearrange("(a b) (s d) -> a b s d", a=1, s=6)
            sp.dma_start(gaB, m6[:, :, GA, :].to_broadcast([P, B, D])).then_inc(s_modb, 16)
            sp.dma_start(modB[:], m6[:, :, SB:CB + 1, :].to_broadcast([P, B, 2, D])).then_inc(s_modb, 16)

            def body(stages, u, a, t, b, c):
                if "A" in stages:
                    sp.wait_ge(a_xn, a + 1)
                    sp.dma_start(xA[:, u:u + 1, :], x_v[:, bass.ds((a + 2) % NT, 1), :]).then_inc(s_xA[u], 16)
                if "C" in stages:
                    sp.wait_ge(c_xg, c + 1)
                    sp.dma_start(xC[:, u:u + 1, :], x_v[:, bass.ds((c + 2) % NT, 1), :]).then_inc(s_xC[u], 16)
                    sp.wait_ge(c_x1, c + 1 + CREDIT)
                    sp.dma_start(x1_dram.rearrange("(g p) d -> p g d", p=P)[:, bass.ds(c, 1), :],
                                 x1[:, u:u + 1, :]).then_inc(c_st[u], 16)
                    sp.wait_ge(c_h2, c * 2 + 2)
                    sp.dma_start(h2_dram.rearrange("(g p) d -> p g d", p=P)[:, bass.ds(c, 1), :],
                                 h2[:, u:u + 1, :]).then_inc(c_st[u], 16)
            phases(sp, body)
            for u in range(2):
                sp.wait_ge(c_st[u], 32 * NT // 2 + 32)
                sp.wait_ge(s_xA[u], 16 * (NT // 2 + 1))
                sp.wait_ge(s_xC[u], 16 * (NT // 2 + 1))

        @block.scalar
        def _(act):
            act.wait_ge(s_modw, 32)
            nc.scalar.activation(ce[:], ct[:], ACT.Exp, scale=-1.0).then_inc(silu_exp, 1)

            def body(stages, u, a, t, b, c):
                if "B" in stages:
                    for j in range(STEPS):
                        act.wait_ge(b_scores, b * STEPS + (j + 1))
                        act.wait_ge(b_split, b * STEPS + (j + 1))
                        exp = nc.scalar.activation(EX[:, j % 4, :], psS[j % 2][:], ACT.Exp, scale=SCALE)
                        if j % 2 == 0:
                            act.wait_ge(b_pv, b * STEPS + (j + 1))
                            exp = nc.scalar.activation(PH[:, j % 4, :], psS[j % 2][:], ACT.Exp, scale=SCALE)
                        exp.then_inc(b_exp, 1)
            phases(act, body)

        @block.gpsimd
        def _(pool):
            nc.gpsimd.memset(mhalf[:], -0.5).then_inc(setup, 1)
            nc.gpsimd.memset(eps[:], LN_EPS).then_inc(setup, 1)
            nc.gpsimd.memset(V[:, :, :, :, 2 * HD:HV], 1.0).then_inc(setup, 1)
            pool.wait_ge(setup, 3)
            pool.wait_ge(s_w, 16 * 8)
            pool.wait_ge(s_modb, 48)

            def body(stages, u, a, t, b, c):
                if "A" in stages:
                    pool.wait_ge(a_step, a * 6 + 4)
                    nc.gpsimd.tensor_tensor(veA[:], mvA[:, 1:2], eps[:], ALU.add).then_inc(a_pool, 1)
                    pool.wait_ge(a_pool, a * 2 + 1)
                    nc.gpsimd.tensor_tensor(rsA[:], veA[:], mhalf[:, 0:1], ALU.pow).then_inc(a_rstd, 1)
                if "C" in stages:
                    cbat = c // TPB
                    pool.wait_ge(s_xC[u], 16 * (c // 2) + 16)
                    pool.wait_ge(c_x1, c + CREDIT)
                    nc.gpsimd.tensor_tensor(xg[:], xC[:, u, :],
                                            gob[:, bass.ds(cbat, 1), :].rearrange("p a d -> p (a d)"), ALU.add).then_inc(c_xg, 1)
                if "C" in stages:
                    pool.wait_ge(c_step, c * 4 + 4)
                    nc.gpsimd.tensor_tensor(veC[:], mvC[:, 1:2], eps[:], ALU.add).then_inc(c_pool, 1)
                    pool.wait_ge(c_pool, c + 1)
                    nc.gpsimd.tensor_tensor(rsC[:], veC[:], mhalf[:, 0:1], ALU.pow).then_inc(c_rstd, 1)
                if "A" in stages:
                    tile = a % TPB
                    cos = rp[:, bass.ds(tile, 1), 0, :].to_broadcast([P, 2 * H, HD])
                    sine = rp[:, bass.ds(tile, 1), 1, :].to_broadcast([P, 2 * H, HD])
                    pool.wait_ge(a_qk, a + 1 + CREDIT)
                    nc.gpsimd.tensor_tensor(rc[:], qk[:], cos, ALU.mult)
                    nc.gpsimd.tensor_tensor(rs_[:, :, 0::2], qk[:, :, 1::2], sine[:, :, 0::2], ALU.mult)
                    nc.gpsimd.tensor_tensor(rs_[:, :, 1::2], qk[:, :, 0::2], sine[:, :, 1::2], ALU.mult).then_inc(a_pool, 1)
                    pool.wait_ge(a_pool, a * 2 + 2)
                    nc.gpsimd.tensor_tensor(rc[:], rc[:], rs_[:], ALU.add).then_inc(a_rope, 1)
                if "C" in stages:
                    pool.wait_ge(c_xn, c + 1)
                    pool.wait_ge(c_st[u], 32 * (c // 2) + 32)
                    nc.gpsimd.tensor_tensor(h2[:, u, :], xnC[:], modB[:, bass.ds(cbat, 1), 1, :].rearrange("p a d -> p (a d)"),
                                            ALU.mult).then_inc(c_h2, 1)
                    pool.wait_ge(c_h2, c * 2 + 1)
                    nc.gpsimd.tensor_tensor(h2[:, u, :], h2[:, u, :], modB[:, bass.ds(cbat, 1), 0, :].rearrange("p a d -> p (a d)"),
                                            ALU.add).then_inc(c_h2, 1)
                if "A" in stages:
                    pool.wait_ge(a_ss, a + 1)
                    nc.gpsimd.tensor_tensor(inv[:], ss[:], mhalf[:], ALU.pow).then_inc(a_inv, 1)
            phases(pool, body)

        @block.vector
        def _(dve):
            dve.wait_ge(silu_exp, 1)
            nc.vector.tensor_scalar(ce[:], ce[:], 1.0, None, ALU.add).then_inc(silu_done, 1)
            dve.wait_ge(silu_done, 1)
            nc.vector.reciprocal(ce[:], ce[:]).then_inc(silu_done, 1)
            dve.wait_ge(silu_done, 2)
            nc.vector.tensor_tensor(cs[:], ct[:], ce[:], ALU.mult).then_inc(silu_done, 1)
            dve.wait_ge(mod_ps, 1)
            for n in range(3):
                ins = nc.vector.tensor_copy(mod[:, n * 512:(n + 1) * 512], (psM[0], psM[1], psS[1])[n][0:B, 0:512])
            nc.vector.tensor_copy(modT[:, 0, :, :], psS[0][:, 0:KD * B].rearrange("p (k b) -> p k b", k=KD))
            nc.vector.tensor_scalar(modT[:, 1, :, :], psS[0][:, KD * B:2 * KD * B].rearrange("p (k b) -> p k b", k=KD),
                                    1.0, None, ALU.add).then_inc(mod_ready, 1)
            dve.wait_ge(mod_ready, 1)
            m6 = mod[:].rearrange("b (s d) -> b s d", s=6)
            nc.vector.tensor_scalar(sgn[:], m6[:, GA::3, :], 0.0, 2.0, ALU.is_ge, ALU.mult).then_inc(mod_ready, 1)
            nc.vector.tensor_scalar(m6[:, CA::3, :], m6[:, CA::3, :], 1.0, None, ALU.add)
            dve.wait_ge(mod_ready, 2)
            nc.vector.tensor_scalar(sgn[:], sgn[:], -1.0, None, ALU.add).then_inc(mod_ready, 1)
            dve.wait_ge(mod_ready, 3)
            nc.vector.tensor_tensor(m6[:, GA::3, :], m6[:, GA::3, :], sgn[:], ALU.mult).then_inc(mod_ready, 1)
            dve.wait_ge(mod_ready, 4)
            nc.vector.tensor_scalar(m6[:, GA::3, :], m6[:, GA::3, :], 0.25, None, ALU.max).then_inc(mod_ready, 1)
            dve.wait_ge(mod_ready, 5)
            nc.vector.tensor_tensor(m6[:, GA::3, :], m6[:, GA::3, :], sgn[:], ALU.mult).then_inc(mod_ready, 1)
            dve.wait_ge(s_modb, 48)
            dve.wait_ge(s_w, 16 * 8)
            dve.wait_ge(setup, 3)
            for b in range(B):
                for k in range(KD):
                    nc.vector.tensor_tensor(wog[:, b, k, :], wo[:, k, :], gaB[:, b, :], ALU.mult)
                ins = nc.vector.tensor_tensor(gob[:, b, :], ob[:], gaB[:, b, :], ALU.mult)
            ins.then_inc(setup, 2)
            dve.wait_ge(setup, 5)

            def variance(step, i, per, st, mv, t):
                dve.wait_ge(step, i * per + 1)
                nc.vector.tensor_tensor(t[:, 0:2], st[:, 1:3], st[:, 4:6], ALU.add)
                nc.vector.tensor_tensor(t[:, 2:3], st[:, 1:2], st[:, 4:5], ALU.subtract).then_inc(step, 1)
                dve.wait_ge(step, i * per + 2)
                nc.vector.tensor_scalar(mv[:, 0:1], t[:, 0:1], 0.5, None, ALU.mult)
                nc.vector.scalar_tensor_tensor(out=t[:, 2:3], in0=t[:, 2:3], scalar=0.25, in1=t[:, 2:3],
                                               op0=ALU.mult, op1=ALU.mult).then_inc(step, 1)
                dve.wait_ge(step, i * per + 3)
                nc.vector.scalar_tensor_tensor(out=mv[:, 1:2], in0=t[:, 1:2], scalar=1.0 / D, in1=t[:, 2:3],
                                               op0=ALU.mult, op1=ALU.add).then_inc(step, 1)

            def turned(u, t, i):
                dve.wait_ge(t_ps, t * 4 + (i + 1))
                nc.vector.tensor_copy((QT, KT)[i % 2][:, u, (i // 2) * 512:(i // 2 + 1) * 512], psM[(1, 0)[i % 2]][:]).then_inc(t_ev, 1)

            def body(stages, u, a, t, b, c):
                if stages == "T1":
                    for i in range(4):
                        turned(0, t, i)
                    return
                for j in range(STEPS):
                    if j == 0 and "C" in stages:
                        dve.wait_ge(c_at_ps, c + CREDIT)
                        dve.wait_ge(b_o, (c // TPB + 1) * (2 * PAIRS) + 2)
                        nc.vector.tensor_copy(aS[:], AT[:, bass.ds((c // TPB) % 2, 1), bass.ds(c % TPB, 1), :]
                                              .rearrange("p a t d -> p (a t d)")).then_inc(c_copy, 1)
                    if j == 1 and "A" in stages:
                        dve.wait_ge(s_xA[u], 16 * (a // 2) + 16)
                        nc.vector.bn_stats(bnA[:], xA[:, u, :]).then_inc(a_step, 1)
                        variance(a_step, a, 6, bnA, mvA, dfA)
                    if j == 2 and "A" in stages:
                        dve.wait_ge(a_rstd, a + 1)
                        nc.vector.tensor_scalar(xnA[:], xA[:, u, :], mvA[:, 0:1], rsA[:, 0:1],
                                                ALU.subtract, ALU.mult).then_inc(a_xn, 1)
                    if j == 3 and "C" in stages:
                        dve.wait_ge(c_at_ps, c + 1 + CREDIT)
                        nc.vector.tensor_copy(aT[:].rearrange("p k t -> p (k t)"), psM[1][:, 0:D]).then_inc(c_at, 1)
                    if j == 4 and "A" in stages:
                        dve.wait_ge(a_hT_ps, a + 1)
                        for k in range(KD):
                            bat = bass.ds(a // TPB, 1)
                            ins = nc.vector.tensor_scalar(hTA[:, k, :], psM[0][:, k * P:(k + 1) * P], modT[:, 1, k, bat],
                                                          modT[:, 0, k, bat], ALU.mult, ALU.add)
                        ins.then_inc(a_hT, 1)
                    if j == 5 and "C" in stages:
                        dve.wait_ge(c_proj, c + 1)
                        dve.wait_ge(c_xg, c + 1)
                        dve.wait_ge(c_st[u], 32 * (c // 2) + 32)
                        nc.vector.tensor_tensor(x1[:, u, :], psM[1][:, 0:D], xg[:], ALU.add).then_inc(c_x1, 1)
                        dve.wait_ge(c_x1, c + 1 + CREDIT)
                        nc.vector.bn_stats(bnC[:], x1[:, u, :]).then_inc(c_step, 1)
                        variance(c_step, c, 4, bnC, mvC, dfC)
                    if j == 6 and "A" in stages:
                        dve.wait_ge(a_qk_ps, a + 1)
                        nc.vector.tensor_tensor(qk[:].rearrange("p h d -> p (h d)"), psM[1][:], qkvb[:, 0:2 * D],
                                                ALU.add).then_inc(a_qk, 1)
                        dve.wait_ge(a_v_ps, a + 1)
                        nc.vector.tensor_tensor(vA[:].rearrange("p h d -> p (h d)"), psM[0][:, 0:D], qkvb[:, 2 * D:3 * D],
                                                ALU.add).then_inc(a_vps, 1)
                    if j == 7 and "A" in stages:
                        vt = V[:, bass.ds((a // TPB) % 2, 1), bass.ds(a % TPB, 1), :, :].rearrange("p a t h d -> p (a t h) d")
                        dve.wait_ge(a_vps, a + 1 + CREDIT)
                        nc.vector.tensor_copy(vt[:, :, 0:HD], vA[:]).then_inc(a_v, 1)
                        dve.wait_ge(a_v, a * 2 + 1)
                        nc.vector.tensor_tensor(vt[:, :, HD:2 * HD], vA[:], vt[:, :, 0:HD], ALU.subtract).then_inc(a_v, 1)
                    if j == 7 and "C" in stages:
                        dve.wait_ge(c_rstd, c + 1)
                        nc.vector.tensor_scalar(xnC[:], x1[:, u, :], mvC[:, 0:1], rsC[:, 0:1],
                                                ALU.subtract, ALU.mult).then_inc(c_xn, 1)
                    if j == 9 and "A" in stages:
                        dve.wait_ge(a_rope, a + 1)
                        nc.vector.tensor_tensor(rs_[:], rc[:], rc[:], ALU.mult).then_inc(a_step, 1)
                        dve.wait_ge(a_step, a * 6 + 5)
                        nc.vector.tensor_reduce(ss[:], rs_[:], AX.X, ALU.add).then_inc(a_ss, 1)
                    if j == 11 and "A" in stages:
                        dve.wait_ge(a_inv, a + 1)
                        nc.vector.scalar_tensor_tensor(out=rc[:], in0=inv[:].rearrange("p (h a) -> p h a", a=1).to_broadcast([P, 2 * H, HD]),
                                                       scalar=NORM_CAP, in1=rc[:], op0=ALU.min, op1=ALU.mult).then_inc(a_step, 1)
                        dve.wait_ge(a_step, a * 6 + 6)
                        for part in range(2):
                            for q in range(2):
                                dst = QK[:, bass.ds((a // TPB) % 2, 1), bass.ds(a % TPB, 1), q, :, :, :].rearrange(
                                    "p a t h f d -> p (a t h) f d")
                                full = rc[:, q * H:(q + 1) * H, :].rearrange("p h (a d) -> p h a d", a=1).to_broadcast([P, H, 2, HD])
                                hi = dst[:, :, 0:1, :].to_broadcast([P, H, 2, HD])
                                two = (dst[:, :, part::2, :], dst[:, :, 2 * part:2 * part + 2, :])[q]
                                if part == 0:
                                    ins = nc.vector.tensor_copy(two, full)
                                else:
                                    ins = nc.vector.tensor_tensor(two, full, hi, ALU.subtract)
                            ins.then_inc(a_split, 1)
                            if part == 0:
                                dve.wait_ge(a_split, a * 2 + 1)
                    if j == 12 and "C" in stages:
                        dve.wait_ge(c_h2T_ps, c + 1)
                        nc.vector.tensor_copy(h2T[:].rearrange("p k t -> p (k t)"), psM[0][:, 0:D]).then_inc(c_h2T, 1)
                    if j == 15 and "C" in stages:
                        dve.wait_ge(c_lg_ps, c + 1)
                        nc.vector.tensor_copy(LG[:, bass.ds(c, 1), :].rearrange("p a e -> p (a e)"), psM[1][:, 0:E]).then_inc(c_lg, 1)
                    if "T" in stages:
                        for i, at in enumerate(T_AT):
                            if j == at:
                                turned((u + 1) % 2, t, i)
                    if "B" not in stages:
                        continue
                    dve.wait_ge(b_exp, b * STEPS + (j + 1))
                    dve.wait_ge(b_pv, b * STEPS + (j + 1))
                    if j % 2:
                        nc.vector.tensor_copy(PH[:, j % 4, :], EX[:, j % 4, :]).then_inc(b_hi, 1)
                        dve.wait_ge(b_hi, b * (STEPS // 2) + (j // 2 + 1))
                    nc.vector.tensor_tensor(PL[:, j % 4, :], EX[:, j % 4, :], PH[:, j % 4, :], ALU.subtract).then_inc(b_split, 1)
                if "B" in stages:
                    for hh in range(2):
                        dve.wait_ge(b_pv, b * STEPS + (STEPS - 1 + hh + 4))
                        nc.vector.reciprocal(orec[:, hh, :], psO[hh][:, :, 2 * HD:HV].rearrange("p t a -> p (t a)")).then_inc(b_ostep, 1)
                        dve.wait_ge(b_ostep, b * 4 + (2 * hh + 1))
                        rec = orec[:, hh, :].rearrange("p (t a) -> p t a", a=1).to_broadcast([P, TPB, HD])
                        nc.vector.tensor_tensor(oh[:, hh, :, :], psO[hh][:, :, 0:HD], rec, ALU.mult)
                        nc.vector.tensor_tensor(ol[:, hh, :, :], psO[hh][:, :, HD:2 * HD], rec, ALU.mult).then_inc(b_ostep, 1)
                        dve.wait_ge(b_ostep, b * 4 + (2 * hh + 2))
                        dst = AT[:, bass.ds((b // PAIRS) % 2, 1), :, bass.ds((b % PAIRS) * (2 * HD) + hh * HD, HD)].rearrange(
                            "p a t d -> p (a t) d")
                        nc.vector.tensor_tensor(dst, oh[:, hh, :, :], ol[:, hh, :, :], ALU.add).then_inc(b_o, 1)
            phases(dve, body)

        @block.tensor
        def _(pe):
            pe.sem_inc(b_pv, 4)
            pe.sem_inc(b_split, 4)
            for free in (a_hT, a_vps, a_qk, c_at, c_x1, c_at_ps, c_h2T, c_lg):
                pe.sem_inc(free, CREDIT)
            pe.sem_inc(b_o, 2)
            for u in range(2):
                pe.sem_inc(c_st[u], 32)
            pe.wait_ge(silu_done, 3)
            for n in range(3):
                for k in range(KD):
                    mm = nc.tensor.matmul((psM[0], psM[1], psS[1])[n][0:B, 0:512], cs[:, k, :], wm[:, k, n * 512:(n + 1) * 512],
                                          start=(k == 0), stop=(k == KD - 1))
            for n in range(2 * KD):
                for k in range(KD):
                    mm = nc.tensor.matmul(psS[0][:, n * B:(n + 1) * B], wm[:, k, n * P:(n + 1) * P], cs[:, k, :],
                                          start=(k == 0), stop=(k == KD - 1))
            mm.then_inc(mod_ps, 1)
            pe.wait_ge(mod_ready, 1)
            pe.wait_ge(s_w, 16 * 8)
            pe.wait_ge(setup, 5)

            def free_bank(me, stages, a, t, c):
                for order in (["hT", "v", "T1", "h2T", "T3"], ["at", "proj", "qk", "T0", "T2", "lg"]):
                    if me not in order:
                        continue
                    i = order.index(me)
                    for back in range(1, len(order) + 1):
                        prev = order[(i - back) % len(order)]
                        new = 0 if back > i else 1
                        if prev in ("hT", "v", "qk") and "A" in stages:
                            pe.wait_ge({"hT": a_hT, "v": a_vps, "qk": a_qk}[prev], a + new + CREDIT)
                            return
                        if prev in ("at", "proj", "h2T", "lg") and "C" in stages:
                            pe.wait_ge({"at": c_at, "proj": c_x1, "h2T": c_h2T, "lg": c_lg}[prev], c + new + CREDIT)
                            return
                        if prev[0] == "T" and "T" in stages:
                            pe.wait_ge(t_ev, (t + (new - 1)) * 4 + (int(prev[1]) + 1))
                            return

            def scores(u, j):
                kt, hh = j // 2, j % 2
                rows = slice(64 * hh, 64 * hh + 64)
                for q in range(QCH):
                    mm = nc.tensor.matmul(psS[j % 2][:, q * 512:(q + 1) * 512], KT[rows, u, kt * P:(kt + 1) * P],
                                          QT[rows, u, q * 512:(q + 1) * 512], start=True, stop=True)
                mm.then_inc(b_scores, 1)

            def turn(stages, a, t, c, i):
                if stages:
                    free_bank(f"T{i}", stages, a, t, c)
                q, half = i % 2, i // 2
                bank = psM[(1, 0)[q]]
                bat = t // PAIRS
                pe.wait_ge(a_split, (bat * TPB + 4 * half + 4) * 2)
                for n in range(4):
                    lhsT = QK[:, bass.ds(bat % 2, 1), 4 * half + n, q, bass.ds((t % PAIRS) * 2, 2), :, :].rearrange(
                        "p a h f d -> p (a h f d)")
                    mm = nc.tensor.matmul(bank[:, n * P:(n + 1) * P], lhsT, idn16[:], start=True, stop=True)
                mm.then_inc(t_ps, 1)

            def body(stages, u, a, t, b, c):
                if stages == "T1":
                    pe.wait_ge(a_vps, TPB + CREDIT)
                    pe.wait_ge(a_qk, TPB + CREDIT)
                    for i in range(4):
                        if i >= 2:
                            pe.wait_ge(t_ev, i - 1)
                        turn("", a, 0, c, i)
                    pe.wait_ge(t_ev, 4)
                    scores(0, 0)
                    scores(0, 1)
                    return
                for j in range(STEPS):
                    if j == 2 and "C" in stages:
                        pe.wait_ge(c_copy, c + 1)
                        free_bank("at", stages, a, t, c)
                        for k in range(KD):
                            mm = nc.tensor.transpose(psM[1][:, k * P:(k + 1) * P], aS[:, k * P:(k + 1) * P], idn[:])
                        mm.then_inc(c_at_ps, 1)
                    if j == 3 and "A" in stages:
                        pe.wait_ge(a_xn, a + 1)
                        free_bank("hT", stages, a, t, c)
                        for k in range(KD):
                            mm = nc.tensor.transpose(psM[0][:, k * P:(k + 1) * P], xnA[:, k * P:(k + 1) * P], idn[:])
                        mm.then_inc(a_hT_ps, 1)
                    if j == 4 and "C" in stages:
                        pe.wait_ge(c_at, c + 1 + CREDIT)
                        for k in range(KD):
                            mm = nc.tensor.matmul(psM[1][:, 0:D], aT[:, k, :],
                                                  wog[:, bass.ds(c // TPB, 1), k, :].rearrange("p a d -> p (a d)"),
                                                  start=(k == 0), stop=(k == KD - 1))
                        mm.then_inc(c_proj, 1)
                    if j == 5 and "A" in stages:
                        pe.wait_ge(a_hT, a + 1 + CREDIT)
                        for k in range(KD):
                            mm = nc.tensor.matmul(psM[0][:, 0:D], hTA[:, k, :], wqkv[:, k, 2 * D:3 * D],
                                                  start=(k == 0), stop=(k == KD - 1))
                        mm.then_inc(a_v_ps, 1)
                    if j == 6 and "A" in stages:
                        free_bank("qk", stages, a, t, c)
                        for k in range(KD):
                            mm = nc.tensor.matmul(psM[1][:, :], hTA[:, k, :], wqkv[:, k, 0:2 * D],
                                                  start=(k == 0), stop=(k == KD - 1))
                        mm.then_inc(a_qk_ps, 1)
                    if j == 11 and "C" in stages:
                        pe.wait_ge(c_h2, c * 2 + 2)
                        free_bank("h2T", stages, a, t, c)
                        for k in range(KD):
                            mm = nc.tensor.transpose(psM[0][:, k * P:(k + 1) * P], h2[:, u, k * P:(k + 1) * P], idn[:])
                        mm.then_inc(c_h2T_ps, 1)
                    if j == 14 and "C" in stages:
                        free_bank("lg", stages, a, t, c)
                        pe.wait_ge(c_h2T, c + 1 + CREDIT)
                        for k in range(KD):
                            mm = nc.tensor.matmul(psM[1][:, 0:E], h2T[:, k, :], gw[:, k, :], start=(k == 0), stop=(k == KD - 1))
                        mm.then_inc(c_lg_ps, 1)
                    if "T" in stages:
                        for i, at in enumerate(T_AT):
                            if j == at:
                                turn(stages, a, t, c, i)
                    if "B" not in stages:
                        continue
                    pe.wait_ge(b_exp, b * STEPS + (j + 1))
                    if j + 2 < STEPS:
                        scores(u, j + 2)
                    elif "T" in stages:
                        if j + 2 == STEPS:
                            pe.wait_ge(t_ev, t * 4 + 4)
                        scores((u + 1) % 2, j + 2 - STEPS)
                    kt, hh = j // 2, j % 2
                    if kt == 0:
                        pe.wait_ge(b_o, b * 2 + (hh + 1))
                    pe.wait_ge(b_split, b * STEPS + (j + 1 + 4))
                    rhs = V[:, bass.ds((b // PAIRS) % 2, 1), kt, bass.ds((b % PAIRS) * 2 + hh, 1), :].rearrange(
                        "p a h d -> p (a h d)")
                    for q in range(TPB):
                        for part in (PH, PL):
                            mm = nc.tensor.matmul(psO[hh][:, q, 0:HV], part[:, j % 4, q * P:(q + 1) * P], rhs,
                                                  start=(kt == 0 and q == 0 and part is PH), stop=(kt == TPB - 1),
                                                  skip_group_check=True)
                    mm.then_inc(b_pv, 1)
            phases(pe, body)


def experts(nc, w1, w2, w3, ident, below, counts, mod_dram, x1_dram, h2_dram, xs_dram, ys_dram, LG, out):
    with ExitStack() as ctx:
        def sb(name, shape, dt=F32):
            return ctx.enter_context(nc.sbuf_tensor(name, shape, dt))

        def sem(name):
            return ctx.enter_context(nc.semaphore(name))

        NE = [P, NT, E]
        H2 = sb("H2", [P, NT, D])
        X1 = sb("X1", [P, NT, D])
        gbB = sb("gbB", [P, B, D])
        zero = sb("zero", [P, D])
        eye = sb("eye", [P, P])
        bel = sb("bel", [P, 2, P])
        cnt = sb("cnt", [P, 64])
        key = sb("key", NE)
        hot = sb("hot", [P, 2, NT, E])
        both = sb("both", NE)
        lg2 = sb("lg2", NE)
        tmp = sb("tmp", NE)
        keep = sb("keep", [P, 2, NT, E])
        dif = sb("dif", [P, 2, NT, E])
        scan = sb("scan", [P, 2, NT, E])
        cum = sb("cum", NE)
        val = sb("val", [P, 2, NT])
        kmax = sb("kmax", [P, NT])
        mult = sb("mult", [P, 2, NT])
        posf = sb("posf", [P, 2, NT])
        pos = sb("pos", [P, 2, NT], mybir.dt.uint32)
        ge = sb("ge", [P, E, 16])
        nblk = sb("nblk", [P, E])
        first = sb("first", [P, 4, E])
        blk = sb("blk", [P, BLOCKS + 1, E])
        blkf = sb("blkf", [P, BLOCKS + 1])
        blki = sb("blki", [P, BLOCKS + 1], mybir.dt.int32)
        W1 = sb("W1", [P, 2, KD, F])
        W3 = sb("W3", [P, 2, KD, F])
        W2 = sb("W2", [P, 2, FC, D])
        xr = sb("xr", [P, 2, RC, D])
        xT = sb("xT", [P, KD, ROWS])
        sg = sb("sg", [P, 2, ROWS])
        hd = sb("hd", [P, 2, FC, ROWS])
        yr = sb("yr", [P, 2, RC, D])
        ya = sb("ya", [P, 2, 2, D])
        yo = sb("yo", [P, 2, D])

        psR = ctx.enter_context(nc.psum_tensor("psR", [P, 2, NT, E], F32))
        psX = ctx.enter_context(nc.psum_tensor("psX", [P, KD, ROWS], F32))
        psG = [ctx.enter_context(nc.psum_tensor(f"psG{i}", [P, 2, ROWS], F32)) for i in range(3)]
        psY = [ctx.enter_context(nc.psum_tensor(f"psY{i}", [P, RC, D], F32)) for i in range(2)]

        s_in = sem("s_in")
        s_h2 = sem("s_h2")
        s_x1 = sem("s_x1")
        s_zero = sem("s_zero")
        z_ready = sem("z_ready")
        s_blk = sem("s_blk")
        r_step = sem("r_step")
        r_dif = sem("r_dif")
        r_exp = sem("r_exp")
        r_hot = sem("r_hot")
        r_cum = sem("r_cum")
        r_pos = sem("r_pos")
        r_sent = sem("r_sent")
        s_w = [sem(f"s_w{u}") for u in range(2)]
        s_xr = [sem(f"s_xr{u}") for u in range(2)]
        m_xT_ps = sem("m_xT_ps")
        m_xT = sem("m_xT")
        m_gu = sem("m_gu")
        m_sg = sem("m_sg")
        m_h = sem("m_h")
        m_y_ps = sem("m_y_ps")
        m_y = sem("m_y")
        s_ys = [sem(f"s_ys{u}") for u in range(2)]
        f_y = [sem(f"f_y{u}") for u in range(2)]
        f_step = sem("f_step")
        s_out = [sem(f"s_out{u}") for u in range(2)]

        rows = lambda d: d.rearrange("(g p) d -> p g d", p=P)
        w1_v = w1.rearrange("e (k p) f -> p (e k) f", p=P)
        w3_v = w3.rearrange("e (k p) f -> p (e k) f", p=P)
        w2_v = w2.rearrange("e (f p) d -> p (e f) d", p=P)
        ys_v = ys_dram.rearrange("(g p) d -> p g d", p=P)
        xs_v = xs_dram.rearrange("(g p) d -> p g d", p=P)

        def blocks(eng, body):
            with eng.Fori(0, BLOCKS // 2) as it:
                for u in range(2):
                    body(u, it * 2 + u)
            if BLOCKS % 2:
                body(0, BLOCKS - 1)

        block = ctx.enter_context(nc.Block())

        @block.sync
        def _(sp):
            sp.dma_start(bel[:], below).then_inc(s_in, 16)
            sp.dma_start(cnt[:], counts).then_inc(s_in, 16)
            sp.dma_start(eye[:], ident).then_inc(s_in, 16)
            m6 = mod_dram.rearrange("(a b) (s d) -> a b s d", a=1, s=6)
            sp.dma_start(gbB[:], m6[:, :, GB, :].to_broadcast([P, B, D])).then_inc(s_in, 16)
            sp.dma_start(H2[:], rows(h2_dram)).then_inc(s_h2, 16)
            sp.dma_start(X1[:], rows(x1_dram)).then_inc(s_x1, 16)
            sp.wait_ge(z_ready, 1)
            sp.dma_start(xs_v, zero[:].rearrange("p (a d) -> p a d", a=1).to_broadcast([P, BLOCKS * RC, D])).then_inc(s_zero, 16)
            sp.wait_ge(s_blk, 1)

            def body(u, i):
                e = sp.value_load(blki[0:1, bass.ds(i, 1)], min_val=0, max_val=E - 1)
                sp.wait_ge(m_y_ps, i + 1)
                sp.dma_start(W1[:, u, :, :], w1_v[:, bass.ds(e * KD, KD), :]).then_inc(s_w[u], 16)
                sp.dma_start(W3[:, u, :, :], w3_v[:, bass.ds(e * KD, KD), :]).then_inc(s_w[u], 16)
                sp.dma_start(W2[:, u, :, :], w2_v[:, bass.ds(e * FC, FC), :]).then_inc(s_w[u], 16)
                sp.wait_ge(r_sent, 2 * NT * 16)
                sp.dma_start(xr[:, u, :, :], xs_v[:, bass.ds(i * RC, RC), :]).then_inc(s_xr[u], 16)
            blocks(sp, body)
            for t in range(NT):
                sp.wait_ge(f_step, 4 * t + 4)
                sp.dma_start(rows(out.rearrange("b s d -> (b s) d"))[:, t, :], yo[:, t % 2, :]).then_inc(s_out[t % 2], 16)
            for u in range(2):
                sp.wait_ge(s_out[u], 16 * NT // 2)

        @block.scalar
        def _(act):
            act.wait_ge(r_dif, 1)
            nc.scalar.activation(dif[:], dif[:], ACT.Exp).then_inc(r_exp, 1)

            def body(u, i):
                for f in range(FC):
                    act.wait_ge(m_gu, i * FC + (f + 1))
                    act.wait_ge(m_h, i * FC + (f + 1))
                    nc.scalar.activation(sg[:, f % 2, :], psG[f % 2][:, 0, :], ACT.Silu).then_inc(m_sg, 1)
                act.wait_ge(m_y_ps, i + 3)
                act.wait_ge(s_ys[u], 16 * (i // 2) + 16)
                nc.scalar.copy(yr[:, u, :, :], psY[u][:]).then_inc(m_y, 1)
                act.wait_ge(m_y, i + 2)
                act.dma_start(ys_v[:, bass.ds(i * RC, RC), :], yr[:, u, :, :]).then_inc(s_ys[u], 16)
            blocks(act, body)
            act.wait_ge(s_ys[0], 16 * (BLOCKS // 2 + 2))
            act.wait_ge(s_ys[1], 16 * (BLOCKS // 2 + 1))

        @block.gpsimd
        def _(pool):
            pool.wait_ge(s_h2, 16)
            pool.wait_ge(s_zero, 16)
            pool.wait_ge(r_pos, 1)
            for t in range(NT):
                for n in range(2):
                    nc.gpsimd.indirect_dma_start(xs_dram, bass.IndirectOffsetOnAxis(ap=pos[:, n, t:t + 1], axis=0),
                                                 H2[:, t, :], None).then_inc(r_sent, 16)
            pool.wait_ge(s_ys[0], 16 * (BLOCKS // 2 + 2))
            pool.wait_ge(s_ys[1], 16 * (BLOCKS // 2 + 1))
            for t in range(NT):
                if t >= 2:
                    pool.wait_ge(f_step, 4 * (t - 1) - 1)
                for n in range(2):
                    nc.gpsimd.indirect_dma_start(ya[:, t % 2, n, :], None, ys_dram,
                                                 bass.IndirectOffsetOnAxis(ap=pos[:, n, t:t + 1], axis=0)).then_inc(f_y[t % 2], 16)

        @block.vector
        def _(dve):
            steps = [0]

            def link(ins):
                steps[0] += 1
                ins.then_inc(r_step, 1)
                dve.wait_ge(r_step, steps[0])

            def over(a, n=NT):
                return a.rearrange("p (t a) -> p t a", a=1).to_broadcast([P, n, E])

            nc.vector.memset(zero[:], 0.0).then_inc(z_ready, 1)
            dve.wait_ge(s_in, 64)
            order = cnt[:, 0:E].rearrange("p (a e) -> p a e", a=1).to_broadcast(NE)
            for n in range(2):
                src = (LG, lg2)[n]
                link(nc.vector.tensor_reduce(val[:, n, :], src[:], AX.X, ALU.max))
                link(nc.vector.tensor_tensor(key[:], src[:], over(val[:, n, :]), ALU.is_equal))
                link(nc.vector.tensor_tensor(key[:], key[:], order, ALU.mult))
                link(nc.vector.tensor_reduce(kmax[:], key[:], AX.X, ALU.max))
                link(nc.vector.tensor_tensor(hot[:, n, :, :], key[:], over(kmax[:]), ALU.is_equal))
                link(nc.vector.scalar_tensor_tensor(out=tmp[:], in0=LG[:], scalar=-1.0, in1=LG[:], op0=ALU.mult, op1=ALU.max))
                link(nc.vector.tensor_tensor(tmp[:], tmp[:], over(val[:, n, :]), ALU.max))
                link(nc.vector.tensor_tensor(keep[:, n, :, :], over(val[:, n, :]), LG[:], ALU.subtract))
                link(nc.vector.scalar_tensor_tensor(out=keep[:, n, :, :], in0=tmp[:], scalar=2.0 * JITTER, in1=keep[:, n, :, :],
                                                    op0=ALU.mult, op1=ALU.is_ge))
                link(nc.vector.tensor_tensor(dif[:, n, :, :], src[:], over(val[:, n, :]), ALU.subtract))
                if n == 0:
                    link(nc.vector.tensor_scalar(tmp[:], hot[:, 0, :, :], -1.0, 1.0, ALU.mult, ALU.add))
                    link(nc.vector.tensor_tensor(tmp[:], tmp[:], LG[:], ALU.mult))
                    link(nc.vector.scalar_tensor_tensor(out=lg2[:], in0=hot[:, 0, :, :], scalar=LOWEST, in1=tmp[:],
                                                        op0=ALU.mult, op1=ALU.add))
            nc.vector.tensor_tensor(both[:], hot[:, 0, :, :], hot[:, 1, :, :], ALU.add).then_inc(r_hot, 1)
            nc.vector.tensor_copy(tmp[:], tmp[:]).then_inc(r_dif, 1)
            dve.wait_ge(r_cum, 1)
            nc.vector.tensor_copy(cum[:], psR[:, 0, :, :])
            link(nc.vector.tensor_copy(scan[:, 0, :, :], psR[:, 1, :, :]))
            link(nc.vector.tensor_copy(tmp[:], psR[:, 1, :, :]))
            src, shift = 0, 1
            while shift < NT:
                nc.vector.tensor_copy(scan[:, 1 - src, 0:shift, :], scan[:, src, 0:shift, :])
                link(nc.vector.tensor_tensor(scan[:, 1 - src, shift:NT, :], scan[:, src, shift:NT, :],
                                             scan[:, src, 0:NT - shift, :], ALU.add))
                src, shift = 1 - src, 2 * shift
            total = scan[:, src, NT - 1, :]
            link(nc.vector.tensor_tensor(tmp[:], scan[:, src, :, :], tmp[:], ALU.subtract))
            link(nc.vector.tensor_tensor(cum[:], cum[:], tmp[:], ALU.add))
            link(nc.vector.tensor_tensor(ge[:], total.rearrange("p (e a) -> p e a", a=1).to_broadcast([P, E, 16]),
                                         cnt[:, 8:24].rearrange("p (a j) -> p a j", a=1).to_broadcast([P, E, 16]), ALU.is_gt))
            link(nc.vector.tensor_reduce(nblk[:], ge[:], AX.X, ALU.add))
            link(nc.vector.tensor_copy(first[:, 0, :], nblk[:]))
            src, shift = 0, 1
            while shift < E:
                nc.vector.tensor_copy(first[:, 1 - src, 0:shift], first[:, src, 0:shift])
                link(nc.vector.tensor_tensor(first[:, 1 - src, shift:E], first[:, src, shift:E], first[:, src, 0:E - shift], ALU.add))
                src, shift = 1 - src, 2 * shift
            end = first[:, src, :]
            link(nc.vector.tensor_tensor(first[:, 2, :], end, nblk[:], ALU.subtract))
            link(nc.vector.tensor_scalar(first[:, 3, :], first[:, 2, :], float(ROWS), None, ALU.mult))
            link(nc.vector.tensor_tensor(blk[:], end.rearrange("p (a e) -> p a e", a=1).to_broadcast([P, BLOCKS + 1, E]),
                                         cnt[:, 24:64].rearrange("p (t a) -> p t a", a=1)[:, 0:BLOCKS + 1, :].to_broadcast([P, BLOCKS + 1, E]),
                                         ALU.is_le))
            link(nc.vector.tensor_reduce(blkf[:], blk[:], AX.X, ALU.add))
            nc.vector.tensor_scalar(blki[:], blkf[:], float(E - 1), None, ALU.min).then_inc(s_blk, 1)
            link(nc.vector.tensor_tensor(cum[:], cum[:], first[:, 3, :].rearrange("p (a e) -> p a e", a=1).to_broadcast(NE), ALU.add))
            for n in range(2):
                link(nc.vector.tensor_tensor(tmp[:], cum[:], hot[:, n, :, :], ALU.mult))
                link(nc.vector.tensor_reduce(posf[:, n, :], tmp[:], AX.X, ALU.add))
            nc.vector.tensor_copy(pos[:], posf[:]).then_inc(r_pos, 1)
            dve.wait_ge(r_exp, 1)
            for n in range(2):
                link(nc.vector.tensor_tensor(tmp[:], dif[:, n, :, :], keep[:, n, :, :], ALU.mult))
                link(nc.vector.tensor_reduce(val[:, n, :], tmp[:], AX.X, ALU.add))
            link(nc.vector.reciprocal(mult[:], val[:]))

            def body(u, i):
                dve.wait_ge(m_xT_ps, i + 1)
                nc.vector.tensor_copy(xT[:], psX[:]).then_inc(m_xT, 1)
                for f in range(FC):
                    dve.wait_ge(m_sg, i * FC + (f + 1))
                    nc.vector.tensor_tensor(hd[:, u, f, :], sg[:, f % 2, :], psG[f % 2][:, 1, :], ALU.mult).then_inc(m_h, 1)
            blocks(dve, body)
            dve.wait_ge(s_x1, 16)
            for t in range(NT):
                y = ya[:, t % 2, :, :]
                dve.wait_ge(f_y[t % 2], 32 * (t // 2 + 1))
                if t >= 2:
                    dve.wait_ge(s_out[t % 2], 16 * (t // 2))
                nc.vector.tensor_scalar(yo[:, t % 2, :], y[:, 0, :], mult[:, 0, t:t + 1], None, ALU.mult).then_inc(f_step, 1)
                dve.wait_ge(f_step, 4 * t + 1)
                nc.vector.scalar_tensor_tensor(out=yo[:, t % 2, :], in0=y[:, 1, :], scalar=mult[:, 1, t:t + 1], in1=yo[:, t % 2, :],
                                               op0=ALU.mult, op1=ALU.add).then_inc(f_step, 1)
                dve.wait_ge(f_step, 4 * t + 2)
                nc.vector.tensor_tensor(yo[:, t % 2, :], yo[:, t % 2, :], gbB[:, t // TPB, :], ALU.mult).then_inc(f_step, 1)
                dve.wait_ge(f_step, 4 * t + 3)
                nc.vector.tensor_tensor(yo[:, t % 2, :], yo[:, t % 2, :], X1[:, t, :], ALU.add).then_inc(f_step, 1)

        @block.tensor
        def _(pe):
            pe.sem_inc(m_y_ps, 2)
            pe.sem_inc(m_h, 2)
            pe.sem_inc(m_y, 1)
            for u in range(2):
                pe.sem_inc(s_ys[u], 16)
            pe.wait_ge(s_in, 64)
            pe.wait_ge(r_hot, 1)
            for n in range(2):
                mm = nc.tensor.matmul(psR[:, n, :, :].rearrange("p t e -> p (t e)"), bel[:, n, :], both[:].rearrange("p t e -> p (t e)"),
                                      start=True, stop=True)
            mm.then_inc(r_cum, 1)

            def body(u, i):
                pe.wait_ge(s_xr[u], 16 * (i // 2) + 16)
                for r in range(RC):
                    for k in range(KD):
                        mm = nc.tensor.transpose(psX[:, k, r * P:(r + 1) * P], xr[:, u, r, k * P:(k + 1) * P], eye[:])
                mm.then_inc(m_xT_ps, 1)
                pe.wait_ge(s_w[u], 48 * (i // 2) + 48)
                pe.wait_ge(m_xT, i + 1)
                for f in range(FC):
                    pe.wait_ge(m_h, i * FC + (f + 1))
                    for n, w in enumerate((W1, W3)):
                        for k in range(KD):
                            mm = nc.tensor.matmul(psG[f % 2][:, n, :], w[:, u, k, f * P:(f + 1) * P], xT[:, k, :],
                                                  start=(k == 0), stop=(k == KD - 1), skip_group_check=True)
                    mm.then_inc(m_gu, 1)
                pe.wait_ge(m_y, i + 1)
                for f in range(FC):
                    pe.wait_ge(m_h, i * FC + (f + 3))
                    for r in range(RC):
                        mm = nc.tensor.matmul(psY[u][:, r, :], hd[:, u, f, r * P:(r + 1) * P], W2[:, u, f, :],
                                              start=(f == 0 and r == 0), stop=(f == FC - 1), skip_group_check=True)
                mm.then_inc(m_y_ps, 1)
            blocks(pe, body)


def kernel(**inputs):
    import numpy as np
    import concourse.bacc as bacc
    from concourse.bass_utils import run_bass_kernel_spmd as run

    pos = np.arange(S, dtype=np.float32)
    freq = (np.float32(1.0) / np.float32(2500) ** (np.arange(HD // 2, dtype=np.float32) / np.float32(HD // 2))).astype(np.float32)
    theta = pos[:, None] * freq[None, :]
    rope = np.stack([np.repeat(np.cos(theta), 2, axis=1),
                     np.stack([-np.sin(theta), np.sin(theta)], axis=2).reshape(S, HD)], axis=1)
    rope = np.ascontiguousarray(rope.reshape(TPB, P, 2, HD).transpose(1, 0, 2, 3)).astype(np.float32)
    below = np.stack([np.triu(np.ones((P, P), np.float32), 1), np.ones((P, P), np.float32)], axis=1)
    below = np.ascontiguousarray(below)
    counts = np.concatenate([E - np.arange(E), np.arange(16) * ROWS, np.arange(40)]).astype(np.float32)
    counts = np.ascontiguousarray(np.tile(counts, (P, 1)))
    arrays = {
        "x": np.ascontiguousarray(inputs["L0_attn_tokens"]),
        "qkv_wT": np.ascontiguousarray(np.asarray(inputs["L0_attn_qkv_w"]).T),
        "qkv_b": np.ascontiguousarray(inputs["L0_attn_qkv_b"]),
        "out_wT": np.ascontiguousarray(np.asarray(inputs["L0_attn_out_w"]).T),
        "out_b": np.ascontiguousarray(inputs["L0_attn_out_b"]),
        "cT": np.ascontiguousarray(np.asarray(inputs["L0_c"]).T),
        "wmod": np.ascontiguousarray(inputs["L0_wmod"]),
        "gate_w": np.ascontiguousarray(inputs["L0_ffn_gate_w"]),
        "w1": np.ascontiguousarray(inputs["L0_ffn_w1"]),
        "w2": np.ascontiguousarray(inputs["L0_ffn_w2"]),
        "w3": np.ascontiguousarray(inputs["L0_ffn_w3"]),
        "ident": np.eye(P, dtype=np.float32),
        "ident16": np.eye(P, dtype=np.float16),
        "rope": rope,
        "below": below,
        "counts": counts,
    }
    nc = bacc.Bacc("TRN2", target_bir_lowering=False, num_devices=1)
    args = [nc.dram_tensor(n, a.shape, mybir.dt.from_np(a.dtype), kind="ExternalInput").ap() for n, a in arrays.items()]
    args.append(nc.dram_tensor("y", (B, S, D), F32, kind="ExternalOutput").ap())
    adaln(nc, *args)
    r = run(nc, [arrays], core_ids=[0])
    return r.results[0]["y"]
```

```python
from contextlib import ExitStack

import concourse.bass as bass
from concourse import mybir

F32 = mybir.dt.float32
F16 = mybir.dt.float16
ALU = mybir.AluOpType
ACT = mybir.ActivationFunctionType
AX = mybir.AxisListType

P = 128
B, S, D = 4, 1024, 256
H, HD = 16, 16
KD = D // P
TPB = S // P
NT = B * TPB
PAIRS = H // 2
HV = 2 * HD + 1
STEPS = 2 * TPB
T_AT = (7, 9, 12, 15)
LO_POOL = (0, 4, 10, 12, 14)
LO_DVE = tuple(j for j in range(STEPS) if j not in LO_POOL)
QCH = S // 512
LN_EPS = 1e-5
CREDIT = 1
NORM_CAP = 1e12
SCALE = HD ** -0.5
E, F = 8, 1024
FC = F // P
ROWS = 256
RC = ROWS // P
BLOCKS = (2 * B * S + E * (ROWS - 1)) // ROWS
JITTER = 0.01
LOWEST = -3.0e38
GU = 2
STEPS_E = FC // GU
WS = 64.0
SA, CA, GA, SB, CB, GB = range(6)


def adaln(nc, x, qkv_wT, qkv_b, out_wT, out_b, cT, wmod, gate_w, w1, w2, w3, ident, ident16, rope, below, counts, out):
    mod_dram = nc.dram_tensor("mod_dram", (B, 6 * D), F32, kind="Internal").ap()
    x1_dram = nc.dram_tensor("x1_dram", (B * S, D), F32, kind="Internal").ap()
    h2_dram = nc.dram_tensor("h2_dram", (B * S, D), F32, kind="Internal").ap()

    xs_dram = nc.dram_tensor("xs_dram", (BLOCKS * ROWS, D), F32, kind="Internal").ap()
    ys_dram = nc.dram_tensor("ys_dram", (BLOCKS * ROWS, D), F32, kind="Internal").ap()

    with ExitStack() as whole:
        LG = whole.enter_context(nc.sbuf_tensor("LG", [P, NT, E], F32))
        attention(nc, x, qkv_wT, qkv_b, out_wT, out_b, cT, wmod, gate_w, ident, ident16, rope, mod_dram, x1_dram, h2_dram, LG)
        experts(nc, w1, w2, w3, ident, below, counts, mod_dram, x1_dram, h2_dram, xs_dram, ys_dram, LG, out)


def attention(nc, x, qkv_wT, qkv_b, out_wT, out_b, cT, wmod, gate_w, ident, ident16, rope, mod_dram, x1_dram, h2_dram, LG):
    with ExitStack() as ctx:
        def sb(name, shape, dt=F32):
            return ctx.enter_context(nc.sbuf_tensor(name, shape, dt))

        def sem(name):
            return ctx.enter_context(nc.semaphore(name))

        modB = sb("modB", [P, B, 2, D])
        idn = sb("idn", [P, P])
        idn16 = sb("idn16", [P, P], F16)
        wqkv = sb("wqkv", [P, KD, 3 * D])
        qkvb = sb("qkvb", [P, 3 * D])
        wo = sb("wo", [P, KD, D])
        wog = sb("wog", [P, B, KD, D])
        ob = sb("ob", [P, D])
        gob = sb("gob", [P, B, D])
        rp = sb("rp", [P, TPB, 2, HD])
        ct = sb("ct", [P, KD, B])
        ce = sb("ce", [P, KD, B])
        cs = sb("cs", [P, KD, B])
        modT = sb("modT", [P, 2, KD, B])
        xA = sb("xA", [P, 2, D])
        xC = sb("xC", [P, 2, D])
        mod = sb("mod", [B, 6 * D])
        sgn = sb("sgn", [B, 2, D])
        eps = sb("eps", [P, 1])
        mhalf = sb("mhalf", [P, 2 * H])
        bnA = sb("bnA", [P, 6])
        dfA = sb("dfA", [P, 3])
        mvA = sb("mvA", [P, 2])
        veA = sb("veA", [P, 1])
        rsA = sb("rsA", [P, 1])
        xnA = sb("xnA", [P, D])
        hTA = sb("hTA", [P, KD, P])
        qk = sb("qk", [P, 2 * H, HD])
        rc = sb("rc", [P, 2 * H, HD])
        rs_ = sb("rs_", [P, 2 * H, HD])
        ss = sb("ss", [P, 2 * H])
        inv = sb("inv", [P, 2 * H])
        QK = sb("QK", [P, 2, TPB, 2, H, 4, HD], F16)
        V = sb("V", [P, 2, TPB, H, HV], F16)
        vA = sb("vA", [P, H, HD])
        EX = sb("EX", [P, 4, S])
        PH = sb("PH", [P, 4, S], F16)
        PL = sb("PL", [P, 4, S], F16)
        wm = EX[:, 0:3, :].rearrange("p a n -> p (a n)").rearrange("p (k n) -> p k n", k=KD)
        gaB = EX[:, 3, :].rearrange("p (b d) -> p b d", b=B)
        QT = sb("QT", [P, 2, S], F16)
        KT = sb("KT", [P, 2, S], F16)
        orec = sb("orec", [P, 2, TPB])
        osum = sb("osum", [P, 2, TPB, HD])
        AT = sb("AT", [P, 2, TPB, D])
        aS = sb("aS", [P, D])
        aT = sb("aT", [P, KD, P])
        xg = sb("xg", [P, D])
        x1 = sb("x1", [P, 2, D])
        bnC = sb("bnC", [P, 6])
        dfC = sb("dfC", [P, 3])
        mvC = sb("mvC", [P, 2])
        veC = sb("veC", [P, 1])
        rsC = sb("rsC", [P, 1])
        xnC = sb("xnC", [P, D])
        h2 = sb("h2", [P, 2, D])
        h2T = sb("h2T", [P, KD, P])
        gw = sb("gw", [P, KD, E])

        psS = [ctx.enter_context(nc.psum_tensor(f"psS{i}", [P, S], F32)) for i in range(2)]
        psO = [ctx.enter_context(nc.psum_tensor(f"psO{i}", [P, TPB, 64], F32)) for i in range(2)]
        psM = [ctx.enter_context(nc.psum_tensor(f"psM{i}", [P, 512], F32)) for i in range(2)]

        s_xA = [sem(f"s_xA{u}") for u in range(2)]
        s_xC = [sem(f"s_xC{u}") for u in range(2)]
        s_w = sem("s_w")
        s_modw = sem("s_modw")
        s_modb = sem("s_modb")
        setup = sem("setup")
        silu_exp = sem("silu_exp")
        silu_done = sem("silu_done")
        mod_ps = sem("mod_ps")
        mod_ready = sem("mod_ready")
        a_step = sem("a_step")
        a_rstd = sem("a_rstd")
        a_pool = sem("a_pool")
        a_turn = sem("a_turn")
        a_norm = sem("a_norm")
        a_sq = sem("a_sq")
        a_xn = sem("a_xn")
        a_hT_ps = sem("a_hT_ps")
        a_hT = sem("a_hT")
        a_qk_ps = sem("a_qk_ps")
        a_v_ps = sem("a_v_ps")
        a_qk = sem("a_qk")
        a_vps = sem("a_vps")
        a_v = sem("a_v")
        a_rope = sem("a_rope")
        a_ss = sem("a_ss")
        a_inv = sem("a_inv")
        a_split = sem("a_split")
        t_ps = sem("t_ps")
        t_q = sem("t_q")
        t_k = sem("t_k")
        b_scores = sem("b_scores")
        b_exp = sem("b_exp")
        b_hi = sem("b_hi")
        b_split = sem("b_split")
        p_split = sem("p_split")
        b_pv = sem("b_pv")
        b_ostep = sem("b_ostep")
        b_o = sem("b_o")
        c_copy = sem("c_copy")
        c_at_ps = sem("c_at_ps")
        c_at = sem("c_at")
        c_proj = sem("c_proj")
        c_xg = sem("c_xg")
        c_x1 = sem("c_x1")
        c_step = sem("c_step")
        c_var = sem("c_var")
        c_pool = sem("c_pool")
        c_rstd = sem("c_rstd")
        c_xn = sem("c_xn")
        c_h2 = sem("c_h2")
        c_st = [sem(f"c_st{u}") for u in range(2)]
        c_h2T_ps = sem("c_h2T_ps")
        c_h2T = sem("c_h2T")
        c_lg_ps = sem("c_lg_ps")
        c_lg = sem("c_lg")

        x_v = x.rearrange("b (t p) d -> p (b t) d", p=P)

        PHASES = [("LAR", 0, 0, 0, 0, TPB // 2),
                  ("t", 0, 0, 0, 0, 1),
                  ("LARTB", TPB, 1, 0, 0, PAIRS // 2),
                  ("LARTBC", 2 * TPB, PAIRS + 1, PAIRS, 0, PAIRS),
                  ("TBC", 0, 3 * PAIRS + 1, 3 * PAIRS, 2 * TPB, PAIRS // 2 - 1),
                  ("tBC", 0, 4 * PAIRS - 1, 4 * PAIRS - 2, 3 * TPB - 2, 1),
                  ("C", 0, 0, 0, 3 * TPB, TPB // 2)]

        def phases(eng, body):
            body("L", 0, -2, 0, 0, 0)
            body("LA", 1, -1, 0, 0, 0)
            for stages, r0, t0, b0, c0, n in PHASES:
                if stages == "t":
                    body("first", 0, 0, 0, 0, 0)
                elif n == 1:
                    body("TBC", 0, r0, t0, b0, c0)
                    body("BC", 1, r0 + 1, t0 + 1, b0 + 1, c0 + 1)
                else:
                    with eng.Fori(0, n) as it:
                        for u in range(2):
                            body(stages, u, it * 2 + (r0 + u), it * 2 + (t0 + u), it * 2 + (b0 + u), it * 2 + (c0 + u))

        def wait_split(eng, j, b, before):
            if j in LO_POOL:
                eng.wait_ge(p_split, (b + (1 - before)) * len(LO_POOL) + (LO_POOL.index(j) + 1))
            else:
                eng.wait_ge(b_split, (b + (1 - before)) * len(LO_DVE) + (LO_DVE.index(j) + 1))

        block = ctx.enter_context(nc.Block())

        @block.sync
        def _(sp):
            sp.dma_start(ct[:], cT.rearrange("(k p) b -> p k b", p=P)).then_inc(s_modw, 16)
            sp.dma_start(wm[:], wmod.rearrange("(k p) n -> p k n", p=P)).then_inc(s_modw, 16)
            for u in range(2):
                sp.dma_start(xA[:, u, :], x_v[:, u, :]).then_inc(s_xA[u], 16)
                sp.dma_start(xC[:, u, :], x_v[:, u, :]).then_inc(s_xC[u], 16)
            sp.dma_start(wqkv[:], qkv_wT.rearrange("(k p) n -> p k n", p=P)).then_inc(s_w, 16)
            sp.dma_start(wo[:], out_wT.rearrange("(k p) n -> p k n", p=P)).then_inc(s_w, 16)
            sp.dma_start(qkvb[:], qkv_b.rearrange("(a n) -> a n", a=1).to_broadcast([P, 3 * D])).then_inc(s_w, 16)
            sp.dma_start(ob[:], out_b.rearrange("(a n) -> a n", a=1).to_broadcast([P, D])).then_inc(s_w, 16)
            sp.dma_start(idn[:], ident).then_inc(s_w, 16)
            sp.dma_start(idn16[:], ident16).then_inc(s_w, 16)
            sp.dma_start(rp[:], rope).then_inc(s_w, 16)
            sp.dma_start(gw[:], gate_w.rearrange("(k p) e -> p k e", p=P)).then_inc(s_w, 16)
            sp.wait_ge(mod_ready, 6)
            sp.dma_start(mod_dram, mod[:]).then_inc(s_modb, 16)
            sp.wait_ge(s_modb, 16)
            m6 = mod_dram.rearrange("(a b) (s d) -> a b s d", a=1, s=6)
            sp.dma_start(gaB, m6[:, :, GA, :].to_broadcast([P, B, D])).then_inc(s_modb, 16)
            sp.dma_start(modB[:], m6[:, :, SB:CB + 1, :].to_broadcast([P, B, 2, D])).then_inc(s_modb, 16)

            def body(stages, u, r, t, b, c):
                if "L" in stages:
                    sp.wait_ge(a_xn, r + 3)
                    sp.dma_start(xA[:, u:u + 1, :], x_v[:, bass.ds((r + 4) % NT, 1), :]).then_inc(s_xA[u], 16)
                if "C" in stages:
                    sp.wait_ge(c_xg, c + 1)
                    sp.dma_start(xC[:, u:u + 1, :], x_v[:, bass.ds((c + 2) % NT, 1), :]).then_inc(s_xC[u], 16)
                    sp.wait_ge(c_x1, c + 1 + CREDIT)
                    sp.dma_start(x1_dram.rearrange("(g p) d -> p g d", p=P)[:, bass.ds(c, 1), :],
                                 x1[:, u:u + 1, :]).then_inc(c_st[u], 16)
                    sp.wait_ge(c_h2, c * 2 + 2)
                    sp.dma_start(h2_dram.rearrange("(g p) d -> p g d", p=P)[:, bass.ds(c, 1), :],
                                 h2[:, u:u + 1, :]).then_inc(c_st[u], 16)
            phases(sp, body)
            for u in range(2):
                sp.wait_ge(c_st[u], 32 * NT // 2 + 32)
                sp.wait_ge(s_xA[u], 16 * (NT // 2 + 2))
                sp.wait_ge(s_xC[u], 16 * (NT // 2 + 1))

        @block.scalar
        def _(act):
            act.wait_ge(s_modw, 32)
            nc.scalar.activation(ce[:], ct[:], ACT.Exp, scale=-1.0).then_inc(silu_exp, 1)

            def turned(u, t, i):
                act.wait_ge(t_ps, t * 4 + (i + 1))
                half = slice(i // 2 * 512, (i // 2 + 1) * 512)
                nc.scalar.copy((QT, KT)[i % 2][:, u, half], psM[i % 2][:]).then_inc((t_q, t_k)[i % 2], 1)

            def body(stages, u, r, t, b, c):
                if stages == "first":
                    for i in range(4):
                        turned(0, 0, i)
                    return
                for j in range(STEPS):
                    if "B" in stages:
                        act.wait_ge(b_scores, b * STEPS + (j + 1))
                        wait_split(act, (j - 4) % STEPS, b, int(j < 4))
                        exp = nc.scalar.activation(EX[:, j % 4, :], psS[j % 2][:], ACT.Exp, scale=SCALE)
                        if j % 2 == 0:
                            act.wait_ge(b_pv, b * STEPS + (j + 1))
                            exp = nc.scalar.activation(PH[:, j % 4, :], psS[j % 2][:], ACT.Exp, scale=SCALE)
                        exp.then_inc(b_exp, 1)
                    if j == 0 and "C" in stages:
                        act.wait_ge(c_at_ps, c + CREDIT)
                        act.wait_ge(b_o, (c // TPB + 1) * (2 * PAIRS) + 2)
                        nc.scalar.copy(aS[:], AT[:, bass.ds((c // TPB) % 2, 1), bass.ds(c % TPB, 1), :]
                                       .rearrange("p a t d -> p (a t d)")).then_inc(c_copy, 1)
                    if j == 2 and "A" in stages:
                        act.wait_ge(a_hT_ps, r + 2)
                        bat = bass.ds((r + 1) // TPB % B, 1)
                        for k in range(KD):
                            ins = nc.scalar.activation(hTA[:, k, :], psM[0][:, k * P:(k + 1) * P], ACT.Identity,
                                                       bias=modT[:, 0, k, bat], scale=modT[:, 1, k, bat])
                        ins.then_inc(a_hT, 1)
                    if j == 3 and "C" in stages:
                        act.wait_ge(c_at_ps, c + 1 + CREDIT)
                        nc.scalar.copy(aT[:].rearrange("p k t -> p (k t)"), psM[1][:, 0:D]).then_inc(c_at, 1)
                    if j == 4 and "R" in stages:
                        act.wait_ge(a_rope, r + 1)
                        nc.scalar.activation(rs_[:], rc[:], ACT.Square).then_inc(a_sq, 1)
                    if j == 12 and "C" in stages:
                        act.wait_ge(c_h2T_ps, c + 1)
                        nc.scalar.copy(h2T[:].rearrange("p k t -> p (k t)"), psM[1][:, 0:D]).then_inc(c_h2T, 1)
                    if "T" in stages and j - 1 in T_AT:
                        turned((u + 1) % 2, t, T_AT.index(j - 1))
                if "C" in stages:
                    act.wait_ge(c_lg_ps, c + 1)
                    nc.scalar.copy(LG[:, bass.ds(c, 1), :].rearrange("p a e -> p (a e)"), psM[0][:, 0:E]).then_inc(c_lg, 1)
                if "T" in stages:
                    turned((u + 1) % 2, t, 3)
            phases(act, body)

        @block.gpsimd
        def _(pool):
            nc.gpsimd.memset(mhalf[:], -0.5).then_inc(setup, 1)
            nc.gpsimd.memset(eps[:], LN_EPS).then_inc(setup, 1)
            nc.gpsimd.memset(V[:, :, :, :, 2 * HD:HV], 1.0).then_inc(setup, 1)
            pool.wait_ge(setup, 3)
            pool.wait_ge(s_w, 16 * 8)
            pool.wait_ge(s_modb, 48)

            def low(b, i):
                j = LO_POOL[i]
                pool.wait_ge(b_exp, b * STEPS + (j + 1))
                pool.wait_ge(b_pv, b * STEPS + (j + 1))
                nc.gpsimd.tensor_tensor(PL[:, j % 4, :], EX[:, j % 4, :], PH[:, j % 4, :], ALU.subtract).then_inc(p_split, 1)

            def body(stages, u, r, t, b, c):
                if "C" in stages:
                    cbat = c // TPB
                    pool.wait_ge(s_xC[u], 16 * (c // 2) + 16)
                    pool.wait_ge(c_x1, c + CREDIT)
                    nc.gpsimd.tensor_tensor(xg[:], xC[:, u, :],
                                            gob[:, bass.ds(cbat, 1), :].rearrange("p a d -> p (a d)"), ALU.add).then_inc(c_xg, 1)
                if "B" in stages:
                    low(b, 0)
                if "R" in stages:
                    tile = r % TPB
                    cos = rp[:, bass.ds(tile, 1), 0, :].to_broadcast([P, 2 * H, HD])
                    sine = rp[:, bass.ds(tile, 1), 1, :].to_broadcast([P, 2 * H, HD])
                    pool.wait_ge(a_qk, r + 1 + CREDIT)
                    pool.wait_ge(a_split, r * 2 + 2)
                    nc.gpsimd.tensor_tensor(rc[:], qk[:], cos, ALU.mult)
                    nc.gpsimd.tensor_tensor(rs_[:, :, 0::2], qk[:, :, 1::2], sine[:, :, 0::2], ALU.mult)
                    nc.gpsimd.tensor_tensor(rs_[:, :, 1::2], qk[:, :, 0::2], sine[:, :, 1::2], ALU.mult).then_inc(a_turn, 1)
                    pool.wait_ge(a_turn, r + 1)
                    nc.gpsimd.tensor_tensor(rc[:], rc[:], rs_[:], ALU.add).then_inc(a_rope, 1)
                if "L" in stages:
                    pool.wait_ge(a_step, (r + 2) * 4 + 4)
                    nc.gpsimd.tensor_tensor(veA[:], mvA[:, 1:2], eps[:], ALU.add).then_inc(a_pool, 1)
                    pool.wait_ge(a_pool, r + 3)
                    nc.gpsimd.tensor_tensor(rsA[:], veA[:], mhalf[:, 0:1], ALU.pow).then_inc(a_rstd, 1)
                if "B" in stages:
                    low(b, 1)
                if "C" in stages:
                    pool.wait_ge(c_step, c * 4 + 4)
                    nc.gpsimd.tensor_tensor(veC[:], mvC[:, 1:2], eps[:], ALU.add).then_inc(c_pool, 1)
                    pool.wait_ge(c_pool, c + 1)
                    nc.gpsimd.tensor_tensor(rsC[:], veC[:], mhalf[:, 0:1], ALU.pow).then_inc(c_rstd, 1)
                if "R" in stages:
                    pool.wait_ge(a_ss, r + 1)
                    nc.gpsimd.tensor_tensor(inv[:], ss[:], mhalf[:], ALU.pow).then_inc(a_inv, 1)
                if "C" in stages:
                    pool.wait_ge(c_xn, c + 1)
                    pool.wait_ge(c_st[u], 32 * (c // 2) + 32)
                    nc.gpsimd.tensor_tensor(h2[:, u, :], xnC[:], modB[:, bass.ds(cbat, 1), 1, :].rearrange("p a d -> p (a d)"),
                                            ALU.mult).then_inc(c_h2, 1)
                    pool.wait_ge(c_h2, c * 2 + 1)
                    nc.gpsimd.tensor_tensor(h2[:, u, :], h2[:, u, :], modB[:, bass.ds(cbat, 1), 0, :].rearrange("p a d -> p (a d)"),
                                            ALU.add).then_inc(c_h2, 1)
                if "B" in stages:
                    for i in range(2, len(LO_POOL)):
                        low(b, i)
            phases(pool, body)

        @block.vector
        def _(dve):
            dve.wait_ge(silu_exp, 1)
            nc.vector.tensor_scalar(ce[:], ce[:], 1.0, None, ALU.add).then_inc(silu_done, 1)
            dve.wait_ge(silu_done, 1)
            nc.vector.reciprocal(ce[:], ce[:]).then_inc(silu_done, 1)
            dve.wait_ge(silu_done, 2)
            nc.vector.tensor_tensor(cs[:], ct[:], ce[:], ALU.mult).then_inc(silu_done, 1)
            dve.wait_ge(mod_ps, 1)
            for n in range(3):
                ins = nc.vector.tensor_copy(mod[:, n * 512:(n + 1) * 512], (psM[0], psM[1], psS[1])[n][0:B, 0:512])
            nc.vector.tensor_copy(modT[:, 0, :, :], psS[0][:, 0:KD * B].rearrange("p (k b) -> p k b", k=KD))
            nc.vector.tensor_scalar(modT[:, 1, :, :], psS[0][:, KD * B:2 * KD * B].rearrange("p (k b) -> p k b", k=KD),
                                    1.0, None, ALU.add).then_inc(mod_ready, 1)
            dve.wait_ge(mod_ready, 1)
            m6 = mod[:].rearrange("b (s d) -> b s d", s=6)
            nc.vector.tensor_scalar(sgn[:], m6[:, GA::3, :], 0.0, 2.0, ALU.is_ge, ALU.mult).then_inc(mod_ready, 1)
            nc.vector.tensor_scalar(m6[:, CA::3, :], m6[:, CA::3, :], 1.0, None, ALU.add)
            dve.wait_ge(mod_ready, 2)
            nc.vector.tensor_scalar(sgn[:], sgn[:], -1.0, None, ALU.add).then_inc(mod_ready, 1)
            dve.wait_ge(mod_ready, 3)
            nc.vector.tensor_tensor(m6[:, GA::3, :], m6[:, GA::3, :], sgn[:], ALU.mult).then_inc(mod_ready, 1)
            dve.wait_ge(mod_ready, 4)
            nc.vector.tensor_scalar(m6[:, GA::3, :], m6[:, GA::3, :], 0.25, None, ALU.max).then_inc(mod_ready, 1)
            dve.wait_ge(mod_ready, 5)
            nc.vector.tensor_tensor(m6[:, GA::3, :], m6[:, GA::3, :], sgn[:], ALU.mult).then_inc(mod_ready, 1)
            dve.wait_ge(s_modb, 48)
            dve.wait_ge(s_w, 16 * 8)
            dve.wait_ge(setup, 3)
            for b in range(B):
                for k in range(KD):
                    nc.vector.tensor_tensor(wog[:, b, k, :], wo[:, k, :], gaB[:, b, :], ALU.mult)
                ins = nc.vector.tensor_tensor(gob[:, b, :], ob[:], gaB[:, b, :], ALU.mult)
            ins.then_inc(setup, 2)
            dve.wait_ge(setup, 5)

            def variance(step, i, per, st, mv, t):
                dve.wait_ge(step, i * per + 1)
                nc.vector.tensor_tensor(t[:, 0:2], st[:, 1:3], st[:, 4:6], ALU.add)
                nc.vector.tensor_tensor(t[:, 2:3], st[:, 1:2], st[:, 4:5], ALU.subtract).then_inc(step, 1)
                dve.wait_ge(step, i * per + 2)
                nc.vector.tensor_scalar(mv[:, 0:1], t[:, 0:1], 0.5, None, ALU.mult)
                nc.vector.scalar_tensor_tensor(out=t[:, 2:3], in0=t[:, 2:3], scalar=0.25, in1=t[:, 2:3],
                                               op0=ALU.mult, op1=ALU.mult).then_inc(step, 1)
                dve.wait_ge(step, i * per + 3)
                nc.vector.scalar_tensor_tensor(out=mv[:, 1:2], in0=t[:, 1:2], scalar=1.0 / D, in1=t[:, 2:3],
                                               op0=ALU.mult, op1=ALU.add).then_inc(step, 1)

            def body(stages, u, r, t, b, c):
                if stages == "first":
                    return
                for j in range(STEPS):
                    if j == 1 and "R" in stages:
                        vt = V[:, bass.ds((r // TPB) % 2, 1), bass.ds(r % TPB, 1), :, :].rearrange("p a t h d -> p (a t h) d")
                        dve.wait_ge(a_vps, r + 1 + CREDIT)
                        nc.vector.tensor_copy(vt[:, :, 0:HD], vA[:]).then_inc(a_v, 1)
                        dve.wait_ge(a_v, r * 2 + 1)
                        nc.vector.tensor_tensor(vt[:, :, HD:2 * HD], vA[:], vt[:, :, 0:HD], ALU.subtract).then_inc(a_v, 1)
                    if j == 2 and "L" in stages:
                        dve.wait_ge(s_xA[u], 16 * ((r + 2) // 2) + 16)
                        nc.vector.bn_stats(bnA[:], xA[:, u, :]).then_inc(a_step, 1)
                        variance(a_step, r + 2, 4, bnA, mvA, dfA)
                    if j == 4 and "L" in stages:
                        dve.wait_ge(a_rstd, r + 3)
                        if "A" in stages:
                            dve.wait_ge(a_hT_ps, r + 2)
                        nc.vector.tensor_scalar(xnA[:], xA[:, u, :], mvA[:, 0:1], rsA[:, 0:1],
                                                ALU.subtract, ALU.mult).then_inc(a_xn, 1)
                    if j == 4 and "A" in stages:
                        dve.wait_ge(a_v_ps, r + 2)
                        nc.vector.tensor_tensor(vA[:].rearrange("p h d -> p (h d)"), psM[0][:, 0:D], qkvb[:, 2 * D:3 * D],
                                                ALU.add).then_inc(a_vps, 1)
                    if j == 5 and "C" in stages:
                        dve.wait_ge(c_proj, c + 1)
                        dve.wait_ge(c_xg, c + 1)
                        dve.wait_ge(c_st[u], 32 * (c // 2) + 32)
                        nc.vector.tensor_tensor(x1[:, u, :], psM[1][:, 0:D], xg[:], ALU.add).then_inc(c_x1, 1)
                        dve.wait_ge(c_x1, c + 1 + CREDIT)
                        nc.vector.bn_stats(bnC[:], x1[:, u, :]).then_inc(c_step, 1)
                        variance(c_step, c, 4, bnC, mvC, dfC)
                    if j == 6 and "R" in stages:
                        dve.wait_ge(a_sq, r + 1)
                        nc.vector.tensor_reduce(ss[:], rs_[:], AX.X, ALU.add).then_inc(a_ss, 1)
                    if j == 7 and "A" in stages:
                        dve.wait_ge(a_qk_ps, r + 2)
                        if "R" in stages:
                            dve.wait_ge(a_rope, r + 1)
                        nc.vector.tensor_tensor(qk[:].rearrange("p h d -> p (h d)"), psM[1][:], qkvb[:, 0:2 * D],
                                                ALU.add).then_inc(a_qk, 1)
                    if j == 8 and "C" in stages:
                        dve.wait_ge(c_rstd, c + 1)
                        nc.vector.tensor_scalar(xnC[:], x1[:, u, :], mvC[:, 0:1], rsC[:, 0:1],
                                                ALU.subtract, ALU.mult).then_inc(c_xn, 1)
                    if j == 11 and "R" in stages:
                        dve.wait_ge(a_inv, r + 1)
                        nc.vector.scalar_tensor_tensor(out=rc[:], in0=inv[:].rearrange("p (h a) -> p h a", a=1).to_broadcast([P, 2 * H, HD]),
                                                       scalar=NORM_CAP, in1=rc[:], op0=ALU.min, op1=ALU.mult).then_inc(a_norm, 1)
                        dve.wait_ge(a_norm, r + 1)
                        for part in range(2):
                            for q in range(2):
                                dst = QK[:, bass.ds((r // TPB) % 2, 1), bass.ds(r % TPB, 1), q, :, :, :].rearrange(
                                    "p a t h f d -> p (a t h) f d")
                                full = rc[:, q * H:(q + 1) * H, :].rearrange("p h (a d) -> p h a d", a=1).to_broadcast([P, H, 2, HD])
                                hi = dst[:, :, 0:1, :].to_broadcast([P, H, 2, HD])
                                two = (dst[:, :, part::2, :], dst[:, :, 2 * part:2 * part + 2, :])[q]
                                if part == 0:
                                    ins = nc.vector.tensor_copy(two, full)
                                else:
                                    ins = nc.vector.tensor_tensor(two, full, hi, ALU.subtract)
                            ins.then_inc(a_split, 1)
                            if part == 0:
                                dve.wait_ge(a_split, r * 2 + 1 + 2)
                    if "B" in stages and j in LO_DVE:
                        dve.wait_ge(b_exp, b * STEPS + (j + 1))
                        dve.wait_ge(b_pv, b * STEPS + (j + 1))
                        if j % 2:
                            nc.vector.tensor_copy(PH[:, j % 4, :], EX[:, j % 4, :]).then_inc(b_hi, 1)
                            dve.wait_ge(b_hi, b * (STEPS // 2) + (j // 2 + 1))
                        nc.vector.tensor_tensor(PL[:, j % 4, :], EX[:, j % 4, :], PH[:, j % 4, :], ALU.subtract).then_inc(b_split, 1)
                if "B" in stages:
                    for hh in range(2):
                        dve.wait_ge(b_pv, b * STEPS + (STEPS - 1 + hh + 4))
                        nc.vector.reciprocal(orec[:, hh, :], psO[hh][:, :, 2 * HD:HV].rearrange("p t a -> p (t a)"))
                        nc.vector.tensor_copy(osum[:, hh, :, :], psO[hh][:, :, HD:2 * HD]).then_inc(b_ostep, 1)
                        dve.wait_ge(b_ostep, b * 4 + (2 * hh + 1))
                        nc.vector.tensor_tensor(osum[:, hh, :, :], psO[hh][:, :, 0:HD], osum[:, hh, :, :], ALU.add).then_inc(b_ostep, 1)
                    dve.wait_ge(b_ostep, b * 4 + 4)
                    for hh in range(2):
                        rec = orec[:, hh, :].rearrange("p (t a) -> p t a", a=1).to_broadcast([P, TPB, HD])
                        dst = AT[:, bass.ds((b // PAIRS) % 2, 1), :, bass.ds((b % PAIRS) * (2 * HD) + hh * HD, HD)].rearrange(
                            "p a t d -> p (a t) d")
                        nc.vector.tensor_tensor(dst, osum[:, hh, :, :], rec, ALU.mult).then_inc(b_o, 1)
            phases(dve, body)

        @block.tensor
        def _(pe):
            pe.sem_inc(b_pv, 4)
            pe.sem_inc(b_split, len(LO_DVE))
            pe.sem_inc(p_split, len(LO_POOL))
            pe.sem_inc(a_split, 2)
            for free in (a_hT, a_vps, a_qk, c_at, c_x1, c_at_ps, c_h2T, c_lg):
                pe.sem_inc(free, CREDIT)
            pe.sem_inc(b_o, 2)
            for u in range(2):
                pe.sem_inc(c_st[u], 32)
            pe.wait_ge(silu_done, 3)
            for n in range(3):
                for k in range(KD):
                    mm = nc.tensor.matmul((psM[0], psM[1], psS[1])[n][0:B, 0:512], cs[:, k, :], wm[:, k, n * 512:(n + 1) * 512],
                                          start=(k == 0), stop=(k == KD - 1))
            for n in range(2 * KD):
                for k in range(KD):
                    mm = nc.tensor.matmul(psS[0][:, n * B:(n + 1) * B], wm[:, k, n * P:(n + 1) * P], cs[:, k, :],
                                          start=(k == 0), stop=(k == KD - 1))
            mm.then_inc(mod_ps, 1)
            pe.wait_ge(mod_ready, 1)
            pe.wait_ge(s_w, 16 * 8)
            pe.wait_ge(setup, 5)

            def free_bank(me, stages, r, t, c):
                for order in (["hT", "v", "q0", "q1", "lg"], ["at", "proj", "qk", "k0", "h2T", "k1"]):
                    if me not in order:
                        continue
                    i = order.index(me)
                    for back in range(1, len(order) + 1):
                        prev = order[(i - back) % len(order)]
                        new = 0 if back > i else 1
                        if prev in ("hT", "v", "qk") and "A" in stages:
                            pe.wait_ge({"hT": a_hT, "v": a_vps, "qk": a_qk}[prev], r + (1 + new + CREDIT))
                            return
                        if prev in ("at", "proj", "h2T", "lg") and "C" in stages:
                            pe.wait_ge({"at": c_at, "proj": c_x1, "h2T": c_h2T, "lg": c_lg}[prev], c + (new + CREDIT))
                            return
                        if prev[0] in "qk" and prev != "qk" and "T" in stages:
                            pe.wait_ge({"q": t_q, "k": t_k}[prev[0]], (t + (new - 1)) * 2 + (int(prev[1]) + 1))
                            return

            def scores(u, j):
                kt, hh = j // 2, j % 2
                rows = slice(64 * hh, 64 * hh + 64)
                for q in range(QCH):
                    mm = nc.tensor.matmul(psS[j % 2][:, q * 512:(q + 1) * 512], KT[rows, u, kt * P:(kt + 1) * P],
                                          QT[rows, u, q * 512:(q + 1) * 512], start=True, stop=True)
                mm.then_inc(b_scores, 1)

            def turn(stages, r, t, c, i):
                q, half = i % 2, i // 2
                if stages:
                    free_bank("qk"[q] + str(half), stages, r, t, c)
                bat = t // PAIRS
                pe.wait_ge(a_split, (bat * TPB + 4 * half + 4) * 2 + 2)
                for n in range(4):
                    lhsT = QK[:, bass.ds(bat % 2, 1), 4 * half + n, q, bass.ds((t % PAIRS) * 2, 2), :, :].rearrange(
                        "p a h f d -> p (a h f d)")
                    mm = nc.tensor.matmul(psM[q][:, n * P:(n + 1) * P], lhsT, idn16[:], start=True, stop=True)
                mm.then_inc(t_ps, 1)

            def values(b, j):
                kt, hh = j // 2, j % 2
                if kt == 0:
                    pe.wait_ge(b_o, b * 2 + (hh + 1))
                wait_split(pe, j, b, 0)
                rhs = V[:, bass.ds((b // PAIRS) % 2, 1), kt, bass.ds((b % PAIRS) * 2 + hh, 1), :].rearrange(
                    "p a h d -> p (a h d)")
                for q in range(TPB):
                    for part in (PH, PL):
                        mm = nc.tensor.matmul(psO[hh][:, q, 0:HV], part[:, j % 4, q * P:(q + 1) * P], rhs,
                                              start=(kt == 0 and q == 0 and part is PH), stop=(kt == TPB - 1),
                                              skip_group_check=True)
                mm.then_inc(b_pv, 1)

            def body(stages, u, r, t, b, c):
                if stages == "first":
                    pe.wait_ge(a_vps, TPB + 1 + CREDIT)
                    pe.wait_ge(a_qk, TPB + 1 + CREDIT)
                    for i in range(4):
                        if i >= 2:
                            pe.wait_ge((t_q, t_k)[i % 2], 1)
                        turn("", r, 0, c, i)
                    pe.wait_ge(t_q, 2)
                    pe.wait_ge(t_k, 1)
                    scores(0, 0)
                    scores(0, 1)
                    return
                for j in range(STEPS):
                    if j == 1 and "A" in stages:
                        pe.wait_ge(a_xn, r + 2)
                        free_bank("hT", stages, r, t, c)
                        for k in range(KD):
                            mm = nc.tensor.transpose(psM[0][:, k * P:(k + 1) * P], xnA[:, k * P:(k + 1) * P], idn[:])
                        mm.then_inc(a_hT_ps, 1)
                    if j == 2 and "B" in stages:
                        pe.wait_ge(t_k, b * 2 + 2)
                    if j == 2 and "C" in stages:
                        pe.wait_ge(c_copy, c + 1)
                        free_bank("at", stages, r, t, c)
                        for k in range(KD):
                            mm = nc.tensor.transpose(psM[1][:, k * P:(k + 1) * P], aS[:, k * P:(k + 1) * P], idn[:])
                        mm.then_inc(c_at_ps, 1)
                    if j == 3 and "A" in stages:
                        pe.wait_ge(a_hT, r + 2 + CREDIT)
                        for k in range(KD):
                            mm = nc.tensor.matmul(psM[0][:, 0:D], hTA[:, k, :], wqkv[:, k, 2 * D:3 * D],
                                                  start=(k == 0), stop=(k == KD - 1))
                        mm.then_inc(a_v_ps, 1)
                    if j == 4 and "C" in stages:
                        pe.wait_ge(c_at, c + 1 + CREDIT)
                        for k in range(KD):
                            mm = nc.tensor.matmul(psM[1][:, 0:D], aT[:, k, :],
                                                  wog[:, bass.ds(c // TPB, 1), k, :].rearrange("p a d -> p (a d)"),
                                                  start=(k == 0), stop=(k == KD - 1))
                        mm.then_inc(c_proj, 1)
                    if j == 6 and "A" in stages:
                        free_bank("qk", stages, r, t, c)
                        for k in range(KD):
                            mm = nc.tensor.matmul(psM[1][:, :], hTA[:, k, :], wqkv[:, k, 0:2 * D],
                                                  start=(k == 0), stop=(k == KD - 1))
                        mm.then_inc(a_qk_ps, 1)
                    if j == 11 and "C" in stages:
                        pe.wait_ge(c_h2, c * 2 + 2)
                        free_bank("h2T", stages, r, t, c)
                        for k in range(KD):
                            mm = nc.tensor.transpose(psM[1][:, k * P:(k + 1) * P], h2[:, u, k * P:(k + 1) * P], idn[:])
                        mm.then_inc(c_h2T_ps, 1)
                    if j == 14 and "C" in stages:
                        free_bank("lg", stages, r, t, c)
                        pe.wait_ge(c_h2T, c + 1 + CREDIT)
                        for k in range(KD):
                            mm = nc.tensor.matmul(psM[0][:, 0:E], h2T[:, k, :], gw[:, k, :], start=(k == 0), stop=(k == KD - 1))
                        mm.then_inc(c_lg_ps, 1)
                    if "T" in stages and j in T_AT:
                        turn(stages, r, t, c, T_AT.index(j))
                    if "B" not in stages:
                        continue
                    pe.wait_ge(b_exp, b * STEPS + (j + 1))
                    if j + 2 < STEPS:
                        scores(u, j + 2)
                    elif "T" in stages:
                        if j + 2 == STEPS:
                            pe.wait_ge(t_q, t * 2 + 2)
                            pe.wait_ge(t_k, t * 2 + 1)
                        scores((u + 1) % 2, j + 2 - STEPS)
                    if j > 0:
                        values(b, j - 1)
                    if j == STEPS - 1:
                        values(b, j)
            phases(pe, body)


def experts(nc, w1, w2, w3, ident, below, counts, mod_dram, x1_dram, h2_dram, xs_dram, ys_dram, LG, out):
    with ExitStack() as ctx:
        def sb(name, shape, dt=F32):
            return ctx.enter_context(nc.sbuf_tensor(name, shape, dt))

        def sem(name):
            return ctx.enter_context(nc.semaphore(name))

        NE = [P, NT, E]
        H2 = sb("H2", [P, NT, D])
        X1 = H2
        gbB = sb("gbB", [P, B, D])
        zero = sb("zero", [P, D])
        eye = sb("eye", [P, P])
        bel = sb("bel", [P, 2, P])
        cnt = sb("cnt", [P, 64])
        key = sb("key", NE)
        hot = sb("hot", [P, 2, NT, E])
        both = sb("both", NE)
        lg2 = sb("lg2", NE)
        tmp = sb("tmp", NE)
        keep = sb("keep", [P, 2, NT, E])
        dif = sb("dif", [P, 2, NT, E])
        scan = sb("scan", [P, 2, NT, E])
        cum = sb("cum", NE)
        val = sb("val", [P, 2, NT])
        kmax = sb("kmax", [P, NT])
        mult = sb("mult", [P, 2, NT])
        posf = sb("posf", [P, 2, NT])
        pos = sb("pos", [P, 2, NT], mybir.dt.uint32)
        ge = sb("ge", [P, E, 16])
        nblk = sb("nblk", [P, E])
        first = sb("first", [P, 4, E])
        blk = sb("blk", [P, BLOCKS + 1, E])
        blkf = sb("blkf", [P, BLOCKS + 1])
        blki = sb("blki", [P, BLOCKS + 1], mybir.dt.int32)
        wf = sb("wf", [P, 2, 3, KD * F])
        wh = sb("wh", [P, 2, 3, KD * F], F16)
        wl = sb("wl", [P, 2, 3, KD * F], F16)
        xr = sb("xr", [P, 2, RC, D])
        xh = sb("xh", [P, 2, KD, ROWS], F16)
        xl = sb("xl", [P, 2, KD, ROWS], F16)
        sg = sb("sg", [P, 2, GU, ROWS])
        hf = sb("hf", [P, 2, GU, ROWS])
        hh = sb("hh", [P, 2, FC, ROWS], F16)
        hl = sb("hl", [P, 2, FC, ROWS], F16)
        yr = sb("yr", [P, 2, RC, D])
        ya = sb("ya", [P, 2, 2, D])
        yo = sb("yo", [P, 2, D])

        psR = ctx.enter_context(nc.psum_tensor("psR", [P, 2, NT, E], F32))
        psX = ctx.enter_context(nc.psum_tensor("psX", [P, KD, ROWS], F32))
        psG = [ctx.enter_context(nc.psum_tensor(f"psG{i}", [P, GU, 2, ROWS], F32)) for i in range(2)]
        psY = [ctx.enter_context(nc.psum_tensor(f"psY{i}", [P, RC, D], F32)) for i in range(2)]

        s_in = sem("s_in")
        s_h2 = sem("s_h2")
        s_x1 = sem("s_x1")
        s_zero = sem("s_zero")
        z_ready = sem("z_ready")
        s_blk = sem("s_blk")
        r_step = sem("r_step")
        r_dif = sem("r_dif")
        r_exp = sem("r_exp")
        r_hot = sem("r_hot")
        r_cum = sem("r_cum")
        r_pos = sem("r_pos")
        r_sent = sem("r_sent")
        s_w = [sem(f"s_w{u}") for u in range(2)]
        s_xr = [sem(f"s_xr{u}") for u in range(2)]
        m_xT_ps = sem("m_xT_ps")
        m_xh = sem("m_xh")
        m_xT = sem("m_xT")
        m_gu = sem("m_gu")
        m_sg = sem("m_sg")
        m_hf = sem("m_hf")
        m_hh = sem("m_hh")
        m_hl = sem("m_hl")
        w_hi = sem("w_hi")
        w_lo = sem("w_lo")
        m_y_ps = sem("m_y_ps")
        m_y = sem("m_y")
        s_ys = [sem(f"s_ys{u}") for u in range(2)]
        f_y = [sem(f"f_y{u}") for u in range(2)]
        f_step = sem("f_step")
        s_out = [sem(f"s_out{u}") for u in range(2)]

        rows = lambda d: d.rearrange("(g p) d -> p g d", p=P)
        w_v = (w1.rearrange("e (k p) f -> p (e k) f", p=P), w3.rearrange("e (k p) f -> p (e k) f", p=P),
               w2.rearrange("e (f p) d -> p (e f) d", p=P))
        chunks = (KD, KD, FC)
        W2 = 2
        ys_v = ys_dram.rearrange("(g p) d -> p g d", p=P)
        xs_v = xs_dram.rearrange("(g p) d -> p g d", p=P)

        def blocks(eng, body):
            with eng.Fori(0, (BLOCKS - 1) // 2) as it:
                for u in range(2):
                    body(u, it * 2 + u, True)
            for i in range((BLOCKS - 1) // 2 * 2, BLOCKS):
                body(i % 2, i, i + 1 < BLOCKS)

        block = ctx.enter_context(nc.Block())

        @block.sync
        def _(sp):
            sp.dma_start(bel[:], below).then_inc(s_in, 16)
            sp.dma_start(cnt[:], counts).then_inc(s_in, 16)
            sp.dma_start(eye[:], ident).then_inc(s_in, 16)
            m6 = mod_dram.rearrange("(a b) (s d) -> a b s d", a=1, s=6)
            sp.dma_start(gbB[:], m6[:, :, GB, :].to_broadcast([P, B, D])).then_inc(s_in, 16)
            sp.dma_start(H2[:], rows(h2_dram)).then_inc(s_h2, 16)
            sp.wait_ge(z_ready, 1)
            sp.dma_start(xs_v, zero[:].rearrange("p (a d) -> p a d", a=1).to_broadcast([P, BLOCKS * RC, D])).then_inc(s_zero, 16)
            sp.wait_ge(s_blk, 1)

            def body(u, i, more):
                e = sp.value_load(blki[0:1, bass.ds(i, 1)], min_val=0, max_val=E - 1)
                sp.wait_ge(w_lo, i * 3 + 3)
                for n in range(3):
                    c = chunks[n]
                    sp.dma_start(wf[:, u, n, :].rearrange("p (c f) -> p c f", c=c), w_v[n][:, bass.ds(e * c, c), :]).then_inc(s_w[u], 16)
                sp.wait_ge(r_sent, 2 * NT * 16)
                sp.wait_ge(m_xT_ps, i + 1)
                sp.dma_start(xr[:, u, :, :], xs_v[:, bass.ds(i * RC, RC), :]).then_inc(s_xr[u], 16)
            blocks(sp, body)
            sp.dma_start(X1[:], rows(x1_dram)).then_inc(s_x1, 16)
            for t in range(NT):
                sp.wait_ge(f_step, 4 * t + 4)
                sp.dma_start(rows(out.rearrange("b s d -> (b s) d"))[:, t, :], yo[:, t % 2, :]).then_inc(s_out[t % 2], 16)
            for u in range(2):
                sp.wait_ge(s_out[u], 16 * NT // 2)

        @block.scalar
        def _(act):
            act.wait_ge(r_dif, 1)
            nc.scalar.activation(dif[:], dif[:], ACT.Exp).then_inc(r_exp, 1)

            def split_w(u, i, n):
                if n == 0:
                    act.wait_ge(s_w[u], 48 * (i // 2) + 48)
                    act.wait_ge(m_y_ps, i + 1)
                nc.scalar.activation(wh[:, u, n, :], wf[:, u, n, :], ACT.Copy, scale=WS).then_inc(w_hi, 1)

            def split_x(u, i):
                act.wait_ge(m_xT_ps, i + 1 + 2)
                nc.scalar.copy(xh[:, u, :, :], psX[:]).then_inc(m_xh, 1)

            for n in range(3):
                split_w(0, 0, n)
            split_x(0, 0)

            def body(u, i, more):
                for p in range(STEPS_E):
                    act.wait_ge(m_gu, i * STEPS_E + (p + 1))
                    act.wait_ge(m_hf, i * STEPS_E + (p + 1))
                    nc.scalar.activation(sg[:, p % 2, :, :], psG[p % 2][:, :, 0, :], ACT.Silu, scale=1.0 / WS).then_inc(m_sg, 1)
                    if more and p < 3:
                        split_w(1 - u, i + 1, p)
                if more:
                    split_x(1 - u, i + 1)
                act.wait_ge(m_y_ps, i + 3)
                act.wait_ge(s_ys[u], 16 * (i // 2) + 16)
                nc.scalar.activation(yr[:, u, :, :], psY[u][:], ACT.Copy, scale=1.0 / WS).then_inc(m_y, 1)
                act.wait_ge(m_y, i + 3)
                act.dma_start(ys_v[:, bass.ds(i * RC, RC), :], yr[:, u, :, :]).then_inc(s_ys[u], 16)
            blocks(act, body)
            act.wait_ge(s_ys[0], 16 * (BLOCKS // 2 + 2))
            act.wait_ge(s_ys[1], 16 * (BLOCKS // 2 + 1))

        @block.gpsimd
        def _(pool):
            pool.wait_ge(s_h2, 16)
            pool.wait_ge(s_zero, 16)
            pool.wait_ge(r_pos, 1)
            for t in range(NT):
                for n in range(2):
                    nc.gpsimd.indirect_dma_start(xs_dram, bass.IndirectOffsetOnAxis(ap=pos[:, n, t:t + 1], axis=0),
                                                 H2[:, t, :], None).then_inc(r_sent, 16)

            def body(u, i, more):
                for p in range(STEPS_E):
                    pool.wait_ge(m_hh, i * STEPS_E + (p + 1))
                    nc.gpsimd.tensor_tensor(hl[:, u, p * GU:(p + 1) * GU, :], hf[:, p % 2, :, :],
                                            hh[:, u, p * GU:(p + 1) * GU, :], ALU.subtract).then_inc(m_hl, 1)
            blocks(pool, body)
            pool.wait_ge(s_ys[0], 16 * (BLOCKS // 2 + 2))
            pool.wait_ge(s_ys[1], 16 * (BLOCKS // 2 + 1))
            for t in range(NT):
                if t >= 2:
                    pool.wait_ge(f_step, 4 * (t - 1) - 1)
                for n in range(2):
                    nc.gpsimd.indirect_dma_start(ya[:, t % 2, n, :], None, ys_dram,
                                                 bass.IndirectOffsetOnAxis(ap=pos[:, n, t:t + 1], axis=0)).then_inc(f_y[t % 2], 16)

        @block.vector
        def _(dve):
            steps = [0]

            def link(ins):
                steps[0] += 1
                ins.then_inc(r_step, 1)
                dve.wait_ge(r_step, steps[0])

            def over(a, n=NT):
                return a.rearrange("p (t a) -> p t a", a=1).to_broadcast([P, n, E])

            nc.vector.memset(zero[:], 0.0).then_inc(z_ready, 1)
            dve.wait_ge(s_in, 64)
            order = cnt[:, 0:E].rearrange("p (a e) -> p a e", a=1).to_broadcast(NE)
            for n in range(2):
                src = (LG, lg2)[n]
                link(nc.vector.tensor_reduce(val[:, n, :], src[:], AX.X, ALU.max))
                link(nc.vector.tensor_tensor(key[:], src[:], over(val[:, n, :]), ALU.is_equal))
                link(nc.vector.tensor_tensor(key[:], key[:], order, ALU.mult))
                link(nc.vector.tensor_reduce(kmax[:], key[:], AX.X, ALU.max))
                link(nc.vector.tensor_tensor(hot[:, n, :, :], key[:], over(kmax[:]), ALU.is_equal))
                link(nc.vector.scalar_tensor_tensor(out=tmp[:], in0=LG[:], scalar=-1.0, in1=LG[:], op0=ALU.mult, op1=ALU.max))
                link(nc.vector.tensor_tensor(tmp[:], tmp[:], over(val[:, n, :]), ALU.max))
                link(nc.vector.tensor_tensor(keep[:, n, :, :], over(val[:, n, :]), LG[:], ALU.subtract))
                link(nc.vector.scalar_tensor_tensor(out=keep[:, n, :, :], in0=tmp[:], scalar=2.0 * JITTER, in1=keep[:, n, :, :],
                                                    op0=ALU.mult, op1=ALU.is_ge))
                link(nc.vector.tensor_tensor(dif[:, n, :, :], src[:], over(val[:, n, :]), ALU.subtract))
                if n == 0:
                    link(nc.vector.tensor_scalar(tmp[:], hot[:, 0, :, :], -1.0, 1.0, ALU.mult, ALU.add))
                    link(nc.vector.tensor_tensor(tmp[:], tmp[:], LG[:], ALU.mult))
                    link(nc.vector.scalar_tensor_tensor(out=lg2[:], in0=hot[:, 0, :, :], scalar=LOWEST, in1=tmp[:],
                                                        op0=ALU.mult, op1=ALU.add))
            nc.vector.tensor_tensor(both[:], hot[:, 0, :, :], hot[:, 1, :, :], ALU.add).then_inc(r_hot, 1)
            nc.vector.tensor_copy(tmp[:], tmp[:]).then_inc(r_dif, 1)
            dve.wait_ge(r_cum, 1)
            nc.vector.tensor_copy(cum[:], psR[:, 0, :, :])
            link(nc.vector.tensor_copy(scan[:, 0, :, :], psR[:, 1, :, :]))
            link(nc.vector.tensor_copy(tmp[:], psR[:, 1, :, :]))
            src, shift = 0, 1
            while shift < NT:
                nc.vector.tensor_copy(scan[:, 1 - src, 0:shift, :], scan[:, src, 0:shift, :])
                link(nc.vector.tensor_tensor(scan[:, 1 - src, shift:NT, :], scan[:, src, shift:NT, :],
                                             scan[:, src, 0:NT - shift, :], ALU.add))
                src, shift = 1 - src, 2 * shift
            total = scan[:, src, NT - 1, :]
            link(nc.vector.tensor_tensor(tmp[:], scan[:, src, :, :], tmp[:], ALU.subtract))
            link(nc.vector.tensor_tensor(cum[:], cum[:], tmp[:], ALU.add))
            link(nc.vector.tensor_tensor(ge[:], total.rearrange("p (e a) -> p e a", a=1).to_broadcast([P, E, 16]),
                                         cnt[:, 8:24].rearrange("p (a j) -> p a j", a=1).to_broadcast([P, E, 16]), ALU.is_gt))
            link(nc.vector.tensor_reduce(nblk[:], ge[:], AX.X, ALU.add))
            link(nc.vector.tensor_copy(first[:, 0, :], nblk[:]))
            src, shift = 0, 1
            while shift < E:
                nc.vector.tensor_copy(first[:, 1 - src, 0:shift], first[:, src, 0:shift])
                link(nc.vector.tensor_tensor(first[:, 1 - src, shift:E], first[:, src, shift:E], first[:, src, 0:E - shift], ALU.add))
                src, shift = 1 - src, 2 * shift
            end = first[:, src, :]
            link(nc.vector.tensor_tensor(first[:, 2, :], end, nblk[:], ALU.subtract))
            link(nc.vector.tensor_scalar(first[:, 3, :], first[:, 2, :], float(ROWS), None, ALU.mult))
            link(nc.vector.tensor_tensor(blk[:], end.rearrange("p (a e) -> p a e", a=1).to_broadcast([P, BLOCKS + 1, E]),
                                         cnt[:, 24:64].rearrange("p (t a) -> p t a", a=1)[:, 0:BLOCKS + 1, :].to_broadcast([P, BLOCKS + 1, E]),
                                         ALU.is_le))
            link(nc.vector.tensor_reduce(blkf[:], blk[:], AX.X, ALU.add))
            nc.vector.tensor_scalar(blki[:], blkf[:], float(E - 1), None, ALU.min).then_inc(s_blk, 1)
            link(nc.vector.tensor_tensor(cum[:], cum[:], first[:, 3, :].rearrange("p (a e) -> p a e", a=1).to_broadcast(NE), ALU.add))
            for n in range(2):
                link(nc.vector.tensor_tensor(tmp[:], cum[:], hot[:, n, :, :], ALU.mult))
                link(nc.vector.tensor_reduce(posf[:, n, :], tmp[:], AX.X, ALU.add))
            nc.vector.tensor_copy(pos[:], posf[:]).then_inc(r_pos, 1)
            dve.wait_ge(r_exp, 1)
            for n in range(2):
                link(nc.vector.tensor_tensor(tmp[:], dif[:, n, :, :], keep[:, n, :, :], ALU.mult))
                link(nc.vector.tensor_reduce(val[:, n, :], tmp[:], AX.X, ALU.add))
            link(nc.vector.reciprocal(mult[:], val[:]))

            def split_w(u, i, n):
                dve.wait_ge(w_hi, i * 3 + (n + 1))
                nc.vector.scalar_tensor_tensor(out=wl[:, u, n, :], in0=wf[:, u, n, :], scalar=WS, in1=wh[:, u, n, :],
                                               op0=ALU.mult, op1=ALU.subtract).then_inc(w_lo, 1)

            def split_x(u, i):
                dve.wait_ge(m_xh, i + 1)
                nc.vector.tensor_tensor(xl[:, u, :, :], psX[:], xh[:, u, :, :], ALU.subtract).then_inc(m_xT, 1)

            for n in range(3):
                split_w(0, 0, n)
            split_x(0, 0)

            def body(u, i, more):
                for p in range(STEPS_E):
                    dve.wait_ge(m_sg, i * STEPS_E + (p + 1))
                    dve.wait_ge(m_hl, i * STEPS_E + (p + 1))
                    nc.vector.scalar_tensor_tensor(out=hf[:, p % 2, :, :], in0=psG[p % 2][:, :, 1, :], scalar=1.0 / WS,
                                                   in1=sg[:, p % 2, :, :], op0=ALU.mult, op1=ALU.mult).then_inc(m_hf, 1)
                    if p == 0:
                        dve.wait_ge(m_y_ps, i + 1)
                    dve.wait_ge(m_hf, i * STEPS_E + (p + 3))
                    nc.vector.tensor_copy(hh[:, u, p * GU:(p + 1) * GU, :], hf[:, p % 2, :, :]).then_inc(m_hh, 1)
                    if more and p > 0:
                        split_w(1 - u, i + 1, p - 1)
                if more:
                    split_x(1 - u, i + 1)
            blocks(dve, body)
            dve.wait_ge(s_x1, 16)
            for t in range(NT):
                y = ya[:, t % 2, :, :]
                dve.wait_ge(f_y[t % 2], 32 * (t // 2 + 1))
                if t >= 2:
                    dve.wait_ge(s_out[t % 2], 16 * (t // 2))
                nc.vector.tensor_scalar(yo[:, t % 2, :], y[:, 0, :], mult[:, 0, t:t + 1], None, ALU.mult).then_inc(f_step, 1)
                dve.wait_ge(f_step, 4 * t + 1)
                nc.vector.scalar_tensor_tensor(out=yo[:, t % 2, :], in0=y[:, 1, :], scalar=mult[:, 1, t:t + 1], in1=yo[:, t % 2, :],
                                               op0=ALU.mult, op1=ALU.add).then_inc(f_step, 1)
                dve.wait_ge(f_step, 4 * t + 2)
                nc.vector.tensor_tensor(yo[:, t % 2, :], yo[:, t % 2, :], gbB[:, t // TPB, :], ALU.mult).then_inc(f_step, 1)
                dve.wait_ge(f_step, 4 * t + 3)
                nc.vector.tensor_tensor(yo[:, t % 2, :], yo[:, t % 2, :], X1[:, t, :], ALU.add).then_inc(f_step, 1)

        @block.tensor
        def _(pe):
            for free in (m_y_ps, m_hf, m_hl, m_y, m_xT_ps):
                pe.sem_inc(free, 2)
            pe.sem_inc(w_lo, 6)
            for u in range(2):
                pe.sem_inc(s_ys[u], 16)
            pe.wait_ge(s_in, 64)
            pe.wait_ge(r_hot, 1)
            for n in range(2):
                mm = nc.tensor.matmul(psR[:, n, :, :].rearrange("p t e -> p (t e)"), bel[:, n, :], both[:].rearrange("p t e -> p (t e)"),
                                      start=True, stop=True)
            mm.then_inc(r_cum, 1)

            def turn(u, i):
                pe.wait_ge(s_xr[u], 16 * (i // 2) + 16)
                for r in range(RC):
                    for k in range(KD):
                        mm = nc.tensor.transpose(psX[:, k, r * P:(r + 1) * P], xr[:, u, r, k * P:(k + 1) * P], eye[:])
                mm.then_inc(m_xT_ps, 1)

            turn(0, 0)
            HALVES = ((0, 0), (1, 0), (0, 1))

            def body(u, i, more):
                pe.wait_ge(m_xT, i + 1)
                pe.wait_ge(w_lo, i * 3 + (2 + 6))
                for p in range(STEPS_E):
                    pe.wait_ge(m_hf, i * STEPS_E + (p + 1))
                    for g in range(GU):
                        f = p * GU + g
                        for n in range(2):
                            for k in range(KD):
                                for a, b in HALVES:
                                    mm = nc.tensor.matmul(psG[p % 2][:, g, n, :], (wh, wl)[a][:, u, n, k * F + f * P:k * F + (f + 1) * P],
                                                          (xh, xl)[b][:, u, k, :], start=(k == 0 and (a, b) == (0, 0)),
                                                          stop=(k == KD - 1 and (a, b) == HALVES[-1]), skip_group_check=True)
                    mm.then_inc(m_gu, 1)
                if more:
                    turn(1 - u, i + 1)
                pe.wait_ge(m_y, i + 1)
                pe.wait_ge(w_lo, i * 3 + (3 + 6))
                for f in range(FC):
                    if f % GU == 0:
                        pe.wait_ge(m_hl, i * STEPS_E + (f // GU + 1 + 2))
                    for r in range(RC):
                        for a, b in HALVES:
                            mm = nc.tensor.matmul(psY[u][:, r, :], (hh, hl)[a][:, u, f, r * P:(r + 1) * P],
                                                  (wh, wl)[b][:, u, W2, f * D:(f + 1) * D],
                                                  start=(f == 0 and r == 0 and (a, b) == (0, 0)), stop=(f == FC - 1), skip_group_check=True)
                mm.then_inc(m_y_ps, 1)
            blocks(pe, body)


def kernel(**inputs):
    import numpy as np
    import concourse.bacc as bacc
    from concourse.bass_utils import run_bass_kernel_spmd as run

    pos = np.arange(S, dtype=np.float32)
    freq = (np.float32(1.0) / np.float32(2500) ** (np.arange(HD // 2, dtype=np.float32) / np.float32(HD // 2))).astype(np.float32)
    theta = pos[:, None] * freq[None, :]
    rope = np.stack([np.repeat(np.cos(theta), 2, axis=1),
                     np.stack([-np.sin(theta), np.sin(theta)], axis=2).reshape(S, HD)], axis=1)
    rope = np.ascontiguousarray(rope.reshape(TPB, P, 2, HD).transpose(1, 0, 2, 3)).astype(np.float32)
    below = np.stack([np.triu(np.ones((P, P), np.float32), 1), np.ones((P, P), np.float32)], axis=1)
    below = np.ascontiguousarray(below)
    counts = np.concatenate([E - np.arange(E), np.arange(16) * ROWS, np.arange(40)]).astype(np.float32)
    counts = np.ascontiguousarray(np.tile(counts, (P, 1)))
    arrays = {
        "x": np.ascontiguousarray(inputs["L0_attn_tokens"]),
        "qkv_wT": np.ascontiguousarray(np.asarray(inputs["L0_attn_qkv_w"]).T),
        "qkv_b": np.ascontiguousarray(inputs["L0_attn_qkv_b"]),
        "out_wT": np.ascontiguousarray(np.asarray(inputs["L0_attn_out_w"]).T),
        "out_b": np.ascontiguousarray(inputs["L0_attn_out_b"]),
        "cT": np.ascontiguousarray(np.asarray(inputs["L0_c"]).T),
        "wmod": np.ascontiguousarray(inputs["L0_wmod"]),
        "gate_w": np.ascontiguousarray(inputs["L0_ffn_gate_w"]),
        "w1": np.ascontiguousarray(inputs["L0_ffn_w1"]),
        "w2": np.ascontiguousarray(inputs["L0_ffn_w2"]),
        "w3": np.ascontiguousarray(inputs["L0_ffn_w3"]),
        "ident": np.eye(P, dtype=np.float32),
        "ident16": np.eye(P, dtype=np.float16),
        "rope": rope,
        "below": below,
        "counts": counts,
    }
    nc = bacc.Bacc("TRN2", target_bir_lowering=False, num_devices=1)
    args = [nc.dram_tensor(n, a.shape, mybir.dt.from_np(a.dtype), kind="ExternalInput").ap() for n, a in arrays.items()]
    args.append(nc.dram_tensor("y", (B, S, D), F32, kind="ExternalOutput").ap())
    adaln(nc, *args)
    r = run(nc, [arrays], core_ids=[0])
    return r.results[0]["y"]
```

```python
from contextlib import ExitStack

import concourse.bass as bass
from concourse import mybir

F32 = mybir.dt.float32
F16 = mybir.dt.float16
ALU = mybir.AluOpType
ACT = mybir.ActivationFunctionType
AX = mybir.AxisListType

P = 128
B, S, D = 4, 1024, 256
H, HD = 16, 16
KD = D // P
TPB = S // P
NT = B * TPB
PAIRS = H // 2
HV = 2 * HD + 1
STEPS = 2 * TPB
T_AT = (7, 9, 12, 15)
LAG = 2
LO_POOL = (0, 4, 10, 12, 14)
LO_DVE = tuple(j for j in range(STEPS) if j not in LO_POOL)
QCH = S // 512
LN_EPS = 1e-5
CREDIT = 1
NORM_CAP = 1e12
SCALE = HD ** -0.5
E, F = 8, 1024
FC = F // P
ROWS = 256
RC = ROWS // P
BLOCKS = (2 * B * S + E * (ROWS - 1)) // ROWS
JITTER = 0.01
LOWEST = -3.0e38
GU = 2
STEPS_E = FC // GU
TILES_B = BLOCKS * RC
LIST = 8
LISTS = 2 * NT // LIST
ROUND = 1.5 * 2.0 ** 23
END = 4
ENDS = NT // END
YB = 4
WS = 64.0
SA, CA, GA, SB, CB, GB = range(6)


def adaln(nc, x, qkv_wT, qkv_b, out_wT, out_b, cT, wmod, gate_w, w1, w2, w3, ident, ident16, rope, below, counts, out):
    mod_dram = nc.dram_tensor("mod_dram", (B, 6 * D), F32, kind="Internal").ap()
    x1_dram = nc.dram_tensor("x1_dram", (B * S, D), F32, kind="Internal").ap()
    h2_dram = nc.dram_tensor("h2_dram", (B * S, D), F32, kind="Internal").ap()
    ys_dram = nc.dram_tensor("ys_dram", (2 * B * S + BLOCKS * ROWS, D), F32, kind="Internal").ap()

    with ExitStack() as whole:
        LG = whole.enter_context(nc.sbuf_tensor("LG", [P, NT, E], F32))
        attention(nc, x, qkv_wT, qkv_b, out_wT, out_b, cT, wmod, gate_w, ident, ident16, rope, mod_dram, x1_dram, h2_dram, LG)
        experts(nc, w1, w2, w3, ident, below, counts, mod_dram, x1_dram, h2_dram, ys_dram, LG, out)


def attention(nc, x, qkv_wT, qkv_b, out_wT, out_b, cT, wmod, gate_w, ident, ident16, rope, mod_dram, x1_dram, h2_dram, LG):
    with ExitStack() as ctx:
        def sb(name, shape, dt=F32):
            return ctx.enter_context(nc.sbuf_tensor(name, shape, dt))

        def sem(name):
            return ctx.enter_context(nc.semaphore(name))

        modB = sb("modB", [P, B, 2, D])
        idn = sb("idn", [P, P])
        idn16 = sb("idn16", [P, P], F16)
        wqkv = sb("wqkv", [P, KD, 3 * D])
        qkvb = sb("qkvb", [P, 3 * D])
        wo = sb("wo", [P, KD, D])
        wog = sb("wog", [P, B, KD, D])
        ob = sb("ob", [P, D])
        gob = sb("gob", [P, B, D])
        rp = sb("rp", [P, TPB, 2, HD])
        ct = sb("ct", [P, KD, B])
        ce = sb("ce", [P, KD, B])
        cs = sb("cs", [P, KD, B])
        modT = sb("modT", [P, 2, KD, B])
        xA = sb("xA", [P, 2, D])
        xC = sb("xC", [P, 2, D])
        mod = sb("mod", [B, 6 * D])
        sgn = sb("sgn", [B, 2, D])
        eps = sb("eps", [P, 1])
        mhalf = sb("mhalf", [P, 2 * H])
        bnA = sb("bnA", [P, 6])
        dfA = sb("dfA", [P, 3])
        mvA = sb("mvA", [P, 2])
        veA = sb("veA", [P, 1])
        rsA = sb("rsA", [P, 1])
        xnA = sb("xnA", [P, D])
        hTA = sb("hTA", [P, KD, P])
        qk = sb("qk", [P, 2 * H, HD])
        rc = sb("rc", [P, 2 * H, HD])
        rs_ = sb("rs_", [P, 2 * H, HD])
        ss = sb("ss", [P, 2 * H])
        inv = sb("inv", [P, 2 * H])
        QK = sb("QK", [P, 2, TPB, 2, H, 4, HD], F16)
        V = sb("V", [P, 2, TPB, H, HV], F16)
        vA = sb("vA", [P, H, HD])
        EX = sb("EX", [P, 4, S])
        PH = sb("PH", [P, 4, S], F16)
        PL = sb("PL", [P, 4, S], F16)
        wm = EX[:, 0:3, :].rearrange("p a n -> p (a n)").rearrange("p (k n) -> p k n", k=KD)
        gaB = EX[:, 3, :].rearrange("p (b d) -> p b d", b=B)
        QT = sb("QT", [P, 2, S], F16)
        KT = sb("KT", [P, 2, S], F16)
        orec = sb("orec", [P, 2, TPB])
        osum = sb("osum", [P, 2, TPB, HD])
        AT = sb("AT", [P, 2, TPB, D])
        aS = sb("aS", [P, D])
        aT = sb("aT", [P, KD, P])
        xg = sb("xg", [P, D])
        x1 = sb("x1", [P, 2, D])
        bnC = sb("bnC", [P, 6])
        dfC = sb("dfC", [P, 3])
        mvC = sb("mvC", [P, 2, 2])
        veC = sb("veC", [P, 1])
        rsC = sb("rsC", [P, 2, 1])
        xnC = sb("xnC", [P, D])
        h2 = sb("h2", [P, 2, D])
        h2T = sb("h2T", [P, KD, P])
        gw = sb("gw", [P, KD, E])

        psS = [ctx.enter_context(nc.psum_tensor(f"psS{i}", [P, S], F32)) for i in range(2)]
        psO = [ctx.enter_context(nc.psum_tensor(f"psO{i}", [P, TPB, 64], F32)) for i in range(2)]
        psM = [ctx.enter_context(nc.psum_tensor(f"psM{i}", [P, 512], F32)) for i in range(2)]

        s_xA = [sem(f"s_xA{u}") for u in range(2)]
        s_xC = [sem(f"s_xC{u}") for u in range(2)]
        s_w = sem("s_w")
        s_modw = sem("s_modw")
        s_modb = sem("s_modb")
        setup = sem("setup")
        silu_exp = sem("silu_exp")
        silu_done = sem("silu_done")
        mod_ps = sem("mod_ps")
        mod_ready = sem("mod_ready")
        mod_t = sem("mod_t")
        a_step = sem("a_step")
        a_rstd = sem("a_rstd")
        a_pool = sem("a_pool")
        a_turn = sem("a_turn")
        a_norm = sem("a_norm")
        a_sq = sem("a_sq")
        a_root = sem("a_root")
        a_xn = sem("a_xn")
        a_hT_ps = sem("a_hT_ps")
        a_hT = sem("a_hT")
        a_qk_ps = sem("a_qk_ps")
        a_v_ps = sem("a_v_ps")
        a_qk = sem("a_qk")
        a_vps = sem("a_vps")
        a_v = sem("a_v")
        a_vlo = sem("a_vlo")
        a_rope = sem("a_rope")
        a_ss = sem("a_ss")
        a_inv = sem("a_inv")
        a_split = sem("a_split")
        t_ps = sem("t_ps")
        t_q = sem("t_q")
        t_k = sem("t_k")
        b_scores = sem("b_scores")
        b_exp = sem("b_exp")
        b_hi = sem("b_hi")
        b_split = sem("b_split")
        p_split = sem("p_split")
        b_pv = sem("b_pv")
        b_ostep = sem("b_ostep")
        b_o = sem("b_o")
        c_copy = sem("c_copy")
        c_at_ps = sem("c_at_ps")
        c_at = sem("c_at")
        c_proj = sem("c_proj")
        c_xg = sem("c_xg")
        c_x1 = sem("c_x1")
        c_step = sem("c_step")
        c_pool = sem("c_pool")
        c_rstd = sem("c_rstd")
        c_xn = sem("c_xn")
        c_h2 = sem("c_h2")
        c_st = [sem(f"c_st{u}") for u in range(2)]
        c_h2T_ps = sem("c_h2T_ps")
        c_h2T = sem("c_h2T")
        c_lg_ps = sem("c_lg_ps")
        c_lg = sem("c_lg")

        x_v = x.rearrange("b (t p) d -> p (b t) d", p=P)

        PHASES = [("LAR", 0, 0, 0, 0, TPB // 2),
                  ("t", 0, 0, 0, 0, 1),
                  ("LARTB", TPB, 1, 0, 0, PAIRS // 2),
                  ("LARTBCD", 2 * TPB, PAIRS + 1, PAIRS, 0, PAIRS),
                  ("TBCD", 0, 3 * PAIRS + 1, 3 * PAIRS, 2 * TPB, PAIRS // 2 - 1),
                  ("tBCD", 0, 4 * PAIRS - 1, 4 * PAIRS - 2, 3 * TPB - 2, 1),
                  ("c", 0, 0, 0, 3 * TPB, 0)]

        def ahead(stages, c, u):
            return (c - 1, 1 - u) if "E" in stages else (c, u)

        def phases(eng, body):
            body("L", 0, -2, 0, 0, 0)
            body("LA", 1, -1, 0, 0, 0)
            for stages, r0, t0, b0, c0, n in PHASES:
                if stages == "t":
                    body("first", 0, 0, 0, 0, 0)
                elif stages == "c":
                    body("C", 0, 0, 0, 0, c0)
                    with eng.Fori(0, TPB // 2 - 1) as it:
                        for u in (1, 0):
                            body("CDE", u, 0, 0, 0, it * 2 + (c0 + 2 - u))
                    body("CDE", 1, 0, 0, 0, NT - 1)
                    body("DE", 0, 0, 0, 0, NT)
                elif n == 1:
                    body("TBCD", 0, r0, t0, b0, c0)
                    body("BCD", 1, r0 + 1, t0 + 1, b0 + 1, c0 + 1)
                else:
                    with eng.Fori(0, n) as it:
                        for u in range(2):
                            body(stages, u, it * 2 + (r0 + u), it * 2 + (t0 + u), it * 2 + (b0 + u), it * 2 + (c0 + u))

        def wait_split(eng, j, b, before):
            if j in LO_POOL:
                eng.wait_ge(p_split, (b + (1 - before)) * len(LO_POOL) + (LO_POOL.index(j) + 1))
            else:
                eng.wait_ge(b_split, (b + (1 - before)) * len(LO_DVE) + (LO_DVE.index(j) + 1))

        def mod_bank(n):
            return psO[n][0:B].rearrange("b t n -> b (t n)") if n < 2 else psS[1][0:B, 0:512]

        block = ctx.enter_context(nc.Block())

        @block.sync
        def _(sp):
            sp.dma_start(ct[:], cT.rearrange("(k p) b -> p k b", p=P)).then_inc(s_modw, 16)
            for u in range(2):
                sp.dma_start(xA[:, u, :], x_v[:, u, :]).then_inc(s_xA[u], 16)
            sp.dma_start(wm[:], wmod.rearrange("(k p) n -> p k n", p=P)).then_inc(s_modw, 16)
            sp.dma_start(wqkv[:], qkv_wT.rearrange("(k p) n -> p k n", p=P)).then_inc(s_w, 16)
            sp.dma_start(wo[:], out_wT.rearrange("(k p) n -> p k n", p=P)).then_inc(s_w, 16)
            sp.dma_start(qkvb[:], qkv_b.rearrange("(a n) -> a n", a=1).to_broadcast([P, 3 * D])).then_inc(s_w, 16)
            sp.dma_start(ob[:], out_b.rearrange("(a n) -> a n", a=1).to_broadcast([P, D])).then_inc(s_w, 16)
            sp.dma_start(idn[:], ident).then_inc(s_w, 16)
            sp.dma_start(idn16[:], ident16).then_inc(s_w, 16)
            sp.dma_start(rp[:], rope).then_inc(s_w, 16)
            sp.dma_start(gw[:], gate_w.rearrange("(k p) e -> p k e", p=P)).then_inc(s_w, 16)
            sp.wait_ge(mod_ready, 6)
            sp.dma_start(mod_dram, mod[:]).then_inc(s_modb, 16)
            sp.wait_ge(s_modb, 16)
            m6 = mod_dram.rearrange("(a b) (s d) -> a b s d", a=1, s=6)
            sp.dma_start(gaB, m6[:, :, GA, :].to_broadcast([P, B, D])).then_inc(s_modb, 16)
            sp.dma_start(modB[:], m6[:, :, SB:CB + 1, :].to_broadcast([P, B, 2, D])).then_inc(s_modb, 16)

            for u in range(2):
                sp.dma_start(xC[:, u, :], x_v[:, u, :]).then_inc(s_xC[u], 16)

            def body(stages, u, r, t, b, c):
                if "L" in stages:
                    sp.wait_ge(a_xn, r + 3)
                    sp.dma_start(xA[:, u:u + 1, :], x_v[:, bass.ds((r + 4) % NT, 1), :]).then_inc(s_xA[u], 16)
                if "C" in stages:
                    sp.wait_ge(c_xg, c + 1)
                    sp.dma_start(xC[:, u:u + 1, :], x_v[:, bass.ds((c + 2) % NT, 1), :]).then_inc(s_xC[u], 16)
                    sp.wait_ge(c_x1, c + 1 + CREDIT)
                    sp.dma_start(x1_dram.rearrange("(g p) d -> p g d", p=P)[:, bass.ds(c, 1), :],
                                 x1[:, u:u + 1, :]).then_inc(c_st[u], 16)
                if "D" in stages:
                    d, v = ahead(stages, c, u)
                    sp.wait_ge(c_h2, d * 2 + 2)
                    sp.dma_start(h2_dram.rearrange("(g p) d -> p g d", p=P)[:, bass.ds(d, 1), :],
                                 h2[:, v:v + 1, :]).then_inc(c_st[v], 16)
            phases(sp, body)
            for u in range(2):
                sp.wait_ge(c_st[u], 32 * NT // 2 + 32)
                sp.wait_ge(s_xA[u], 16 * (NT // 2 + 2))
                sp.wait_ge(s_xC[u], 16 * (NT // 2 + 1))

        @block.scalar
        def _(act):
            act.wait_ge(s_modw, 32)
            nc.scalar.activation(ce[:], ct[:], ACT.Exp, scale=-1.0).then_inc(silu_exp, 1)

            def turned(u, t, i):
                act.wait_ge(t_ps, t * 4 + (i + 1))
                half = slice(i // 2 * 512, (i // 2 + 1) * 512)
                nc.scalar.copy((QT, KT)[i % 2][:, u, half], psM[i % 2][:]).then_inc((t_q, t_k)[i % 2], 1)

            def body(stages, u, r, t, b, c):
                if stages == "first":
                    for i in range(4):
                        turned(0, 0, i)
                    act.wait_ge(setup, 5)
                    return
                for j in range(STEPS):
                    if "B" in stages:
                        act.wait_ge(b_scores, b * STEPS + (j + 1))
                        wait_split(act, (j - 4) % STEPS, b, int(j < 4))
                        exp = nc.scalar.activation(EX[:, j % 4, :], psS[j % 2][:], ACT.Exp, scale=SCALE)
                        if j % 2 == 0:
                            act.wait_ge(b_pv, b * STEPS + (j + 1))
                            exp = nc.scalar.activation(PH[:, j % 4, :], psS[j % 2][:], ACT.Exp, scale=SCALE)
                        exp.then_inc(b_exp, 1)
                    if j == 0 and "C" in stages:
                        act.wait_ge(c_at_ps, c + CREDIT)
                        act.wait_ge(b_o, (c // TPB + 1) * (2 * PAIRS) + 2)
                        nc.scalar.copy(aS[:], AT[:, bass.ds((c // TPB) % 2, 1), bass.ds(c % TPB, 1), :]
                                       .rearrange("p a t d -> p (a t d)")).then_inc(c_copy, 1)
                    if j == 0 and "R" in stages:
                        act.wait_ge(a_vps, r + 1 + CREDIT)
                        nc.scalar.copy(V[:, bass.ds((r // TPB) % 2, 1), bass.ds(r % TPB, 1), :, 0:HD].rearrange("p a t h d -> p (a t h) d"),
                                       vA[:]).then_inc(a_v, 1)
                    if j == 2 and "A" in stages:
                        if stages == "LA":
                            act.wait_ge(mod_t, 1)
                        act.wait_ge(a_hT_ps, r + 2)
                        bat = bass.ds((r + 1) // TPB % B, 1)
                        for k in range(KD):
                            ins = nc.scalar.activation(hTA[:, k, :], psM[0][:, k * P:(k + 1) * P], ACT.Identity,
                                                       bias=modT[:, 0, k, bat], scale=modT[:, 1, k, bat])
                        ins.then_inc(a_hT, 1)
                    if j == 3 and "C" in stages:
                        act.wait_ge(c_at_ps, c + 1 + CREDIT)
                        nc.scalar.copy(aT[:].rearrange("p k t -> p (k t)"), psM[1][:, 0:D]).then_inc(c_at, 1)
                    if j == 4 and "R" in stages:
                        act.wait_ge(a_rope, r + 1)
                        nc.scalar.activation(rs_[:], rc[:], ACT.Square).then_inc(a_sq, 1)
                    if j == 8 and "R" in stages and "B" not in stages:
                        act.wait_ge(a_ss, r + 1)
                        nc.scalar.sqrt(ss[:], ss[:]).then_inc(a_root, 1)
                    if j == 12 and "D" in stages:
                        act.wait_ge(c_h2T_ps, ahead(stages, c, u)[0] + 1)
                        nc.scalar.copy(h2T[:].rearrange("p k t -> p (k t)"), psM[1][:, 0:D]).then_inc(c_h2T, 1)
                    if "T" in stages and j - 1 in T_AT:
                        turned((u + 1) % 2, t, T_AT.index(j - 1))
                if "D" in stages:
                    d = ahead(stages, c, u)[0]
                    act.wait_ge(c_lg_ps, d + 1)
                    nc.scalar.copy(LG[:, bass.ds(d, 1), :].rearrange("p a e -> p (a e)"), psM[0][:, 0:E]).then_inc(c_lg, 1)
                if "T" in stages:
                    turned((u + 1) % 2, t, 3)
            phases(act, body)

        @block.gpsimd
        def _(pool):
            nc.gpsimd.memset(mhalf[:], -0.5).then_inc(setup, 1)
            nc.gpsimd.memset(eps[:], LN_EPS).then_inc(setup, 1)
            nc.gpsimd.memset(V[:, :, :, :, 2 * HD:HV], 1.0).then_inc(setup, 1)
            pool.wait_ge(setup, 3)

            def low(b, i):
                j = LO_POOL[i]
                pool.wait_ge(b_exp, b * STEPS + (j + 1))
                pool.wait_ge(b_pv, b * STEPS + (j + 1))
                nc.gpsimd.tensor_tensor(PL[:, j % 4, :], EX[:, j % 4, :], PH[:, j % 4, :], ALU.subtract).then_inc(p_split, 1)

            def rms(u, c):
                pool.wait_ge(c_step, c * 4 + 4)
                nc.gpsimd.tensor_tensor(veC[:], mvC[:, u, 1:2], eps[:], ALU.add).then_inc(c_pool, 1)
                pool.wait_ge(c_pool, c + 1)
                nc.gpsimd.tensor_tensor(rsC[:, u, :], veC[:], mhalf[:, 0:1], ALU.pow).then_inc(c_rstd, 1)

            def scaled(v, d):
                bat = bass.ds(d // TPB, 1)
                pool.wait_ge(c_xn, d + 1)
                pool.wait_ge(c_st[v], 32 * (d // 2) + 32)
                nc.gpsimd.tensor_tensor(h2[:, v, :], xnC[:], modB[:, bat, 1, :].rearrange("p a d -> p (a d)"),
                                        ALU.mult).then_inc(c_h2, 1)
                pool.wait_ge(c_h2, d * 2 + 1)
                nc.gpsimd.tensor_tensor(h2[:, v, :], h2[:, v, :], modB[:, bat, 0, :].rearrange("p a d -> p (a d)"),
                                        ALU.add).then_inc(c_h2, 1)

            def body(stages, u, r, t, b, c):
                if stages == "first":
                    pool.wait_ge(setup, 5)
                    pool.wait_ge(s_modb, 48)
                    return
                if "C" in stages:
                    cbat = c // TPB
                    pool.wait_ge(s_xC[u], 16 * (c // 2) + 16)
                    pool.wait_ge(c_x1, c + CREDIT)
                    nc.gpsimd.tensor_tensor(xg[:], xC[:, u, :],
                                            gob[:, bass.ds(cbat, 1), :].rearrange("p a d -> p (a d)"), ALU.add).then_inc(c_xg, 1)
                if "B" in stages:
                    low(b, 0)
                if "E" in stages:
                    scaled(*ahead(stages, c, u)[::-1])
                if "R" in stages and "B" in stages:
                    tile = r % TPB
                    cos = rp[:, bass.ds(tile, 1), 0, :].to_broadcast([P, 2 * H, HD])
                    sine = rp[:, bass.ds(tile, 1), 1, :].to_broadcast([P, 2 * H, HD])
                    pool.wait_ge(a_qk, r + 1 + CREDIT)
                    pool.wait_ge(a_split, r * 2 + 2)
                    nc.gpsimd.tensor_tensor(rc[:], qk[:], cos, ALU.mult)
                    nc.gpsimd.tensor_tensor(rs_[:, :, 0::2], qk[:, :, 1::2], sine[:, :, 0::2], ALU.mult)
                    nc.gpsimd.tensor_tensor(rs_[:, :, 1::2], qk[:, :, 0::2], sine[:, :, 1::2], ALU.mult).then_inc(a_turn, 1)
                    pool.wait_ge(a_turn, r + 1)
                    nc.gpsimd.tensor_tensor(rc[:], rc[:], rs_[:], ALU.add).then_inc(a_rope, 1)
                if "L" in stages:
                    pool.wait_ge(a_step, (r + 2) * 4 + 4)
                    nc.gpsimd.tensor_tensor(veA[:], mvA[:, 1:2], eps[:], ALU.add).then_inc(a_pool, 1)
                    pool.wait_ge(a_pool, r + 3)
                    nc.gpsimd.tensor_tensor(rsA[:], veA[:], mhalf[:, 0:1], ALU.pow).then_inc(a_rstd, 1)
                if "B" in stages:
                    low(b, 1)
                if "C" in stages:
                    rms(u, c)
                if "R" in stages and "B" in stages:
                    pool.wait_ge(a_ss, r + 1)
                    nc.gpsimd.tensor_tensor(inv[:], ss[:], mhalf[:], ALU.pow).then_inc(a_inv, 1)
                if "D" in stages and "E" not in stages:
                    scaled(u, c)
                if "B" in stages:
                    for i in range(2, len(LO_POOL)):
                        low(b, i)
            phases(pool, body)

        @block.vector
        def _(dve):
            dve.wait_ge(silu_exp, 1)
            nc.vector.tensor_scalar(ce[:], ce[:], 1.0, None, ALU.add).then_inc(silu_done, 1)
            dve.wait_ge(silu_done, 1)
            nc.vector.reciprocal(ce[:], ce[:]).then_inc(silu_done, 1)
            dve.wait_ge(silu_done, 2)
            nc.vector.tensor_tensor(cs[:], ct[:], ce[:], ALU.mult).then_inc(silu_done, 1)
            dve.wait_ge(mod_ps, 1)
            nc.vector.tensor_copy(modT[:, 0, :, :], psS[0][:, 0:KD * B].rearrange("p (k b) -> p k b", k=KD))
            nc.vector.tensor_scalar(modT[:, 1, :, :], psS[0][:, KD * B:2 * KD * B].rearrange("p (k b) -> p k b", k=KD),
                                    1.0, None, ALU.add).then_inc(mod_t, 1)

            def mod_rows():
                dve.wait_ge(mod_ps, 2)
                for n in range(3):
                    ins = nc.vector.tensor_copy(mod[:, n * 512:(n + 1) * 512], mod_bank(n))
                ins.then_inc(mod_ready, 1)
                dve.wait_ge(mod_ready, 1)
                m6 = mod[:].rearrange("b (s d) -> b s d", s=6)
                nc.vector.tensor_scalar(sgn[:], m6[:, GA::3, :], 0.0, 2.0, ALU.is_ge, ALU.mult).then_inc(mod_ready, 1)
                nc.vector.tensor_scalar(m6[:, CA::3, :], m6[:, CA::3, :], 1.0, None, ALU.add)
                dve.wait_ge(mod_ready, 2)
                nc.vector.tensor_scalar(sgn[:], sgn[:], -1.0, None, ALU.add).then_inc(mod_ready, 1)
                dve.wait_ge(mod_ready, 3)
                nc.vector.tensor_tensor(m6[:, GA::3, :], m6[:, GA::3, :], sgn[:], ALU.mult).then_inc(mod_ready, 1)
                dve.wait_ge(mod_ready, 4)
                nc.vector.tensor_scalar(m6[:, GA::3, :], m6[:, GA::3, :], 0.25, None, ALU.max).then_inc(mod_ready, 1)
                dve.wait_ge(mod_ready, 5)
                nc.vector.tensor_tensor(m6[:, GA::3, :], m6[:, GA::3, :], sgn[:], ALU.mult).then_inc(mod_ready, 1)

            def gates():
                dve.wait_ge(s_modb, 48)
                for b in range(B):
                    for k in range(KD):
                        nc.vector.tensor_tensor(wog[:, b, k, :], wo[:, k, :], gaB[:, b, :], ALU.mult)
                    ins = nc.vector.tensor_tensor(gob[:, b, :], ob[:], gaB[:, b, :], ALU.mult)
                ins.then_inc(setup, 2)

            def variance(step, i, per, st, mv, t):
                dve.wait_ge(step, i * per + 1)
                nc.vector.tensor_tensor(t[:, 0:2], st[:, 1:3], st[:, 4:6], ALU.add)
                nc.vector.tensor_tensor(t[:, 2:3], st[:, 1:2], st[:, 4:5], ALU.subtract).then_inc(step, 1)
                dve.wait_ge(step, i * per + 2)
                nc.vector.tensor_scalar(mv[:, 0:1], t[:, 0:1], 0.5, None, ALU.mult)
                nc.vector.scalar_tensor_tensor(out=t[:, 2:3], in0=t[:, 2:3], scalar=0.25, in1=t[:, 2:3],
                                               op0=ALU.mult, op1=ALU.mult).then_inc(step, 1)
                dve.wait_ge(step, i * per + 3)
                nc.vector.scalar_tensor_tensor(out=mv[:, 1:2], in0=t[:, 1:2], scalar=1.0 / D, in1=t[:, 2:3],
                                               op0=ALU.mult, op1=ALU.add).then_inc(step, 1)

            def body(stages, u, r, t, b, c):
                if stages == "first":
                    gates()
                    return
                if stages == "LA":
                    mod_rows()
                    dve.wait_ge(s_w, 16 * 8)
                    dve.wait_ge(setup, 3)
                for j in range(STEPS):
                    if "B" in stages and j in LO_DVE:
                        dve.wait_ge(b_exp, b * STEPS + (j + 1))
                        dve.wait_ge(b_pv, b * STEPS + (j + 1))
                        if j % 2:
                            nc.vector.tensor_copy(PH[:, j % 4, :], EX[:, j % 4, :]).then_inc(b_hi, 1)
                    if j == 1 and "R" in stages and "B" not in stages:
                        tile = r % TPB
                        cos = rp[:, bass.ds(tile, 1), 0, :].to_broadcast([P, 2 * H, HD])
                        sine = rp[:, bass.ds(tile, 1), 1, :].to_broadcast([P, 2 * H, HD])
                        dve.wait_ge(a_qk, r + 1 + CREDIT)
                        dve.wait_ge(a_split, r * 2 + 2)
                        nc.vector.tensor_tensor(rc[:], qk[:], cos, ALU.mult)
                        nc.vector.tensor_tensor(rs_[:, :, 0::2], qk[:, :, 1::2], sine[:, :, 0::2], ALU.mult)
                        nc.vector.tensor_tensor(rs_[:, :, 1::2], qk[:, :, 0::2], sine[:, :, 1::2], ALU.mult).then_inc(a_turn, 1)
                        dve.wait_ge(a_turn, r + 1)
                        nc.vector.tensor_tensor(rc[:], rc[:], rs_[:], ALU.add).then_inc(a_rope, 1)
                    if j == 1 and "R" in stages:
                        vt = V[:, bass.ds((r // TPB) % 2, 1), bass.ds(r % TPB, 1), :, :].rearrange("p a t h d -> p (a t h) d")
                        dve.wait_ge(a_v, r + 1)
                        nc.vector.tensor_tensor(vt[:, :, HD:2 * HD], vA[:], vt[:, :, 0:HD], ALU.subtract).then_inc(a_vlo, 1)
                    if j == 2 and "L" in stages:
                        dve.wait_ge(s_xA[u], 16 * ((r + 2) // 2) + 16)
                        nc.vector.bn_stats(bnA[:], xA[:, u, :]).then_inc(a_step, 1)
                        variance(a_step, r + 2, 4, bnA, mvA, dfA)
                    if j == 4 and "L" in stages:
                        dve.wait_ge(a_rstd, r + 3)
                        if "A" in stages:
                            dve.wait_ge(a_hT_ps, r + 2)
                        nc.vector.tensor_scalar(xnA[:], xA[:, u, :], mvA[:, 0:1], rsA[:, 0:1],
                                                ALU.subtract, ALU.mult).then_inc(a_xn, 1)
                    if j == 4 and "A" in stages:
                        dve.wait_ge(a_v_ps, r + 2)
                        nc.vector.tensor_tensor(vA[:].rearrange("p h d -> p (h d)"), psM[0][:, 0:D], qkvb[:, 2 * D:3 * D],
                                                ALU.add).then_inc(a_vps, 1)
                    if j == 5 and "C" in stages:
                        dve.wait_ge(c_proj, c + 1)
                        dve.wait_ge(c_xg, c + 1)
                        dve.wait_ge(c_st[u], 32 * (c // 2) + 32)
                        nc.vector.tensor_tensor(x1[:, u, :], psM[1][:, 0:D], xg[:], ALU.add).then_inc(c_x1, 1)
                        dve.wait_ge(c_x1, c + 1 + CREDIT)
                        nc.vector.bn_stats(bnC[:], x1[:, u, :]).then_inc(c_step, 1)
                        variance(c_step, c, 4, bnC, mvC[:, u, :], dfC)
                    if j == 6 and "R" in stages:
                        dve.wait_ge(a_sq, r + 1)
                        nc.vector.tensor_reduce(ss[:], rs_[:], AX.X, ALU.add).then_inc(a_ss, 1)
                    if j == 7 and "A" in stages:
                        dve.wait_ge(a_qk_ps, r + 2)
                        if "R" in stages:
                            dve.wait_ge(a_rope, r + 1)
                        nc.vector.tensor_tensor(qk[:].rearrange("p h d -> p (h d)"), psM[1][:], qkvb[:, 0:2 * D],
                                                ALU.add).then_inc(a_qk, 1)
                    if j == (0 if "E" in stages else 8) and "D" in stages:
                        d, v = ahead(stages, c, u)
                        dve.wait_ge(c_rstd, d + 1)
                        nc.vector.tensor_scalar(xnC[:], x1[:, v, :], mvC[:, v, 0:1], rsC[:, v, :],
                                                ALU.subtract, ALU.mult).then_inc(c_xn, 1)
                    if j == 11 and "R" in stages:
                        if "B" not in stages:
                            dve.wait_ge(a_root, r + 1)
                            nc.vector.reciprocal(inv[:], ss[:]).then_inc(a_inv, 1)
                        dve.wait_ge(a_inv, r + 1)
                        nc.vector.scalar_tensor_tensor(out=rc[:], in0=inv[:].rearrange("p (h a) -> p h a", a=1).to_broadcast([P, 2 * H, HD]),
                                                       scalar=NORM_CAP, in1=rc[:], op0=ALU.min, op1=ALU.mult).then_inc(a_norm, 1)
                        dve.wait_ge(a_norm, r + 1)
                        for part in range(2):
                            for q in range(2):
                                dst = QK[:, bass.ds((r // TPB) % 2, 1), bass.ds(r % TPB, 1), q, :, :, :].rearrange(
                                    "p a t h f d -> p (a t h) f d")
                                full = rc[:, q * H:(q + 1) * H, :].rearrange("p h (a d) -> p h a d", a=1).to_broadcast([P, H, 2, HD])
                                hi = dst[:, :, 0:1, :].to_broadcast([P, H, 2, HD])
                                two = (dst[:, :, part::2, :], dst[:, :, 2 * part:2 * part + 2, :])[q]
                                if part == 0:
                                    ins = nc.vector.tensor_copy(two, full)
                                else:
                                    ins = nc.vector.tensor_tensor(two, full, hi, ALU.subtract)
                            ins.then_inc(a_split, 1)
                            if part == 0:
                                dve.wait_ge(a_split, r * 2 + 1 + 2)
                    if "B" in stages and j in LO_DVE:
                        if j % 2:
                            dve.wait_ge(b_hi, b * (STEPS // 2) + (j // 2 + 1))
                        nc.vector.tensor_tensor(PL[:, j % 4, :], EX[:, j % 4, :], PH[:, j % 4, :], ALU.subtract).then_inc(b_split, 1)
                if "B" in stages:
                    for hh in range(2):
                        dve.wait_ge(b_pv, b * STEPS + (STEPS - 1 + hh + 4))
                        nc.vector.reciprocal(orec[:, hh, :], psO[hh][:, :, 2 * HD:HV].rearrange("p t a -> p (t a)"))
                        nc.vector.tensor_reduce(osum[:, hh, :, :], psO[hh][:, :, 0:2 * HD].rearrange("p t (f d) -> p t d f", f=2),
                                                AX.X, ALU.add).then_inc(b_ostep, 1)
                    for hh in range(2):
                        dve.wait_ge(b_ostep, b * 2 + (hh + 1))
                        rec = orec[:, hh, :].rearrange("p (t a) -> p t a", a=1).to_broadcast([P, TPB, HD])
                        dst = AT[:, bass.ds((b // PAIRS) % 2, 1), :, bass.ds((b % PAIRS) * (2 * HD) + hh * HD, HD)].rearrange(
                            "p a t d -> p (a t) d")
                        nc.vector.tensor_tensor(dst, osum[:, hh, :, :], rec, ALU.mult).then_inc(b_o, 1)
            phases(dve, body)

        @block.tensor
        def _(pe):
            pe.sem_inc(b_pv, 4)
            pe.sem_inc(b_split, len(LO_DVE))
            pe.sem_inc(p_split, len(LO_POOL))
            pe.sem_inc(a_split, 2)
            for free in (a_hT, a_vps, a_qk, c_at, c_x1, c_at_ps, c_h2T, c_lg):
                pe.sem_inc(free, CREDIT)
            pe.sem_inc(b_o, 2)
            for u in range(2):
                pe.sem_inc(c_st[u], 32)
            pe.wait_ge(silu_done, 3)
            for n in range(2 * KD):
                for k in range(KD):
                    mm = nc.tensor.matmul(psS[0][:, n * B:(n + 1) * B], wm[:, k, n * P:(n + 1) * P], cs[:, k, :],
                                          start=(k == 0), stop=(k == KD - 1))
            mm.then_inc(mod_ps, 1)
            for n in range(3):
                for k in range(KD):
                    mm = nc.tensor.matmul(mod_bank(n), cs[:, k, :], wm[:, k, n * 512:(n + 1) * 512],
                                          start=(k == 0), stop=(k == KD - 1))
            mm.then_inc(mod_ps, 1)
            pe.wait_ge(s_w, 16 * 8)

            def free_bank(me, stages, r, t, c):
                for order in (["hT", "v", "q0", "q1", "lg"], ["at", "proj", "qk", "k0", "h2T", "k1"]):
                    if me not in order:
                        continue
                    i = order.index(me)
                    for back in range(1, len(order) + 1):
                        prev = order[(i - back) % len(order)]
                        new = 0 if back > i else 1
                        if prev in ("hT", "v", "qk") and "A" in stages:
                            pe.wait_ge({"hT": a_hT, "v": a_vps, "qk": a_qk}[prev], r + (1 + new + CREDIT))
                            return
                        if prev in ("at", "proj") and "C" in stages:
                            pe.wait_ge({"at": c_at, "proj": c_x1}[prev], c + (new + CREDIT))
                            return
                        if prev in ("h2T", "lg") and "D" in stages:
                            pe.wait_ge({"h2T": c_h2T, "lg": c_lg}[prev], ahead(stages, c, 0)[0] + (new + CREDIT))
                            return
                        if prev[0] in "qk" and prev != "qk" and "T" in stages:
                            pe.wait_ge({"q": t_q, "k": t_k}[prev[0]], (t + (new - 1)) * 2 + (int(prev[1]) + 1))
                            return

            def scores(u, j):
                kt, hh = j // 2, j % 2
                rows = slice(64 * hh, 64 * hh + 64)
                for q in range(QCH):
                    mm = nc.tensor.matmul(psS[j % 2][:, q * 512:(q + 1) * 512], KT[rows, u, kt * P:(kt + 1) * P],
                                          QT[rows, u, q * 512:(q + 1) * 512], start=True, stop=True)
                mm.then_inc(b_scores, 1)

            def turn(stages, r, t, c, i):
                q, half = i % 2, i // 2
                if stages:
                    free_bank("qk"[q] + str(half), stages, r, t, c)
                bat = t // PAIRS
                pe.wait_ge(a_split, (bat * TPB + 4 * half + 4) * 2 + 2)
                for n in range(4):
                    lhsT = QK[:, bass.ds(bat % 2, 1), 4 * half + n, q, bass.ds((t % PAIRS) * 2, 2), :, :].rearrange(
                        "p a h f d -> p (a h f d)")
                    mm = nc.tensor.matmul(psM[q][:, n * P:(n + 1) * P], lhsT, idn16[:], start=True, stop=True)
                mm.then_inc(t_ps, 1)

            def values(b, j):
                kt, hh = j // 2, j % 2
                if kt == 0:
                    pe.wait_ge(b_o, b * 2 + (hh + 1))
                wait_split(pe, j, b, 0)
                rhs = V[:, bass.ds((b // PAIRS) % 2, 1), kt, bass.ds((b % PAIRS) * 2 + hh, 1), :].rearrange(
                    "p a h d -> p (a h d)")
                for q in range(TPB):
                    for part in (PH, PL):
                        mm = nc.tensor.matmul(psO[hh][:, q, 0:HV], part[:, j % 4, q * P:(q + 1) * P], rhs,
                                              start=(kt == 0 and q == 0 and part is PH), stop=(kt == TPB - 1),
                                              skip_group_check=True)
                mm.then_inc(b_pv, 1)

            def body(stages, u, r, t, b, c):
                if stages == "first":
                    pe.wait_ge(a_vps, TPB + 1 + CREDIT)
                    pe.wait_ge(a_qk, TPB + 1 + CREDIT)
                    for i in range(4):
                        if i >= 2:
                            pe.wait_ge((t_q, t_k)[i % 2], 1)
                        turn("", r, 0, c, i)
                    pe.wait_ge(t_q, 2)
                    pe.wait_ge(t_k, 1)
                    pe.wait_ge(mod_ready, 1)
                    scores(0, 0)
                    scores(0, 1)
                    pe.wait_ge(setup, 5)
                    return
                for j in range(STEPS):
                    if j == 1 and "A" in stages:
                        pe.wait_ge(a_xn, r + 2)
                        free_bank("hT", stages, r, t, c)
                        for k in range(KD):
                            mm = nc.tensor.transpose(psM[0][:, k * P:(k + 1) * P], xnA[:, k * P:(k + 1) * P], idn[:])
                        mm.then_inc(a_hT_ps, 1)
                    if j == 2 and "B" in stages:
                        pe.wait_ge(t_k, b * 2 + 2)
                    if j == 2 and "C" in stages:
                        pe.wait_ge(c_copy, c + 1)
                        if "E" in stages:
                            pe.wait_ge(c_x1, c + CREDIT)
                        free_bank("at", stages, r, t, c)
                        for k in range(KD):
                            mm = nc.tensor.transpose(psM[1][:, k * P:(k + 1) * P], aS[:, k * P:(k + 1) * P], idn[:])
                        mm.then_inc(c_at_ps, 1)
                    if j == 3 and "A" in stages:
                        pe.wait_ge(a_hT, r + 2 + CREDIT)
                        for k in range(KD):
                            mm = nc.tensor.matmul(psM[0][:, 0:D], hTA[:, k, :], wqkv[:, k, 2 * D:3 * D],
                                                  start=(k == 0), stop=(k == KD - 1))
                        mm.then_inc(a_v_ps, 1)
                    if j == 4 and "C" in stages:
                        pe.wait_ge(c_at, c + 1 + CREDIT)
                        for k in range(KD):
                            mm = nc.tensor.matmul(psM[1][:, 0:D], aT[:, k, :],
                                                  wog[:, bass.ds(c // TPB, 1), k, :].rearrange("p a d -> p (a d)"),
                                                  start=(k == 0), stop=(k == KD - 1))
                        mm.then_inc(c_proj, 1)
                    if j == 6 and "A" in stages:
                        free_bank("qk", stages, r, t, c)
                        for k in range(KD):
                            mm = nc.tensor.matmul(psM[1][:, :], hTA[:, k, :], wqkv[:, k, 0:2 * D],
                                                  start=(k == 0), stop=(k == KD - 1))
                        mm.then_inc(a_qk_ps, 1)
                    if j == 11 and "D" in stages:
                        d, v = ahead(stages, c, u)
                        pe.wait_ge(c_h2, d * 2 + 2)
                        free_bank("h2T", stages, r, t, c)
                        for k in range(KD):
                            mm = nc.tensor.transpose(psM[1][:, k * P:(k + 1) * P], h2[:, v, k * P:(k + 1) * P], idn[:])
                        mm.then_inc(c_h2T_ps, 1)
                    if j == 14 and "D" in stages:
                        free_bank("lg", stages, r, t, c)
                        pe.wait_ge(c_h2T, ahead(stages, c, u)[0] + 1 + CREDIT)
                        for k in range(KD):
                            mm = nc.tensor.matmul(psM[0][:, 0:E], h2T[:, k, :], gw[:, k, :], start=(k == 0), stop=(k == KD - 1))
                        mm.then_inc(c_lg_ps, 1)
                    if "T" in stages and j in T_AT:
                        turn(stages, r, t, c, T_AT.index(j))
                    if "B" not in stages:
                        continue
                    pe.wait_ge(b_exp, b * STEPS + (j + 1))
                    if j + 2 < STEPS:
                        scores(u, j + 2)
                    elif "T" in stages:
                        if j + 2 == STEPS:
                            pe.wait_ge(t_q, t * 2 + 2)
                            pe.wait_ge(t_k, t * 2 + 1)
                        scores((u + 1) % 2, j + 2 - STEPS)
                    if j >= LAG:
                        values(b, j - LAG)
                    if j == STEPS - 1:
                        for late in range(STEPS - LAG, STEPS):
                            values(b, late)
            phases(pe, body)


def experts(nc, w1, w2, w3, ident, below, counts, mod_dram, x1_dram, h2_dram, ys_dram, LG, out):
    with ExitStack() as ctx:
        def sb(name, shape, dt=F32):
            return ctx.enter_context(nc.sbuf_tensor(name, shape, dt))

        def sem(name):
            return ctx.enter_context(nc.semaphore(name))

        NE = [P, NT, E]
        X1 = sb("X1", [P, NT, D])
        gbB = sb("gbB", [P, B, D])
        eye = sb("eye", [P, P])
        bel = sb("bel", [P, 2, P])
        cnt = sb("cnt", [P, 64 + P + 1])
        key = sb("key", NE)
        hot = sb("hot", [P, 2, NT, E])
        both = sb("both", NE)
        lg2 = sb("lg2", NE)
        tmp = sb("tmp", NE)
        keep = sb("keep", [P, 2, NT, E])
        dif = sb("dif", [P, 2, NT, E])
        scan = sb("scan", [P, 2, NT, E])
        cum = sb("cum", NE)
        val = sb("val", [P, 2, NT])
        kmax = sb("kmax", [P, NT])
        mult = sb("mult", [P, 2, NT])
        posf = sb("posf", [P, 2, NT])
        tileb = sb("tileb", [P, 2, NT])
        placeb = sb("placeb", [P, 2, NT])
        isrow = sb("isrow", [P, 2, LIST, P], F16)
        istile = sb("istile", [P, 2, LIST, TILES_B], F16)
        token = sb("token", [P, 2, LIST, 2, TILES_B], F16)
        listf = sb("listf", [P, 4, TILES_B])
        lists = sb("lists", [P, 2, TILES_B + 2 * RC], mybir.dt.uint32)
        gate = sb("gate", [P, 4])
        come = sb("come", [P, 2, RC], mybir.dt.uint32)
        go = sb("go", [P, 2, RC], mybir.dt.uint32)
        ge = sb("ge", [P, E, 16])
        nblk = sb("nblk", [P, E])
        first = sb("first", [P, 4, E])
        blk = sb("blk", [P, BLOCKS + 1, E])
        blkf = sb("blkf", [P, BLOCKS + 1])
        blki = sb("blki", [P, BLOCKS + 1], mybir.dt.int32)
        wf = sb("wf", [P, 2, 3, KD * F])
        wh = sb("wh", [P, 2, 3, KD * F], F16)
        wl = sb("wl", [P, 2, 3, KD * F], F16)
        xr = sb("xr", [P, 2, RC, D])
        xh = sb("xh", [P, 2, KD, ROWS], F16)
        xl = sb("xl", [P, 2, KD, ROWS], F16)
        sg = sb("sg", [P, 2, GU, ROWS])
        hf = sb("hf", [P, 2, GU, ROWS])
        hh = sb("hh", [P, 2, FC, ROWS], F16)
        hl = sb("hl", [P, 2, FC, ROWS], F16)
        yr = sb("yr", [P, 2, RC, D])
        ya = wf[:].rearrange("p a n f -> p (a n f)").rearrange("p (y n t d) -> p y n t d", n=2, t=END, d=D)

        psR = ctx.enter_context(nc.psum_tensor("psR", [P, 2, NT, E], F32))
        psX = ctx.enter_context(nc.psum_tensor("psX", [P, KD, ROWS], F32))
        psL = psX[:].rearrange("p k r -> p (k r)")[:, 0:2 * TILES_B].rearrange("p (n t) -> p n t", n=2)
        psG = [ctx.enter_context(nc.psum_tensor(f"psG{i}", [P, GU, 2, ROWS], F32)) for i in range(2)]
        psY = [ctx.enter_context(nc.psum_tensor(f"psY{i}", [P, RC, D], F32)) for i in range(2)]

        s_in = sem("s_in")
        l_row = sem("l_row")
        l_first = sem("l_first")
        l_tile = sem("l_tile")
        l_token = sem("l_token")
        l_sum = sem("l_sum")
        l_come = sem("l_come")
        l_go = sem("l_go")
        s_x1 = sem("s_x1")
        s_blk = sem("s_blk")
        r_step = sem("r_step")
        r_dif = sem("r_dif")
        r_exp = sem("r_exp")
        r_hot = sem("r_hot")
        r_cum = sem("r_cum")
        r_mult = sem("r_mult")
        s_w = [sem(f"s_w{u}") for u in range(2)]
        s_xr = [sem(f"s_xr{u}") for u in range(2)]
        m_xT_ps = sem("m_xT_ps")
        m_xh = sem("m_xh")
        m_xT = sem("m_xT")
        m_gu = sem("m_gu")
        m_sg = sem("m_sg")
        m_hf = sem("m_hf")
        m_hh = sem("m_hh")
        m_hl = sem("m_hl")
        w_hi = sem("w_hi")
        w_lo = sem("w_lo")
        m_y_ps = sem("m_y_ps")
        m_y = sem("m_y")
        s_ys = [sem(f"s_ys{u}") for u in range(2)]
        f_y = [sem(f"f_y{u}") for u in range(YB)]
        f_first = sem("f_first")
        f_both = sem("f_both")
        f_gate = sem("f_gate")
        f_x = sem("f_x")
        s_out = sem("s_out")

        rows = lambda d: d.rearrange("(g p) d -> p g d", p=P)
        w_v = (w1.rearrange("e (k p) f -> p (e k) f", p=P), w3.rearrange("e (k p) f -> p (e k) f", p=P),
               w2.rearrange("e (f p) d -> p (e f) d", p=P))
        chunks = (KD, KD, FC)
        W2 = 2

        def reused(i, n):
            return not isinstance(i, int) or i >= n

        def blocks(eng, body):
            for i in range(2):
                body(i, i, True)
            with eng.Fori(0, (BLOCKS - 1) // 2 - 1) as it:
                for u in range(2):
                    body(u, it * 2 + (2 + u), True)
            for i in range((BLOCKS - 1) // 2 * 2, BLOCKS):
                body(i % 2, i, i + 1 < BLOCKS)

        block = ctx.enter_context(nc.Block())

        @block.sync
        def _(sp):
            sp.dma_start(bel[:], below).then_inc(s_in, 16)
            sp.dma_start(cnt[:], counts).then_inc(s_in, 16)
            sp.dma_start(eye[:], ident).then_inc(s_in, 16)
            m6 = mod_dram.rearrange("(a b) (s d) -> a b s d", a=1, s=6)
            sp.dma_start(gbB[:], m6[:, :, GB, :].to_broadcast([P, B, D])).then_inc(s_in, 16)
            sp.wait_ge(s_blk, 1)

            def body(u, i, more):
                e = sp.value_load(blki[0:1, bass.ds(i, 1)], min_val=0, max_val=E - 1)
                sp.wait_ge(w_lo, i * 3 + 3)
                for n in range(3):
                    c = chunks[n]
                    sp.dma_start(wf[:, u, n, :].rearrange("p (c f) -> p c f", c=c), w_v[n][:, bass.ds(e * c, c), :]).then_inc(s_w[u], 16)
            sp.dma_start(X1[:], rows(x1_dram)).then_inc(s_x1, 16)
            blocks(sp, body)
            y_v = ys_dram[0:2 * B * S, :].rearrange("(n g p) d -> p n g d", n=2, p=P)
            out_v = rows(out.rearrange("b s d -> (b s) d"))

            def load(g):
                for n in range(2):
                    sp.dma_start(ya[:, g % YB, n, :, :], y_v[:, n, g * END:(g + 1) * END, :]).then_inc(f_y[g % YB], 16)

            sp.wait_ge(s_ys[0], 32 * (BLOCKS // 2 + 1))
            sp.wait_ge(s_ys[1], 32 * (BLOCKS // 2))
            for g in range(YB):
                load(g)
            for g in range(ENDS):
                sp.wait_ge(f_x, g + 1)
                sp.dma_start(out_v[:, g * END:(g + 1) * END, :], X1[:, g * END:(g + 1) * END, :]).then_inc(s_out, 16)
                if g + YB < ENDS:
                    load(g + YB)
            sp.wait_ge(s_out, 16 * ENDS)

        @block.scalar
        def _(act):
            act.wait_ge(r_dif, 1)
            nc.scalar.activation(dif[:], dif[:], ACT.Exp).then_inc(r_exp, 1)
            for c in range(LISTS):
                act.wait_ge(l_tile, c + 1)
                nc.scalar.activation(token[:, c % 2, :, 1, :], istile[:, c % 2, :, :], ACT.Identity,
                                     scale=cnt[:, 64 + P:64 + P + 1]).then_inc(l_token, 1)

            def split_w(u, i, n):
                if n == 0:
                    act.wait_ge(s_w[u], 48 * (i // 2) + 48)
                    act.wait_ge(m_y_ps, i + 1)
                nc.scalar.activation(wh[:, u, n, :], wf[:, u, n, :], ACT.Copy, scale=WS).then_inc(w_hi, 1)

            def split_x(u, i):
                act.wait_ge(m_xT_ps, i + 1 + 2)
                nc.scalar.copy(xh[:, u, :, :], psX[:]).then_inc(m_xh, 1)

            for n in range(3):
                split_w(0, 0, n)
            split_x(0, 0)

            def body(u, i, more):
                for p in range(STEPS_E):
                    act.wait_ge(m_gu, i * STEPS_E + (p + 1))
                    act.wait_ge(m_hf, i * STEPS_E + (p + 1))
                    nc.scalar.activation(sg[:, p % 2, :, :], psG[p % 2][:, :, 0, :], ACT.Silu, scale=1.0 / WS).then_inc(m_sg, 1)
                    if more and p < 3:
                        split_w(1 - u, i + 1, p)
                if more:
                    split_x(1 - u, i + 1)
                act.wait_ge(m_y_ps, i + 3)
                if reused(i, 2):
                    act.wait_ge(s_ys[u], 32 * (i // 2))
                nc.scalar.activation(yr[:, u, :, :], psY[u][:], ACT.Copy, scale=1.0 / WS).then_inc(m_y, 1)
            blocks(act, body)
            act.wait_ge(r_mult, 1)
            for g in range(ENDS):
                act.wait_ge(f_y[g % YB], 32 * (g // YB + 1))
                for t in range(END):
                    y = ya[:, g % YB, 0, t, :]
                    ins = nc.scalar.activation(y, y, ACT.Copy, scale=mult[:, 0, g * END + t:g * END + t + 1])
                ins.then_inc(f_first, 1)

        @block.gpsimd
        def _(pool):
            upto = cnt[:, 64:64 + P].rearrange("p (a n) -> p a n", a=1)
            for c in range(LISTS):
                n, t = c * LIST // NT, c * LIST % NT
                pool.wait_ge(l_tile, c + 1)
                nc.gpsimd.tensor_tensor(token[:, c % 2, :, 0, :], istile[:, c % 2, :, :],
                                        upto[:, 0, n * NT + t:n * NT + t + LIST].rearrange("p (t a) -> p t a", a=1).to_broadcast([P, LIST, TILES_B]),
                                        ALU.mult).then_inc(l_first, 1)

            def gather(u, i):
                pool.wait_ge(l_come, i + 1)
                pool.wait_ge(m_xT_ps, i + 1)
                nc.gpsimd.tensor_tensor(gate[:, u:u + 1], cnt[:, 0:1], cnt[:, 0:1], ALU.add)
                for r in range(RC):
                    nc.gpsimd.indirect_dma_start(xr[:, u, r, :], None, h2_dram,
                                                 bass.IndirectOffsetOnAxis(ap=come[:, u, r:r + 1], axis=0)).then_inc(s_xr[u], 16)

            pool.wait_ge(s_in, 64)
            gather(0, 0)

            def body(u, i, more):
                if more:
                    gather(1 - u, i + 1)
                for p in range(STEPS_E):
                    pool.wait_ge(m_hh, i * STEPS_E + (p + 1))
                    nc.gpsimd.tensor_tensor(hl[:, u, p * GU:(p + 1) * GU, :], hf[:, p % 2, :, :],
                                            hh[:, u, p * GU:(p + 1) * GU, :], ALU.subtract).then_inc(m_hl, 1)
                pool.wait_ge(l_go, i + 1)
                pool.wait_ge(m_y, i + 3)
                nc.gpsimd.tensor_tensor(gate[:, 2 + u:3 + u], cnt[:, 0:1], cnt[:, 0:1], ALU.add)
                for r in range(RC):
                    nc.gpsimd.indirect_dma_start(ys_dram, bass.IndirectOffsetOnAxis(ap=go[:, u, r:r + 1], axis=0),
                                                 yr[:, u, r, :], None).then_inc(s_ys[u], 16)
            blocks(pool, body)
            for g in range(ENDS):
                x = X1[:, g * END:(g + 1) * END, :]
                pool.wait_ge(s_x1, 16)
                pool.wait_ge(f_gate, g + 1)
                nc.gpsimd.tensor_tensor(x, x, ya[:, g % YB, 0, :, :], ALU.add).then_inc(f_x, 1)

        @block.vector
        def _(dve):
            steps = [0]

            def link(ins):
                steps[0] += 1
                ins.then_inc(r_step, 1)
                dve.wait_ge(r_step, steps[0])

            def over(a, n=NT):
                return a.rearrange("p (t a) -> p t a", a=1).to_broadcast([P, n, E])

            dve.wait_ge(s_in, 64)
            order = cnt[:, 0:E].rearrange("p (a e) -> p a e", a=1).to_broadcast(NE)
            for n in range(2):
                src = (LG, lg2)[n]
                link(nc.vector.tensor_reduce(val[:, n, :], src[:], AX.X, ALU.max))
                link(nc.vector.tensor_tensor(key[:], src[:], over(val[:, n, :]), ALU.is_equal))
                link(nc.vector.tensor_tensor(key[:], key[:], order, ALU.mult))
                link(nc.vector.tensor_reduce(kmax[:], key[:], AX.X, ALU.max))
                link(nc.vector.tensor_tensor(hot[:, n, :, :], key[:], over(kmax[:]), ALU.is_equal))
                link(nc.vector.scalar_tensor_tensor(out=tmp[:], in0=LG[:], scalar=-1.0, in1=LG[:], op0=ALU.mult, op1=ALU.max))
                link(nc.vector.tensor_tensor(tmp[:], tmp[:], over(val[:, n, :]), ALU.max))
                link(nc.vector.tensor_tensor(keep[:, n, :, :], over(val[:, n, :]), LG[:], ALU.subtract))
                link(nc.vector.scalar_tensor_tensor(out=keep[:, n, :, :], in0=tmp[:], scalar=2.0 * JITTER, in1=keep[:, n, :, :],
                                                    op0=ALU.mult, op1=ALU.is_ge))
                link(nc.vector.tensor_tensor(dif[:, n, :, :], src[:], over(val[:, n, :]), ALU.subtract))
                if n == 0:
                    link(nc.vector.tensor_scalar(tmp[:], hot[:, 0, :, :], -1.0, 1.0, ALU.mult, ALU.add))
                    link(nc.vector.tensor_tensor(tmp[:], tmp[:], LG[:], ALU.mult))
                    link(nc.vector.scalar_tensor_tensor(out=lg2[:], in0=hot[:, 0, :, :], scalar=LOWEST, in1=tmp[:],
                                                        op0=ALU.mult, op1=ALU.add))
            nc.vector.tensor_tensor(both[:], hot[:, 0, :, :], hot[:, 1, :, :], ALU.add).then_inc(r_hot, 1)
            nc.vector.tensor_copy(tmp[:], tmp[:]).then_inc(r_dif, 1)
            dve.wait_ge(r_cum, 1)
            nc.vector.tensor_copy(cum[:], psR[:, 0, :, :])
            link(nc.vector.tensor_copy(scan[:, 0, :, :], psR[:, 1, :, :]))
            link(nc.vector.tensor_copy(tmp[:], psR[:, 1, :, :]))
            src, shift = 0, 1
            while shift < NT:
                nc.vector.tensor_copy(scan[:, 1 - src, 0:shift, :], scan[:, src, 0:shift, :])
                link(nc.vector.tensor_tensor(scan[:, 1 - src, shift:NT, :], scan[:, src, shift:NT, :],
                                             scan[:, src, 0:NT - shift, :], ALU.add))
                src, shift = 1 - src, 2 * shift
            total = scan[:, src, NT - 1, :]
            link(nc.vector.tensor_tensor(tmp[:], scan[:, src, :, :], tmp[:], ALU.subtract))
            link(nc.vector.tensor_tensor(cum[:], cum[:], tmp[:], ALU.add))
            link(nc.vector.tensor_tensor(ge[:], total.rearrange("p (e a) -> p e a", a=1).to_broadcast([P, E, 16]),
                                         cnt[:, 8:24].rearrange("p (a j) -> p a j", a=1).to_broadcast([P, E, 16]), ALU.is_gt))
            link(nc.vector.tensor_reduce(nblk[:], ge[:], AX.X, ALU.add))
            link(nc.vector.tensor_copy(first[:, 0, :], nblk[:]))
            src, shift = 0, 1
            while shift < E:
                nc.vector.tensor_copy(first[:, 1 - src, 0:shift], first[:, src, 0:shift])
                link(nc.vector.tensor_tensor(first[:, 1 - src, shift:E], first[:, src, shift:E], first[:, src, 0:E - shift], ALU.add))
                src, shift = 1 - src, 2 * shift
            end = first[:, src, :]
            link(nc.vector.tensor_tensor(first[:, 2, :], end, nblk[:], ALU.subtract))
            link(nc.vector.tensor_scalar(first[:, 3, :], first[:, 2, :], float(ROWS), None, ALU.mult))
            link(nc.vector.tensor_tensor(blk[:], end.rearrange("p (a e) -> p a e", a=1).to_broadcast([P, BLOCKS + 1, E]),
                                         cnt[:, 24:64].rearrange("p (t a) -> p t a", a=1)[:, 0:BLOCKS + 1, :].to_broadcast([P, BLOCKS + 1, E]),
                                         ALU.is_le))
            link(nc.vector.tensor_reduce(blkf[:], blk[:], AX.X, ALU.add))
            nc.vector.tensor_scalar(blki[:], blkf[:], float(E - 1), None, ALU.min).then_inc(s_blk, 1)
            link(nc.vector.tensor_tensor(cum[:], cum[:], first[:, 3, :].rearrange("p (a e) -> p a e", a=1).to_broadcast(NE), ALU.add))
            for n in range(2):
                link(nc.vector.tensor_tensor(tmp[:], cum[:], hot[:, n, :, :], ALU.mult))
                link(nc.vector.tensor_reduce(posf[:, n, :], tmp[:], AX.X, ALU.add))
            link(nc.vector.tensor_scalar(tileb[:], posf[:], 1.0 / P, -0.5 + 0.5 / P, ALU.mult, ALU.add))
            link(nc.vector.tensor_scalar(tileb[:], tileb[:], ROUND, None, ALU.add))
            link(nc.vector.tensor_scalar(tileb[:], tileb[:], -ROUND, None, ALU.add))
            link(nc.vector.scalar_tensor_tensor(out=placeb[:], in0=tileb[:], scalar=-float(P), in1=posf[:], op0=ALU.mult, op1=ALU.add))
            upto = cnt[:, 64:64 + P].rearrange("p (a n) -> p a n", a=1)
            for c in range(LISTS):
                n, t = c * LIST // NT, c * LIST % NT
                if c >= 2:
                    dve.wait_ge(l_sum, c - 1)
                    dve.wait_ge(l_first, c - 1)
                nc.vector.tensor_tensor(istile[:, c % 2, :, :],
                                        tileb[:, n, t:t + LIST].rearrange("p (t a) -> p t a", a=1).to_broadcast([P, LIST, TILES_B]),
                                        upto[:, :, 0:TILES_B].to_broadcast([P, LIST, TILES_B]), ALU.is_equal).then_inc(l_tile, 1)
                nc.vector.tensor_tensor(isrow[:, c % 2, :, :],
                                        placeb[:, n, t:t + LIST].rearrange("p (t a) -> p t a", a=1).to_broadcast([P, LIST, P]),
                                        upto.to_broadcast([P, LIST, P]), ALU.is_equal).then_inc(l_row, 1)
            nc.vector.memset(lists[:], 0)
            dve.wait_ge(l_sum, LISTS)
            row, go_f, spare, no = (listf[:, k, :] for k in range(4))
            link(nc.vector.tensor_scalar(row, psL[:, 0, :], float(P), None, ALU.mult))
            link(nc.vector.tensor_tensor(row, row, psL[:, 1, :], ALU.add))
            link(nc.vector.tensor_scalar(no, row, 0.0, None, ALU.is_equal))
            link(nc.vector.tensor_scalar(spare, upto[:, 0, 0:TILES_B], float(P), float(2 * B * S), ALU.mult, ALU.add))
            link(nc.vector.tensor_scalar(spare, spare, cnt[:, 64 + P:64 + P + 1], None, ALU.add))
            link(nc.vector.tensor_tensor(spare, spare, no, ALU.mult))
            link(nc.vector.tensor_scalar(row, row, -1.0, None, ALU.add))
            link(nc.vector.tensor_tensor(go_f, row, spare, ALU.add))
            link(nc.vector.tensor_tensor(row, row, no, ALU.add))
            link(nc.vector.tensor_scalar(spare, row, float(B * S), -float(B * S), ALU.is_ge, ALU.mult))
            link(nc.vector.tensor_tensor(row, row, spare, ALU.add))
            link(nc.vector.tensor_copy(lists[:, :, 0:TILES_B], listf[:, 0:2, :]))
            nc.vector.tensor_copy(come[:, 0, :], lists[:, 0, 0:RC]).then_inc(l_come, 1)
            nc.vector.tensor_copy(come[:, 1, :], lists[:, 0, RC:2 * RC]).then_inc(l_come, 1)
            nc.vector.tensor_copy(go[:, 0, :], lists[:, 1, 0:RC]).then_inc(l_go, 1)
            def split_w(u, i, n):
                dve.wait_ge(w_hi, i * 3 + (n + 1))
                nc.vector.scalar_tensor_tensor(out=wl[:, u, n, :], in0=wf[:, u, n, :], scalar=WS, in1=wh[:, u, n, :],
                                               op0=ALU.mult, op1=ALU.subtract).then_inc(w_lo, 1)

            def split_x(u, i):
                dve.wait_ge(m_xh, i + 1)
                nc.vector.tensor_tensor(xl[:, u, :, :], psX[:], xh[:, u, :, :], ALU.subtract).then_inc(m_xT, 1)

            for n in range(3):
                split_w(0, 0, n)
            split_x(0, 0)
            dve.wait_ge(r_exp, 1)
            for n in range(2):
                link(nc.vector.tensor_tensor(tmp[:], dif[:, n, :, :], keep[:, n, :, :], ALU.mult))
                link(nc.vector.tensor_reduce(val[:, n, :], tmp[:], AX.X, ALU.add))
            nc.vector.reciprocal(mult[:], val[:]).then_inc(r_mult, 1)

            def body(u, i, more):
                for p in range(STEPS_E):
                    dve.wait_ge(m_sg, i * STEPS_E + (p + 1))
                    dve.wait_ge(m_hl, i * STEPS_E + (p + 1))
                    nc.vector.scalar_tensor_tensor(out=hf[:, p % 2, :, :], in0=psG[p % 2][:, :, 1, :], scalar=1.0 / WS,
                                                   in1=sg[:, p % 2, :, :], op0=ALU.mult, op1=ALU.mult).then_inc(m_hf, 1)
                    if p == 0:
                        dve.wait_ge(m_y_ps, i + 1)
                    dve.wait_ge(m_hf, i * STEPS_E + (p + 3))
                    nc.vector.tensor_copy(hh[:, u, p * GU:(p + 1) * GU, :], hf[:, p % 2, :, :]).then_inc(m_hh, 1)
                    if more and p > 0:
                        split_w(1 - u, i + 1, p - 1)
                if more:
                    split_x(1 - u, i + 1)
                    nc.vector.tensor_copy(come[:, u, :], lists[:, 0, bass.ds((i + 2) * RC, RC)]).then_inc(l_come, 1)
                    if reused(i, 1):
                        dve.wait_ge(s_ys[1 - u], 32 * ((i + 1) // 2))
                    nc.vector.tensor_copy(go[:, 1 - u, :], lists[:, 1, bass.ds((i + 1) * RC, RC)]).then_inc(l_go, 1)
            blocks(dve, body)
            dve.wait_ge(r_mult, 1)
            for g in range(ENDS):
                acc = ya[:, g % YB, 0, :, :]
                dve.wait_ge(f_first, g + 1)
                for t in range(END):
                    ins = nc.vector.scalar_tensor_tensor(out=acc[:, t, :], in0=ya[:, g % YB, 1, t, :],
                                                         scalar=mult[:, 1, g * END + t:g * END + t + 1], in1=acc[:, t, :],
                                                         op0=ALU.mult, op1=ALU.add)
                ins.then_inc(f_both, 1)
                dve.wait_ge(f_both, g + 1)
                gb = gbB[:, g * END // TPB, :].rearrange("p (a d) -> p a d", a=1).to_broadcast([P, END, D])
                nc.vector.tensor_tensor(acc, acc, gb, ALU.mult).then_inc(f_gate, 1)

        @block.tensor
        def _(pe):
            for free in (m_y_ps, m_hf, m_hl, m_y, m_xT_ps):
                pe.sem_inc(free, 2)
            pe.sem_inc(w_lo, 6)
            pe.wait_ge(s_in, 64)
            pe.wait_ge(r_hot, 1)
            for n in range(2):
                mm = nc.tensor.matmul(psR[:, n, :, :].rearrange("p t e -> p (t e)"), bel[:, n, :], both[:].rearrange("p t e -> p (t e)"),
                                      start=True, stop=True)
            mm.then_inc(r_cum, 1)

            for c in range(LISTS):
                pe.wait_ge(l_row, c + 1)
                pe.wait_ge(l_first, c + 1)
                pe.wait_ge(l_token, c + 1)
                for k in range(LIST):
                    mm = nc.tensor.matmul(psL.rearrange("p n t -> p (n t)"), isrow[:, c % 2, k, :],
                                          token[:, c % 2, k, :, :].rearrange("p n t -> p (n t)"),
                                          start=(c == 0 and k == 0), stop=(c == LISTS - 1 and k == LIST - 1))
                mm.then_inc(l_sum, 1)

            def turn(u, i):
                pe.wait_ge(s_xr[u], 16 * RC * (i // 2) + 16 * RC)
                for r in range(RC):
                    for k in range(KD):
                        mm = nc.tensor.transpose(psX[:, k, r * P:(r + 1) * P], xr[:, u, r, k * P:(k + 1) * P], eye[:])
                mm.then_inc(m_xT_ps, 1)

            pe.wait_ge(l_come, 1)
            turn(0, 0)
            HALVES = ((0, 0), (1, 0), (0, 1))

            def body(u, i, more):
                pe.wait_ge(m_xT, i + 1)
                pe.wait_ge(w_lo, i * 3 + (2 + 6))
                for p in range(STEPS_E):
                    pe.wait_ge(m_hf, i * STEPS_E + (p + 1))
                    for g in range(GU):
                        f = p * GU + g
                        for n in range(2):
                            for k in range(KD):
                                for a, b in HALVES:
                                    mm = nc.tensor.matmul(psG[p % 2][:, g, n, :], (wh, wl)[a][:, u, n, k * F + f * P:k * F + (f + 1) * P],
                                                          (xh, xl)[b][:, u, k, :], start=(k == 0 and (a, b) == (0, 0)),
                                                          stop=(k == KD - 1 and (a, b) == HALVES[-1]), skip_group_check=True)
                    mm.then_inc(m_gu, 1)
                if more:
                    turn(1 - u, i + 1)
                pe.wait_ge(m_y, i + 1)
                pe.wait_ge(w_lo, i * 3 + (3 + 6))
                for f in range(FC):
                    if f % GU == 0:
                        pe.wait_ge(m_hl, i * STEPS_E + (f // GU + 1 + 2))
                    for r in range(RC):
                        for a, b in HALVES:
                            mm = nc.tensor.matmul(psY[u][:, r, :], (hh, hl)[a][:, u, f, r * P:(r + 1) * P],
                                                  (wh, wl)[b][:, u, W2, f * D:(f + 1) * D],
                                                  start=(f == 0 and r == 0 and (a, b) == (0, 0)), stop=(f == FC - 1), skip_group_check=True)
                mm.then_inc(m_y_ps, 1)
            blocks(pe, body)


def kernel(**inputs):
    import numpy as np
    import concourse.bacc as bacc
    from concourse.bass_utils import run_bass_kernel_spmd as run

    pos = np.arange(S, dtype=np.float32)
    freq = (np.float32(1.0) / np.float32(2500) ** (np.arange(HD // 2, dtype=np.float32) / np.float32(HD // 2))).astype(np.float32)
    theta = pos[:, None] * freq[None, :]
    rope = np.stack([np.repeat(np.cos(theta), 2, axis=1),
                     np.stack([-np.sin(theta), np.sin(theta)], axis=2).reshape(S, HD)], axis=1)
    rope = np.ascontiguousarray(rope.reshape(TPB, P, 2, HD).transpose(1, 0, 2, 3)).astype(np.float32)
    below = np.stack([np.triu(np.ones((P, P), np.float32), 1), np.ones((P, P), np.float32)], axis=1)
    below = np.ascontiguousarray(below)
    counts = np.concatenate([E - np.arange(E), np.arange(16) * ROWS, np.arange(40), np.arange(P)]).astype(np.float32)
    counts = np.concatenate([np.tile(counts, (P, 1)), np.arange(1, P + 1, dtype=np.float32)[:, None]], axis=1)
    counts = np.ascontiguousarray(counts)
    arrays = {
        "x": np.ascontiguousarray(inputs["L0_attn_tokens"]),
        "qkv_wT": np.ascontiguousarray(np.asarray(inputs["L0_attn_qkv_w"]).T),
        "qkv_b": np.ascontiguousarray(inputs["L0_attn_qkv_b"]),
        "out_wT": np.ascontiguousarray(np.asarray(inputs["L0_attn_out_w"]).T),
        "out_b": np.ascontiguousarray(inputs["L0_attn_out_b"]),
        "cT": np.ascontiguousarray(np.asarray(inputs["L0_c"]).T),
        "wmod": np.ascontiguousarray(inputs["L0_wmod"]),
        "gate_w": np.ascontiguousarray(inputs["L0_ffn_gate_w"]),
        "w1": np.ascontiguousarray(inputs["L0_ffn_w1"]),
        "w2": np.ascontiguousarray(inputs["L0_ffn_w2"]),
        "w3": np.ascontiguousarray(inputs["L0_ffn_w3"]),
        "ident": np.eye(P, dtype=np.float32),
        "ident16": np.eye(P, dtype=np.float16),
        "rope": rope,
        "below": below,
        "counts": counts,
    }
    nc = bacc.Bacc("TRN2", target_bir_lowering=False, num_devices=1)
    args = [nc.dram_tensor(n, a.shape, mybir.dt.from_np(a.dtype), kind="ExternalInput").ap() for n, a in arrays.items()]
    args.append(nc.dram_tensor("y", (B, S, D), F32, kind="ExternalOutput").ap())
    adaln(nc, *args)
    r = run(nc, [arrays], core_ids=[0])
    return r.results[0]["y"]
```
